# Optimizing a Trainium2 kernel written in Bass

```python
import numpy as np
import jax
import jax.numpy as jnp

def _softmax(x, axis=-1):
    return jax.nn.softmax(x, axis=axis)

def _gelu(x):
    return jax.nn.gelu(x, approximate=True)

def _silu(x):
    return jax.nn.silu(x)

def _sigmoid(x):
    return jax.nn.sigmoid(x)

def _layernorm(x, axis=-1, eps=1e-05):
    m = jnp.mean(x, axis=axis, keepdims=True)
    v = jnp.var(x, axis=axis, keepdims=True)
    return (x - m) / jnp.sqrt(v + eps)

def _scatter_add(tgt, idx, src, axis=0):
    return tgt.at[idx].add(src)

def _segment_sum(src, seg, n):
    return jax.ops.segment_sum(src, seg, n)
kernel_name = 'mk_gps_d1_gnn_r8_932bf4'

def setup_inputs(seed: int=0):
    np.random.seed(seed)
    _w = jnp.asarray

    def _rec_inputs():
        import jax
        import jax.numpy as jnp
        _gk = jax.random.key(seed)
        x = -0.0002117 + 1 * jax.random.normal(jax.random.fold_in(_gk, 1), (6250, 256), jnp.float32)
        _s = jax.random.randint(jax.random.fold_in(_gk, 2), (50000,), 0, 6250, jnp.int32)
        _d = jax.random.randint(jax.random.fold_in(_gk, 3), (50000,), 0, 6250, jnp.int32)
        _loop = jnp.arange(6250, dtype=jnp.int32)
        src = jnp.concatenate([_s, _d, _loop])
        dst = jnp.concatenate([_d, _s, _loop])
        _o = jnp.argsort(dst, stable=True)
        src = src[_o]
        dst = dst[_o]
        edge_weight = jax.random.uniform(jax.random.fold_in(_gk, 12), (106250,), jnp.float32, 0.0, 0.03125)
        return (x, src, dst, edge_weight)
    x, src, dst, edge_weight = _rec_inputs()

    def _L0_gnn_setup():
        import jax, jax.numpy as jnp
        import numpy as np
        N_NODES = 12500
        N_EDGES = 400000
        DIM = 256
        LEAKY_SLOPE = 0.2
        EPS = 1e-12
        key = jax.random.key(seed)
        ks = jax.random.split(key, 8)
        embeddings = jax.random.normal(ks[0], (N_NODES, DIM), dtype=jnp.float32)
        edge_src = jax.random.randint(ks[1], (N_EDGES,), 0, N_NODES, dtype=jnp.int32)
        edge_dst = jax.random.randint(ks[2], (N_EDGES,), 0, N_NODES, dtype=jnp.int32)
        edge_val = jax.random.uniform(ks[3], (N_EDGES,), dtype=jnp.float32) / 32.0
        scale = 1.0 / np.sqrt(DIM)
        W1 = jax.random.normal(ks[4], (DIM, DIM), dtype=jnp.float32) * scale
        b1 = jax.random.normal(ks[5], (DIM,), dtype=jnp.float32) * 0.01
        W2 = jax.random.normal(ks[6], (DIM, DIM), dtype=jnp.float32) * scale
        b2 = jax.random.normal(ks[7], (DIM,), dtype=jnp.float32) * 0.01
        return {'embeddings': embeddings, 'edge_src': edge_src, 'edge_dst': edge_dst, 'edge_val': edge_val, 'W1': W1, 'b1': b1, 'W2': W2, 'b2': b2}
    _L0_gnn_all = _L0_gnn_setup()
    _L0_gnn_in = {k: v for k, v in _L0_gnn_all.items() if k in ('W1', 'b1', 'W2', 'b2')}
    del _L0_gnn_all

    def _L0_mix_setup():
        import jax, jax.numpy as jnp
        import numpy as np
        HEADS = 8
        DIM_HEAD = 32
        SCALE = DIM_HEAD ** (-0.5)
        EPS = 1e-05

        def _layernorm_gamma(x, gamma):
            mu = jnp.mean(x, axis=-1, keepdims=True)
            var = jnp.var(x, axis=-1, keepdims=True)
            return (x - mu) * jax.lax.rsqrt(var + EPS) * gamma
        key = jax.random.key(seed)
        k1, k2, k3 = jax.random.split(key, 3)
        B, N, D = (8, 2048, 256)
        hidden = HEADS * DIM_HEAD
        x = jax.random.normal(k1, (B, N, D), dtype=jnp.float32)
        Wqkv = jax.random.normal(k2, (D, 3 * hidden), dtype=jnp.float32) * D ** (-0.5)
        Wout = jax.random.normal(k3, (hidden, D), dtype=jnp.float32) * hidden ** (-0.5)
        gamma = jnp.ones((D,), dtype=jnp.float32)
        return {'x': x, 'Wqkv': Wqkv, 'Wout': Wout, 'gamma': gamma}
    _L0_mix_all = _L0_mix_setup()
    _L0_mix_in = {k: v for k, v in _L0_mix_all.items() if k in ('Wqkv', 'Wout', 'gamma')}
    del _L0_mix_all

    def _L0_ffn_setup():
        import jax, jax.numpy as jnp
        import numpy as np
        TOP_K = 2
        LN_EPS = 1e-05
        key = jax.random.key(seed)
        ks = jax.random.split(key, 8)
        B, S, D, E, H = (16, 1024, 256, 8, 1024)
        x = jax.random.normal(ks[0], (B, S, D), dtype=jnp.float32)
        Wr = jax.random.normal(ks[1], (D, E), dtype=jnp.float32) * 0.1
        br = jnp.zeros((E,), dtype=jnp.float32)
        ln_g = jnp.ones((E, D), dtype=jnp.float32)
        ln_b = jnp.zeros((E, D), dtype=jnp.float32)
        W1 = jax.random.normal(ks[2], (E, D, H), dtype=jnp.float32) * (1.0 / np.sqrt(D))
        b1 = jnp.zeros((E, H), dtype=jnp.float32)
        W2 = jax.random.normal(ks[3], (E, H, D), dtype=jnp.float32) * (1.0 / np.sqrt(H))
        b2 = jnp.zeros((E, D), dtype=jnp.float32)
        return {'x': x, 'Wr': Wr, 'br': br, 'ln_g': ln_g, 'ln_b': ln_b, 'W1': W1, 'b1': b1, 'W2': W2, 'b2': b2}
    _L0_ffn_all = _L0_ffn_setup()
    _L0_ffn_in = {k: v for k, v in _L0_ffn_all.items() if k in ('Wr', 'br', 'ln_g', 'ln_b', 'W1', 'b1', 'W2', 'b2')}
    del _L0_ffn_all
    return {'x': x, 'src': src, 'dst': dst, 'edge_weight': edge_weight, 'L0_gnn_W1': _L0_gnn_in['W1'], 'L0_gnn_b1': _L0_gnn_in['b1'], 'L0_gnn_W2': _L0_gnn_in['W2'], 'L0_gnn_b2': _L0_gnn_in['b2'], 'L0_mix_Wqkv': _L0_mix_in['Wqkv'], 'L0_mix_Wout': _L0_mix_in['Wout'], 'L0_mix_gamma': _L0_mix_in['gamma'], 'L0_ffn_Wr': _L0_ffn_in['Wr'], 'L0_ffn_br': _L0_ffn_in['br'], 'L0_ffn_ln_g': _L0_ffn_in['ln_g'], 'L0_ffn_ln_b': _L0_ffn_in['ln_b'], 'L0_ffn_W1': _L0_ffn_in['W1'], 'L0_ffn_b1': _L0_ffn_in['b1'], 'L0_ffn_W2': _L0_ffn_in['W2'], 'L0_ffn_b2': _L0_ffn_in['b2']}

def reference(x, src, dst, edge_weight, L0_gnn_W1, L0_gnn_b1, L0_gnn_W2, L0_gnn_b2, L0_mix_Wqkv, L0_mix_Wout, L0_mix_gamma, L0_ffn_Wr, L0_ffn_br, L0_ffn_ln_g, L0_ffn_ln_b, L0_ffn_W1, L0_ffn_b1, L0_ffn_W2, L0_ffn_b2):
    import jax
    import jax.numpy as jnp

    def _L0_gnn_ref(embeddings, edge_src, edge_dst, edge_val, W1, b1, W2, b2):
        import jax, jax.numpy as jnp
        import numpy as np
        N_NODES = 12500
        N_EDGES = 400000
        DIM = 256
        LEAKY_SLOPE = 0.2
        EPS = 1e-12
        ego_emb = embeddings @ W1.T + b1
        messages = edge_val[:, None] * embeddings[edge_src]
        neighbor_emb = jax.ops.segment_sum(messages, edge_dst, num_segments=embeddings.shape[0])
        interaction_emb = neighbor_emb * embeddings
        side_emb = (neighbor_emb + interaction_emb) @ W2.T + b2
        out = ego_emb + side_emb
        out = jnp.where(out >= 0, out, LEAKY_SLOPE * out)
        norm = jnp.sqrt(jnp.sum(out * out, axis=1, keepdims=True))
        return out / jnp.maximum(norm, EPS)

    def _L0_mix_ref(x, Wqkv, Wout, gamma):
        import jax, jax.numpy as jnp
        import numpy as np
        HEADS = 8
        DIM_HEAD = 32
        SCALE = DIM_HEAD ** (-0.5)
        EPS = 1e-05

        def _layernorm_gamma(x, gamma):
            mu = jnp.mean(x, axis=-1, keepdims=True)
            var = jnp.var(x, axis=-1, keepdims=True)
            return (x - mu) * jax.lax.rsqrt(var + EPS) * gamma
        B, N, D = x.shape
        qkv = x @ Wqkv
        q, k, v = jnp.split(qkv, 3, axis=-1)

        def to_heads(t):
            return t.reshape(B, N, HEADS, DIM_HEAD).transpose(0, 2, 1, 3)
        q, k, v = map(to_heads, (q, k, v))
        q = jax.nn.softmax(q, axis=-1) * SCALE
        k = jax.nn.softmax(k, axis=2)
        context = jnp.einsum('bhnd,bhne->bhde', k, v)
        out = jnp.einsum('bhde,bhnd->bhne', context, q)
        out = out.transpose(0, 2, 1, 3).reshape(B, N, HEADS * DIM_HEAD)
        out = out @ Wout
        return _layernorm_gamma(out, gamma)

    def _L0_ffn_ref(x, Wr, br, ln_g, ln_b, W1, b1, W2, b2):
        import jax, jax.numpy as jnp
        import numpy as np
        TOP_K = 2
        LN_EPS = 1e-05
        B, S, D = x.shape
        N = B * S
        xt = x.reshape(N, D)
        logits = xt @ Wr + br
        probs = jax.nn.softmax(logits, axis=-1)
        top_p, top_idx = jax.lax.top_k(probs, TOP_K)
        weights = top_p / top_p.sum(axis=-1, keepdims=True)
        mu = xt.mean(axis=-1, keepdims=True)
        var = ((xt - mu) ** 2).mean(axis=-1, keepdims=True)
        xn = (xt - mu) * jax.lax.rsqrt(var + LN_EPS)
        xe = xn[None, :, :] * ln_g[:, None, :] + ln_b[:, None, :]
        h = jax.nn.gelu(jnp.einsum('end,edh->enh', xe, W1) + b1[:, None, :], approximate=False)
        y = jnp.einsum('enh,ehd->end', h, W2) + b2[:, None, :]
        y_tok = jnp.transpose(y, (1, 0, 2))
        sel = jnp.take_along_axis(y_tok, top_idx[:, :, None], axis=1)
        out = (weights[:, :, None] * sel).sum(axis=1)
        return out.reshape(B, S, D)
    xn = _layernorm(x, axis=-1)
    x = x + _L0_gnn_ref(xn, src, dst, edge_weight, L0_gnn_W1, L0_gnn_b1, L0_gnn_W2, L0_gnn_b2) + _L0_mix_ref(xn[None], L0_mix_Wqkv, L0_mix_Wout, L0_mix_gamma)[0]
    x = x + _L0_ffn_ref(_layernorm(x, axis=-1)[None], L0_ffn_Wr, L0_ffn_br, L0_ffn_ln_g, L0_ffn_ln_b, L0_ffn_W1, L0_ffn_b1, L0_ffn_W2, L0_ffn_b2)[0]
    return x

_drawn_inputs = setup_inputs


def setup_inputs(seed=0):
    import zlib

    import numpy as np

    out = dict(_drawn_inputs(seed))
    spreads = {'L0_mix_gamma': (1.0, 0.2),
     'L0_ffn_br': (0.0, 0.1),
     'L0_ffn_ln_g': (1.0, 0.2),
     'L0_ffn_ln_b': (0.0, 0.1),
     'L0_ffn_b1': (0.0, 0.1),
     'L0_ffn_b2': (0.0, 0.1)}
    factors = {'edge_weight': 4.979, 'L0_gnn_b1': 42.624, 'L0_gnn_W2': 3.706, 'L0_gnn_b2': 110.673}
    for name, (base, spread) in spreads.items():
        noise = np.random.default_rng([zlib.crc32(name.encode()), seed]).standard_normal(out[name].shape)
        drawn = base * np.exp(spread * noise) if base else spread * noise
        out[name] = jnp.asarray(drawn.astype(out[name].dtype))
    for name, factor in factors.items():
        out[name] = (out[name] * factor).astype(out[name].dtype)
    return out
```

```python
import concourse.bass as bass
from concourse import mybir
from contextlib import ExitStack

F32 = mybir.dt.float32
F16 = mybir.dt.float16
I32 = mybir.dt.int32
U32 = mybir.dt.uint32
ALU = mybir.AluOpType
ACT = mybir.ActivationFunctionType
X = mybir.AxisListType.X

P = 128
N = 6250
D = 256
KC = D // P
NT = -(-N // P)
FULL = N // P
LAG = 8
LAST = N - FULL * P
E = 106250
HALF = 8
PER_IT = 2 * HALF
EIT = -(-E // (P * PER_IT))
ET = EIT * PER_IT
EB = -(-ET // P)
GROUP = 4
W = 64
ACCN = NT * P + W
HEADS = 8
DH = D // HEADS
CTX = 4
CTX_IT = FULL // CTX
NEXP = 8
H = 1024
HC = H // P
CAP = NT * P + P
ROW = D + 4
NODE_CHAIN = 33
M_CHAIN = 2
SLOT_TILES = 2 * (-(-(2 * N // P + NEXP) // 2))
WSCALE = 64.0


def program(nc, x, src, dst, edge_weight, gnn_W1, gnn_b1, gnn_W2, gnn_b2, Wqkv, Wout, gamma,
            Wr, br, ln_g, ln_b, ffn_W1, ffn_b1, ffn_W2, ffn_b2, out):
    xn_table = nc.dram_tensor("xn_table", (N, D), F32, kind="Internal").ap()
    slots = nc.dram_tensor("slots", (NEXP * CAP + P, ROW), F32, kind="Internal").ap()
    with ExitStack() as ctx:
        base = ctx.enter_context(nc.sbuf_tensor("base", [P, NEXP], F32))
        pid = ctx.enter_context(nc.sbuf_tensor("pid", [P, 1], F32))
        ident = ctx.enter_context(nc.sbuf_tensor("ident", [P, P], F32))
        padrow = ctx.enter_context(nc.sbuf_tensor("padrow", [P, ROW], F32))
        banks = [ctx.enter_context(nc.psum_tensor(f"bank{i}", [P, 512], F32)) for i in range(8)]
        with ExitStack() as part:
            nodes_and_edges(nc, part, banks, base, pid, ident, padrow, xn_table, slots, x, src, dst, edge_weight,
                            gnn_W1, gnn_b1, gnn_W2, gnn_b2, Wqkv, Wout, gamma, Wr, br, out)
        with ExitStack() as part:
            experts(nc, part, banks, base, pid, ident, padrow, slots, ln_g, ln_b, ffn_W1, ffn_b1, ffn_W2, ffn_b2, out)


class Chain:

    def __init__(self, eng, sem, start=0):
        self.eng, self.sem, self.start, self.n = eng, sem, start, 0

    def did(self, ins):
        ins.then_inc(self.sem, 1)
        self.n += 1

    def __call__(self, ins):
        self.did(ins)
        self.eng.wait_ge(self.sem, self.start + self.n)


def nodes_and_edges(nc, part, banks, base, pid, ident, padrow, xn_table, slots, x, src, dst, edge_weight,
                    gnn_W1, gnn_b1, gnn_W2, gnn_b2, Wqkv, Wout, gamma, Wr, br, out):
    def sb(name, shape, dt=F32):
        return part.enter_context(nc.sbuf_tensor(name, shape, dt))

    def sem(name):
        return part.enter_context(nc.semaphore(name))

    acc_flat = sb("acc", [P, KC * ACCN])
    acc = acc_flat[:, :].rearrange("p (c n) -> p c n", c=KC)
    xall = acc_flat[:, 0:NT * D].rearrange("p (t d) -> p t d", d=D)
    st6 = sb("st6", [P, NT, 6])
    mean = sb("mean", [P, NT])
    rstd = sb("rstd", [P, NT])
    tmp49 = sb("tmp49", [P, NT])
    xs = sb("xs", [P, 2, 4, D])
    xsT = sb("xsT", [P, 2, KC, 4 * P])
    kmaxg = sb("kmaxg", [P, KC, 13])
    negk = sb("negk", [1, 2 * D])
    kmax = sb("kmax", [P, KC])
    e_raw = sb("e_raw", [P, EB, P], I32)
    s_raw = sb("s_raw", [P, EB, P], I32)
    e_blk = sb("e_blk", [P, EB, P])
    s_blk = sb("s_blk", [P, EB, P])
    w_blk = sb("w_blk", [P, EB, P])
    floor_ = sb("floor_", [P, EB])
    dabs = sb("dabs", [P, EB, P])
    gbase = sb("gbase", [P, EB])
    ends = sb("edge_ends", [P, 3, EB])
    badc = sb("badc", [P, 1])
    good = sb("good", [P, 1])
    flag = sb("flag", [P, 1], I32)
    dst0 = sb("dst0", [1, ET // GROUP], I32)
    dwT = sb("dwT", [P, 2, ET + PER_IT])
    dstT, wT = dwT[:, 0, :], dwT[:, 1, :]
    dw = [sb(f"dw{h}", [P, 2, HALF]) for h in range(2)]
    first4 = sb("first4", [P, P])
    dabT = sb("dabT", [P, ET + PER_IT])
    srcT = sb("srcT", [P, ET + PER_IT])
    wallT = sb("wallT", [P, ET + PER_IT])
    idx = [sb(f"idx{h}", [P, HALF], I32) for h in range(2)]
    got = [sb(f"got{h}", [P, HALF, D]) for h in range(2)]
    hot = [sb(f"hot{h}", [P, HALF, W]) for h in range(2)]
    gidx = sb("gidx", [P, 1], I32)
    gdw = sb("gdw", [P, 2])
    ghot = sb("ghot", [P, P])
    iota = sb("iota", [P, P])
    iota8 = sb("iota8", [P, NEXP])
    node0 = sb("node0", [P, 1])
    tri = sb("tri", [P, P])
    ones = sb("ones", [P, P])
    zeros = sb("zeros", [P, D + KC])
    wqkv = sb("wqkv", [P, KC, 3 * D])
    wraw = sb("wraw", [P, 2, KC, D])
    w1T = sb("w1T", [P, KC, D])
    w2T = sb("w2T", [P, KC, D])
    wout = sb("wout", [P, KC, D])
    M = sb("M", [P, KC, D])
    bd = sb("bd", [P, KC, P])
    ksum = sb("ksum", [P, KC])
    wr = sb("wr", [P, KC, NEXP])
    brow = sb("brow", [1, 2, D])
    bsum = sb("bsum", [1, D])
    br_row = sb("br_row", [1, NEXP])
    gam = sb("gam", [P, D])
    xin = sb("xin", [P, 2, D])
    xT = sb("xT", [P, 2, KC, P])
    ek = sb("ek", [P, 2, D])
    v = sb("v", [P, 2, D])
    xn_in = sb("xn_in", [P, D])
    x_in = sb("x_in", [P, D])
    nT = sb("nT", [P, KC, P])
    sT = sb("sT", [P, KC, P])
    qs = sb("qs", [P, D])
    eq = sb("eq", [P, D])
    qn = sb("qn", [P, D])
    qT = sb("qT", [P, KC, P])
    hd = sb("hd", [P, 3, HEADS])
    gr = sb("gr", [P, D])
    gl = sb("gl", [P, D])
    sq = sb("sq", [P, D])
    bn = sb("bn", [P, 3, 6])
    mv = sb("mv", [P, 3, 2])
    ss = sb("ss", [P, 4])
    sd = sb("sd", [P, 4])
    rs = sb("rs", [P, 4])
    t1 = sb("t1", [P, D])
    t2 = sb("t2", [P, D])
    t3 = sb("t3", [P, D])
    x2 = sb("x2", [P, D])
    x2n = sb("x2n", [P, D])
    x2T = sb("x2T", [P, KC, P])
    row = sb("row", [P, ROW])
    lg = sb("lg", [P, NEXP])
    top = sb("top", [P, NEXP])
    topi = sb("topi", [P, NEXP], U32)
    topf = sb("topf", [P, 2])
    oh = sb("oh", [P, 3, NEXP])
    gt = sb("gt", [P, 5])
    rk = sb("rk", [P, NEXP])
    prod = sb("prod", [P, 2, NEXP])
    slotf = sb("slotf", [P, 2])
    slot = sb("slot", [P, 2], I32)
    tok = sb("tok", [P, 1])

    psE = [banks[0], banks[1]]
    psT = banks[2]
    psTc = [banks[2], banks[7]]
    psKV = [banks[3], banks[4]]
    psC = banks[5]

    s_x = [sem(f"s_xload{g}") for g in range(7)]
    s_w = sem("s_w")
    s_e = sem("s_e")
    s_gp = sem("s_gp")
    s_const = sem("s_const")
    s_dve = sem("s_dve")
    s_var = sem("s_var")
    s_st = sem("s_st")
    s_std = sem("s_std")
    s_xs = sem("s_xs")
    s_tab = [sem(f"s_tab{h}") for h in range(2)]
    s_stored = sem("s_stored")
    s_xsTp = sem("s_xsTp")
    s_xsT = sem("s_xsT")
    s_kT = sem("s_kT")
    s_km = sem("s_km")
    s_wt = sem("s_wt")
    s_wtc = sem("s_wtc")
    s_nk = sem("s_nk")
    s_nkc = sem("s_nkc")
    s_blkT = sem("s_blkT")
    s_blkc = sem("s_blkc")
    s_raw0 = sem("s_raw0")
    s_dabs = sem("s_dabs")
    s_gb = sem("s_gb")
    s_bad = sem("s_bad")
    s_badb = sem("s_badb")
    s_flag = sem("s_flag")
    s_table = sem("s_table")
    s_idx = sem("s_idx")
    s_got = [[sem(f"s_got{h}_{k}") for k in range(HALF)] for h in range(2)]
    s_mult = sem("s_mult")
    s_added = sem("s_added")
    s_ch = sem("s_ch")
    s_hold = sem("s_hold")
    s_holdv, s_holdp = sem("s_holdv"), sem("s_holdp")
    s_gi, s_gg, s_gm, s_gd, s_gc = (sem(f"s_general{i}") for i in range(5))
    s_cl = [sem(f"s_cl{h}") for h in range(2)]
    s_cT = sem("s_cT")
    s_cx = sem("s_cx")
    s_ckv = sem("s_ckv")
    s_cek = sem("s_cek")
    s_cc = sem("s_cc")
    s_bd = sem("s_bd")
    s_mp = sem("s_mp")
    s_M = sem("s_M")
    s_nl, s_nlx = sem("s_nl"), sem("s_nlx")
    s_nT = sem("s_nT")
    s_nTc = sem("s_nTc")
    s_sT = sem("s_sT")
    s_q = sem("s_q")
    s_g = sem("s_g")
    s_qs = sem("s_qs")
    s_eq = sem("s_eq")
    s_qn = sem("s_qn")
    s_qT = sem("s_qT")
    s_qTc = sem("s_qTc")
    s_mix = sem("s_mix")
    s_gl = sem("s_gl")
    s_v = sem("s_v")
    s_sd = sem("s_sd")
    s_x2 = sem("s_x2ready")
    s_x2free = sem("s_x2free")
    s_out = sem("s_out")
    s_x2n = sem("s_x2n")
    s_x2T = sem("s_x2T")
    s_x2Tc = sem("s_x2Tc")
    s_lg = sem("s_lg")
    s_d = sem("s_d")
    s_ed = sem("s_ed")
    s_both = sem("s_both")
    s_rank = sem("s_rank")
    s_slot = sem("s_slot")
    s_sc = [sem(f"s_sc{k}") for k in range(2)]
    s_gr = sem("s_gr")
    s_lk = sem("s_lk")

    NW = 14
    NCONST = 8

    def rows_of(t):
        return LAST if isinstance(t, int) and t == FULL else P

    block = part.enter_context(nc.Block())

    @block.sync
    def _(sp):
        sp.wait_ge(s_raw0, 1)
        sp.dma_start(e_raw[:, 0:EB - 1, :], dst[0:(EB - 1) * P * P].rearrange("(b p e) -> p b e", p=P, e=P)).then_inc(s_e, 16)
        LB = ET - (EB - 1) * P
        sp.dma_start(e_raw[0:LB, EB - 1, :], dst[(EB - 1) * P * P:ET * P].rearrange("(p e) -> p e", e=P)).then_inc(s_e, 16)
        for g in range(6):
            sp.dma_start(xall[:, 8 * g:8 * g + 8, :],
                         x[8 * g * P:8 * (g + 1) * P, :].rearrange("(t p) d -> p t d", p=P)).then_inc(s_x[g], 16)
        sp.wait_ge(s_const, 3)
        sp.dma_start(xall[0:LAST, FULL, :], x[FULL * P:N, :]).then_inc(s_x[6], 16)
        with sp.Fori(0, 6) as g:
            for h in range(2):
                sp.wait_ge(s_xs, 2 * g + h + 1)
                sp.dma_start(xn_table[bass.ds((2 * g + h) * 4 * P, 4 * P), :].rearrange("(t p) d -> p t d", p=P),
                             xs[:, h, :, :]).then_inc(s_tab[h], 16)
                sp.wait_ge(s_tab[h], 16 * g + 16)
                sp.sem_inc(s_stored, 1)
        sp.wait_ge(s_xs, 13)
        sp.dma_start(xn_table[FULL * P:N, :], xs[0:LAST, 0, 0, :]).then_inc(s_tab[0], 16)
        sp.wait_ge(s_tab[0], 16 * 7)
        sp.dma_start(out[N:N + P, :], zeros[:, 0:D]).then_inc(s_out, 16)
        sp.sem_inc(s_table, 1)

        def context_load(t, c):
            rows = rows_of(t)
            sp.wait_ge(s_cT, t + 1)
            sp.dma_start(xin[0:rows, c % 2, :], xn_table[bass.ds(t * P, rows), :]).then_inc(s_cl[c % 2], 16)

        def node_load(t):
            rows = rows_of(t)
            sp.wait_ge(s_nT, t + 1)
            sp.dma_start(xn_in[0:rows, :], xn_table[bass.ds(t * P, rows), :]).then_inc(s_nl, 16)
            sp.wait_ge(s_x2free, t + 1)
            sp.dma_start(x_in[0:rows, :], x[bass.ds(t * P, rows), :]).then_inc(s_nlx, 16)

        def node_store(t):
            rows = rows_of(t)
            sp.wait_ge(s_x2, t + 1)
            sp.dma_start(out[bass.ds(t * P, rows), :], x2[0:rows, :]).then_inc(s_out, 16)

        with sp.Fori(0, CTX_IT) as i:
            for c in range(CTX):
                context_load(i * CTX + c, c)
        context_load(FULL, 0)
        with sp.Fori(0, FULL) as t:
            node_load(t)
            node_store(t)
        node_load(FULL)
        node_store(FULL)
        sp.wait_ge(s_out, 16 * NT + 16)

    @block.gpsimd
    def _(pool):
        def diagonal(buf, op, fill, pattern, mult, base_=0):
            return pool.affine_select(out=buf, in_=buf, compare_op=op, fill=fill, base=base_, pattern=pattern,
                                      channel_multiplier=mult)

        pool.memset(ident[:, :], 0.0).then_inc(s_gp, 1)
        pool.memset(tri[:, :], 1.0).then_inc(s_gp, 1)
        pool.iota(iota[:, :], pattern=[[1, P]], base=0, channel_multiplier=0,
                  allow_small_or_imprecise_dtypes=True).then_inc(s_gp, 1)
        pool.iota(pid[:, :], pattern=[[0, 1]], base=0, channel_multiplier=1,
                  allow_small_or_imprecise_dtypes=True).then_inc(s_gp, 1)
        pool.iota(iota8[:, :], pattern=[[1, NEXP]], base=0, channel_multiplier=0,
                  allow_small_or_imprecise_dtypes=True).then_inc(s_gp, 1)
        pool.iota(base[:, :], pattern=[[CAP, NEXP]], base=0, channel_multiplier=0,
                  allow_small_or_imprecise_dtypes=True).then_inc(s_gp, 1)
        pool.iota(floor_[:, :], pattern=[[P, EB]], base=0, channel_multiplier=1,
                  allow_small_or_imprecise_dtypes=True).then_inc(s_gp, 1)
        pool.iota(padrow[:, D:D + 1], pattern=[[0, 1]], base=N, channel_multiplier=1,
                  allow_small_or_imprecise_dtypes=True).then_inc(s_gp, 1)
        pool.memset(first4[:, :], 1.0).then_inc(s_gp, 1)
        pool.wait_ge(s_gp, 9)
        diagonal(ident[:, :], ALU.not_equal, 1.0, [[-1, P]], 1).then_inc(s_gp, 1)
        diagonal(tri[:, :], ALU.is_gt, 0.0, [[1, P]], -1).then_inc(s_gp, 1)
        view = first4[:, :].rearrange("p (g r) -> p g r", r=GROUP)
        diagonal(view, ALU.is_equal, 0.0, [[-GROUP, P // GROUP], [0, GROUP]], 1).then_inc(s_gp, 1)
        pool.wait_ge(s_const, 10)
        for k in range(2):
            r = slice(k * P // 2, (k + 1) * P // 2)
            pool.dma_start(slots[NEXP * CAP + k * P // 2:NEXP * CAP + (k + 1) * P // 2, :], padrow[r, :]).then_inc(s_sc[k], 16)

        pool.wait_ge(s_flag, 1)
        pool.wait_ge(s_table, 1)
        bad = pool.value_load(flag[0:1, 0:1], min_val=0, max_val=1)
        with pool.If(bad):
            with pool.Fori(0, ET) as t:
                pool.wait_ge(s_gi, t + 1)
                pool.sem_inc(s_hold, 1)
                pool.indirect_dma_start(out=got[0][:, 0, :], out_offset=None, in_=xn_table[:, :],
                                        in_offset=bass.IndirectOffsetOnAxis(ap=gidx[:, 0:1], axis=0)).then_inc(s_gg, 16)

        def gathers(i, h):
            pool.wait_ge(s_idx, 2 * i + h + 1)
            pool.sem_inc(s_hold, 1)
            for k in range(HALF):
                pool.indirect_dma_start(out=got[h][:, k, :], out_offset=None, in_=xn_table[:, :],
                                        in_offset=bass.IndirectOffsetOnAxis(ap=idx[h][:, k:k + 1], axis=0)
                                        ).then_inc(s_got[h][k], 16)

        def scatters(t):
            rows = rows_of(t)
            pool.wait_ge(s_slot, t + 2)
            pool.sem_inc(s_hold, 1)
            for k in range(2):
                pool.indirect_dma_start(out=slots[:, :], out_offset=bass.IndirectOffsetOnAxis(ap=slot[0:rows, k:k + 1], axis=0),
                                        in_=row[0:rows, :], in_offset=None).then_inc(s_sc[k], 16)

        with pool.Fori(0, CTX_IT + 2) as i:
            gathers(i, 0)
            gathers(i, 1)
        with pool.Fori(CTX_IT + 2, EIT) as i:
            gathers(i, 0)
            scatters(i - (CTX_IT + 2))
            gathers(i, 1)
        with pool.Fori(EIT - CTX_IT - 2, FULL) as t:
            scatters(t)
        scatters(FULL)
        for k in range(2):
            pool.wait_ge(s_sc[k], 16 * NT + 16)

    @block.scalar
    def _(act):
        act.wait_ge(s_raw0, 2)
        act.dma_start(s_raw[:, 0:EB - 1, :], src[0:(EB - 1) * P * P].rearrange("(b p e) -> p b e", p=P, e=P)).then_inc(s_e, 16)
        LB = ET - (EB - 1) * P
        act.dma_start(s_raw[0:LB, EB - 1, :], src[(EB - 1) * P * P:ET * P].rearrange("(p e) -> p e", e=P)).then_inc(s_e, 16)
        act.dma_start(w_blk[:, 0:EB - 1, :], edge_weight[0:(EB - 1) * P * P].rearrange("(b p e) -> p b e", p=P, e=P)).then_inc(s_e, 16)
        act.dma_start(w_blk[0:LB, EB - 1, :], edge_weight[(EB - 1) * P * P:ET * P].rearrange("(p e) -> p e", e=P)).then_inc(s_e, 16)
        act.dma_start(dst0[0:1, :], dst[0:ET * P].rearrange("(t e) -> e t", e=GROUP * P)[0:1, :],
                      allow_slow_non_contiguous=True).then_inc(s_e, 16)

        def two(ap):
            return ap.rearrange("(c p) n -> p c n", p=P)

        act.dma_start(wqkv[:, :, :], two(Wqkv)).then_inc(s_w, 16)
        act.dma_start(wraw[:, 0, :, :], two(gnn_W1)).then_inc(s_w, 16)
        act.dma_start(wraw[:, 1, :, :], two(gnn_W2)).then_inc(s_w, 16)
        act.dma_start(wout[:, :, :], two(Wout)).then_inc(s_w, 16)
        act.dma_start(wr[:, :, :], two(Wr)).then_inc(s_w, 16)
        act.dma_start(brow[0:1, 0, :], gnn_b1.rearrange("(a n) -> a n", a=1)).then_inc(s_w, 16)
        act.dma_start(brow[0:1, 1, :], gnn_b2.rearrange("(a n) -> a n", a=1)).then_inc(s_w, 16)
        act.dma_start(br_row[0:1, :], br.rearrange("(a n) -> a n", a=1)).then_inc(s_w, 16)
        act.dma_start(gam[:, :], gamma.partition_broadcast(P)).then_inc(s_w, 16)
        act.wait_ge(s_var, 1)
        act.activation(rstd[:, :], tmp49[:, :], ACT.Sqrt).then_inc(s_std, 1)

        def group_copy(g, h):
            act.wait_ge(s_xsTp, g + 3)
            act.wait_ge(s_kT, g + 1)
            for c in range(KC):
                last = act.activation(xsT[:, h, c, :], banks[c][:, :], ACT.Copy)
            last.then_inc(s_xsT, 1)

        with act.Fori(0, 6) as g:
            for h in range(2):
                group_copy(2 * g + h, h)
        act.wait_ge(s_xsTp, 15)
        act.wait_ge(s_kT, 13)
        for c in range(KC):
            last = act.activation(xsT[:, 0, c, 0:P], banks[c][:, 0:P], ACT.Copy)
        last.then_inc(s_xsT, 1)

        for m, wt in enumerate((w1T, w2T)):
            act.wait_ge(s_wt, m + 1)
            act.activation(wt[:, :, :].rearrange("p c n -> p (c n)"), banks[4 + m][:, :], ACT.Copy).then_inc(s_wtc, 1)

        def context(t, c):
            h = c % 2
            rows = rows_of(t)
            act.wait_ge(s_cT, t + 3)
            act.wait_ge(s_ckv, t + 1)
            act.activation(xT[:, h, :, 0:rows], psTc[h][:, 0:256].rearrange("p (c n) -> p c n", c=KC)[:, :, 0:rows],
                           ACT.Copy).then_inc(s_cx, 1)

        def context_exp(t, c):
            h = c % 2
            rows = rows_of(t)
            act.wait_ge(s_ckv, t + 3)
            act.wait_ge(s_cc, t + 1)
            act.activation(ek[0:rows, h, :], psKV[h][0:rows, 0:D], ACT.Exp)
            act.activation(v[0:rows, h, :], psKV[h][0:rows, D:2 * D], ACT.Copy).then_inc(s_cek, 1)

        with act.Fori(0, CTX_IT) as i:
            for c in range(CTX):
                context(i * CTX + c, c)
                if c:
                    context_exp(i * CTX + c - 1, c - 1)
            context_exp(i * CTX + CTX - 1, CTX - 1)
        context(FULL, 0)
        context_exp(FULL, 0)

        def node(t):
            rows = rows_of(t)
            act.wait_ge(s_nT, t + 2)
            act.activation(nT[:, :, 0:rows], psT[:, 0:256].rearrange("p (c n) -> p c n", c=KC)[:, :, 0:rows],
                           ACT.Copy).then_inc(s_nTc, 1)
            act.wait_ge(s_qs, t + 1)
            act.activation(eq[0:rows, :], qs[0:rows, :], ACT.Exp).then_inc(s_eq, 1)
            act.wait_ge(s_g, t + 1)
            act.activation(gr[0:rows, :], banks[4][0:rows, 0:D], ACT.Copy).then_inc(s_gr, 1)
            act.wait_ge(s_lk, t + 1)
            act.activation(sq[0:rows, :], gl[0:rows, :], ACT.Square, accum_out=ss[0:rows, 0:1]).then_inc(s_gl, 1)
            act.wait_ge(s_qT, t + 1)
            act.activation(qT[:, :, 0:rows], psT[:, 256:512].rearrange("p (c n) -> p c n", c=KC)[:, :, 0:rows],
                           ACT.Copy).then_inc(s_qTc, 1)
            act.wait_ge(s_v, 3 * t + 1)
            act.wait_ge(s_gl, t + 1)
            act.activation(sd[0:rows, 0:2], ss[0:rows, 0:2], ACT.Sqrt).then_inc(s_sd, 1)
            for k in (2, 3):
                act.wait_ge(s_v, 3 * t + k)
                act.activation(sd[0:rows, k:k + 1], ss[0:rows, k:k + 1], ACT.Sqrt).then_inc(s_sd, 1)
            act.wait_ge(s_x2T, t + 1)
            act.activation(x2T[:, :, 0:rows], banks[7][:, 0:256].rearrange("p (c n) -> p c n", c=KC)[:, :, 0:rows],
                           ACT.Copy).then_inc(s_x2Tc, 1)
            act.wait_ge(s_d, t + 1)
            act.activation(gt[0:rows, 1:2], gt[0:rows, 0:1], ACT.Exp).then_inc(s_ed, 1)

        with act.Fori(0, FULL) as t:
            node(t)
        node(FULL)

    @block.vector
    def _(dve):
        one = Chain(dve, s_dve)
        dve.memset(e_raw[:, EB - 1, :], 0).then_inc(s_raw0, 1)
        dve.memset(s_raw[:, EB - 1, :], 0).then_inc(s_raw0, 1)
        dve.memset(xall[:, FULL, :], 0.0).then_inc(s_const, 1)
        dve.memset(ones[:, :], 1.0).then_inc(s_const, 1)
        dve.memset(zeros[:, :], 0.0).then_inc(s_const, 1)
        dve.memset(negk[:, :], 0.0).then_inc(s_const, 1)
        dve.memset(padrow[:, 0:D], 0.0).then_inc(s_const, 1)
        dve.memset(padrow[:, D + 1:ROW], 0.0).then_inc(s_const, 1)
        dve.memset(bd[:, :, :], 0.0).then_inc(s_const, 1)
        for buf in (srcT, dstT, wT):
            dve.memset(buf[:, ET:ET + PER_IT], 0.0).then_inc(s_const, 1)
        LB = ET - (EB - 1) * P
        dve.wait_ge(s_e, 16 * 7)
        dve.wait_ge(s_gp, 12)
        dve.tensor_copy(dabs[:, :, :], e_raw[:, :, :]).then_inc(s_dabs, 1)
        one.did(dve.tensor_copy(s_blk[:, :, :], s_raw[:, :, :]))
        one.did(dve.tensor_scalar(floor_[:, :], floor_[:, :], float(P // PER_IT), -float(P * LAG), op0=ALU.mult, op1=ALU.add))
        dve.wait_ge(s_gb, 1)
        one(dve.tensor_copy(gbase[:, :], banks[6][:, 0:EB]))
        one(dve.tensor_tensor(e_blk[:, :, :], dabs[:, :, :], gbase[:, :].unsqueeze(2).to_broadcast([P, EB, P]), ALU.subtract))
        one.did(dve.reduce_max(ends[:, 0, :], e_blk[:, :, :], axis=X))
        one(dve.tensor_reduce(ends[:, 1, :], e_blk[:, :, :], axis=X, op=ALU.min))
        one.did(dve.tensor_tensor(ends[:, 2, :], ends[:, 1, :], gbase[:, :], ALU.add))
        one.did(dve.tensor_scalar(ends[:, 0, :], ends[:, 0, :], float(W), None, op0=ALU.is_ge))
        one(dve.tensor_scalar(ends[:, 1, :], ends[:, 1, :], 0.0, None, op0=ALU.is_lt))
        one(dve.tensor_tensor(ends[:, 2, :], ends[:, 2, :], floor_[:, :], ALU.is_lt))
        one(dve.memset(ends[LB:P, :, EB - 1:EB], 0.0))
        dve.reduce_max(badc[:, :], ends[:, :, :].rearrange("p k b -> p (k b)"), axis=X).then_inc(s_bad, 1)
        for b in range(EB):
            n = P if b < EB - 1 else LB
            dve.wait_ge(s_blkT, b + 1)
            dve.tensor_copy(srcT[:, b * P:b * P + n], banks[4][:, 0:n])
            dve.tensor_copy(dstT[:, b * P:b * P + n], banks[5][:, 0:n])
            dve.tensor_copy(dabT[:, b * P:b * P + n], banks[6][:, 0:n])
            dve.tensor_copy(wallT[:, b * P:b * P + n], banks[7][:, 0:n]).then_inc(s_blkc, 1)
        dve.wait_ge(s_badb, 1)
        one(dve.reduce_max(good[:, :], banks[6][:, 0:P], axis=X))
        one(dve.tensor_copy(flag[:, :], good[:, :]))
        one(dve.tensor_scalar(good[:, :], good[:, :], -1.0, 1.0, op0=ALU.mult, op1=ALU.add))
        one(dve.tensor_scalar(wT[:, 0:ET], wallT[:, 0:ET], good[:, 0:1], None, op0=ALU.mult))
        one(dve.tensor_copy(tok[:, :], pid[:, :]))
        for g in range(6):
            dve.wait_ge(s_x[g], 16)
            with dve.Fori(8 * g, 8 * g + 8) as t:
                dve.bn_stats(st6[:, bass.ds(t, 1), :], xall[:, bass.ds(t, 1), :]).then_inc(s_st, 1)
        dve.wait_ge(s_x[6], 16)
        dve.bn_stats(st6[:, FULL, :], xall[:, FULL, :]).then_inc(s_st, 1)
        dve.wait_ge(s_st, NT)
        one(dve.tensor_tensor(mean[:, :], st6[:, :, 1], st6[:, :, 4], ALU.add))
        one(dve.tensor_scalar(mean[:, :], mean[:, :], 0.5, None, op0=ALU.mult))
        one(dve.tensor_tensor(tmp49[:, :], st6[:, :, 1], st6[:, :, 4], ALU.subtract))
        one(dve.tensor_tensor(tmp49[:, :], tmp49[:, :], tmp49[:, :], ALU.mult))
        one(dve.tensor_scalar(tmp49[:, :], tmp49[:, :], 0.25, 1e-5, op0=ALU.mult, op1=ALU.add))
        one(dve.tensor_tensor(rstd[:, :], st6[:, :, 2], st6[:, :, 5], ALU.add))
        dve.scalar_tensor_tensor(out=tmp49[:, :], in0=rstd[:, :], scalar=1.0 / D, in1=tmp49[:, :],
                                 op0=ALU.mult, op1=ALU.add).then_inc(s_var, 1)
        dve.wait_ge(s_std, 1)
        one(dve.reciprocal(rstd[:, :], rstd[:, :]))

        def normalise(t, h, k):
            return dve.tensor_scalar(xs[:, h, k, :], xall[:, bass.ds(t, 1), :].rearrange("p a d -> p (a d)"),
                                     mean[:, bass.ds(t, 1)], rstd[:, bass.ds(t, 1)], op0=ALU.subtract, op1=ALU.mult)

        def key_max(g, cols):
            dve.wait_ge(s_kT, g + 3)
            for c in range(KC):
                last = dve.reduce_max(kmaxg[:, c, bass.ds(g, 1)], banks[2 + c][:, 0:cols], axis=X)
            last.then_inc(s_km, 1)

        def normalise_group(g, h):
            dve.wait_ge(s_stored, g + 1)
            dve.wait_ge(s_xsTp, g + 1)
            for k in range(4):
                last = normalise(4 * g + k, h, k)
            last.then_inc(s_xs, 1)

        normalise_group(0, 0)
        with dve.Fori(0, 5) as g:
            normalise_group(2 * g + 1, 1)
            key_max(2 * g, 4 * P)
            normalise_group(2 * g + 2, 0)
            key_max(2 * g + 1, 4 * P)
        normalise_group(11, 1)
        key_max(10, 4 * P)
        dve.wait_ge(s_stored, 13)
        dve.wait_ge(s_xsTp, 13)
        normalise(FULL, 0, 0).then_inc(s_xs, 1)
        key_max(11, 4 * P)
        key_max(12, LAST)
        dve.wait_ge(s_km, 14)
        dve.memset(acc_flat[:, :], 0.0).then_inc(s_dve, 1)
        one.n += 1
        one(dve.reduce_max(kmax[:, :], kmaxg[:, :, :], axis=X))
        dve.tensor_scalar(kmax[:, :], kmax[:, :], -1.0, None, op0=ALU.mult).then_inc(s_nk, 1)
        dve.wait_ge(s_nkc, 1)
        dve.tensor_copy(negk[0:1, 0:D], banks[6][0:1, 0:D]).then_inc(s_nkc, 1)
        dve.wait_ge(s_w, 16 * 9)
        dve.tensor_tensor(bsum[0:1, :], brow[0:1, 0, :], brow[0:1, 1, :], ALU.add).then_inc(s_wtc, 1)
        dve.sem_inc(s_flag, 1)

        bad = dve.value_load(flag[0:1, 0:1], min_val=0, max_val=1)
        with dve.If(bad):
            with dve.Fori(0, ET) as t:
                dve.tensor_scalar(gidx[:, :], srcT[:, bass.ds(t, 1)], 0.0, None, op0=ALU.add).then_inc(s_gi, 1)
                dve.tensor_scalar(gdw[:, 0:1], dabT[:, bass.ds(t, 1)], 0.0, None, op0=ALU.add)
                dve.tensor_scalar(gdw[:, 1:2], wallT[:, bass.ds(t, 1)], 0.0, None, op0=ALU.add)
                dve.memset(node0[:, :], 0.0).then_inc(s_gc, 1)
                dve.wait_ge(s_gc, t * (3 * NT + 1) + 1)
                dve.sem_inc(s_holdv, 1)
                with dve.Fori(0, NT) as n:
                    done = t * (3 * NT + 1) + 1 + n * 3
                    dve.tensor_scalar(ghot[:, :], iota[:, :], node0[:, 0:1], gdw[:, 0:1], op0=ALU.add, op1=ALU.is_equal).then_inc(s_gc, 1)
                    dve.wait_ge(s_gc, done + 1)
                    dve.tensor_scalar(ghot[:, :], ghot[:, :], gdw[:, 1:2], None, op0=ALU.mult).then_inc(s_gc, 1)
                    dve.wait_ge(s_gc, done + 2)
                    dve.sem_inc(s_gd, 1)
                    dve.tensor_scalar(node0[:, :], node0[:, :], float(P), None, op0=ALU.add)
                    dve.wait_ge(s_gm, t * NT + n + 1)
                    dve.tensor_tensor(acc[:, :, bass.ds(n * P, P)], acc[:, :, bass.ds(n * P, P)],
                                      banks[7][:, 0:256].rearrange("p (c n) -> p c n", c=KC), ALU.add).then_inc(s_gc, 1)
                    dve.wait_ge(s_gc, done + 3)

        STEPS = 1 + HALF // GROUP
        d0 = [dve.alloc_register(f"first_dst{g}") for g in range(PER_IT // GROUP)]

        def stage(t, h, before):
            dve.tensor_scalar(idx[h][:, :], srcT[:, bass.ds(t, HALF)], 0.0, None, op0=ALU.add)
            dve.tensor_scalar(dw[h][:, :, :], dwT[:, :, bass.ds(t, HALF)], 0.0, None, op0=ALU.add).then_inc(s_ch, 1)
            dve.wait_ge(s_ch, before + 1)
            for k in range(HALF):
                last = dve.tensor_scalar(hot[h][:, k, :], iota[:, 0:W], dw[h][:, 0, k:k + 1], dw[h][:, 1, k:k + 1],
                                         op0=ALU.is_equal, op1=ALU.mult)
            last.then_inc(s_idx, 1)

        def adds(i, h, before):
            if h == 0:
                dve.load(d0, dst0[0:1, bass.ds(i * (PER_IT // GROUP), PER_IT // GROUP)])
            dve.wait_ge(s_mult, 2 * i + h + 1)
            for g in range(HALF // GROUP):
                if g:
                    dve.wait_ge(s_ch, before + g)
                first = dve.snap(d0[h * (HALF // GROUP) + g], min_val=0, max_val=N - 1)
                view = acc[:, :, bass.ds(first, W)]
                dve.tensor_tensor(view, view, psE[h][:, g * KC * W:(g + 1) * KC * W].rearrange("p (c w) -> p c w", c=KC),
                                  ALU.add).then_inc(s_ch, 1)
            dve.wait_ge(s_ch, before + HALF // GROUP)
            dve.sem_inc(s_added, 1)

        def edges(i, h):
            before = 2 + (2 * i + h) * STEPS
            adds(i, h, before)
            stage((i + 1) * PER_IT + h * HALF, h, before + HALF // GROUP)

        for h in range(2):
            stage(h * HALF, h, h)

        NODE_STEPS = NODE_CHAIN
        CH0 = one.start + one.n

        def node(t, between=None):
            rows = rows_of(t)
            r = slice(0, rows)
            ch = Chain(dve, s_dve, CH0 + M_CHAIN + t * NODE_STEPS)
            dve.wait_ge(s_nTc, t + 1)
            dve.scalar_tensor_tensor(out=sT[:, :, 0:rows], in0=nT[:, :, 0:rows], scalar=1.0,
                                     in1=acc[:, :, bass.ds(t * P, rows)], op0=ALU.add, op1=ALU.mult).then_inc(s_sT, 1)
            dve.wait_ge(s_q, t + 1)
            q8 = banks[3][r, 0:D].rearrange("p (h e) -> p h e", h=HEADS)
            qs8, eq8, qn8 = (b[r, :].rearrange("p (h e) -> p h e", h=HEADS) for b in (qs, eq, qn))
            ch(dve.reduce_max(hd[r, 0, :], q8, axis=X))
            dve.tensor_tensor(qs8, q8, hd[r, 0, :].unsqueeze(2).to_broadcast([rows, HEADS, DH]), ALU.subtract).then_inc(s_qs, 1)
            dve.wait_ge(s_eq, t + 1)
            ch(dve.reduce_sum(hd[r, 1, :], eq8, axis=X))
            ch(dve.reciprocal(hd[r, 2, :], hd[r, 1, :]))
            dve.tensor_tensor(qn8, eq8, hd[r, 2, :].unsqueeze(2).to_broadcast([rows, HEADS, DH]), ALU.mult).then_inc(s_qn, 1)
            dve.wait_ge(s_gr, t + 1)
            dve.scalar_tensor_tensor(out=gl[r, :], in0=gr[r, :], scalar=0.2, in1=gr[r, :], op0=ALU.mult, op1=ALU.max).then_inc(s_lk, 1)
            if between:
                between()
            dve.wait_ge(s_mix, t + 1)
            ch(dve.bn_stats(bn[r, 0, :], banks[6][r, 0:D]))
            dve.sem_inc(s_holdv, 1)
            ch(dve.bn_aggr(mv[r, 0, :], bn[r, 0, :]))
            dve.tensor_scalar(ss[r, 1:2], mv[r, 0, 1:2], 1e-5, None, op0=ALU.add).then_inc(s_v, 1)
            dve.wait_ge(s_sd, 3 * t + 1)
            ch(dve.tensor_scalar(sd[r, 0:2], sd[r, 0:2], 1e-12, None, op0=ALU.max))
            ch(dve.reciprocal(rs[r, 0:2], sd[r, 0:2]))
            ch.did(dve.tensor_scalar(t2[r, :], banks[6][r, 0:D], mv[r, 0, 0:1], rs[r, 1:2], op0=ALU.subtract, op1=ALU.mult))
            dve.wait_ge(s_nlx, 16 * t + 16)
            dve.scalar_tensor_tensor(out=t1[r, :], in0=gl[r, :], scalar=rs[r, 0:1], in1=x_in[r, :],
                                     op0=ALU.mult, op1=ALU.add).then_inc(s_x2free, 1)
            dve.wait_ge(ch.sem, ch.start + ch.n)
            ch(dve.tensor_tensor(t3[r, :], t2[r, :], gam[r, :], ALU.mult))
            dve.wait_ge(s_x2free, t + 2)
            dve.wait_ge(s_out, 16 * t + 16)
            dve.tensor_tensor(x2[r, :], t1[r, :], t3[r, :], ALU.add).then_inc(s_x2, 1)
            dve.wait_ge(s_x2, t + 1)
            for k, (a, b) in ((1, (x2, x2n)), (2, (x2n, row))):
                ch(dve.bn_stats(bn[r, k, :], a[r, 0:D]))
                dve.sem_inc(s_holdv, 1)
                ch(dve.bn_aggr(mv[r, k, :], bn[r, k, :]))
                dve.tensor_scalar(ss[r, k + 1:k + 2], mv[r, k, 1:2], 1e-5, None, op0=ALU.add).then_inc(s_v, 1)
                dve.wait_ge(s_sd, 3 * t + k + 1)
                ch(dve.reciprocal(rs[r, k + 1:k + 2], sd[r, k + 1:k + 2]))
                if k == 2:
                    for s in range(2):
                        dve.wait_ge(s_sc[s], 16 * t + 16)
                ins = dve.tensor_scalar(b[r, 0:D], a[r, :], mv[r, k, 0:1], rs[r, k + 1:k + 2], op0=ALU.subtract, op1=ALU.mult)
                if k == 1:
                    ins.then_inc(s_x2n, 1)
                    dve.wait_ge(s_x2n, t + 1)
                else:
                    ch.did(ins)
            dve.wait_ge(s_lg, t + 1)
            ch(dve.tensor_copy(lg[r, :], banks[7][r, 256:256 + NEXP]))
            dve.sem_inc(s_holdv, 1)
            ch(dve.max(top[r, :], lg[r, :]))
            dve.tensor_tensor(gt[r, 0:1], top[r, 1:2], top[r, 0:1], ALU.subtract).then_inc(s_d, 1)
            ch(dve.max_index(topi[r, :], top[r, :], lg[r, :]))
            ch(dve.tensor_copy(topf[r, :], topi[r, 0:2]))
            ch.did(dve.tensor_scalar(oh[r, 0, :], iota8[r, :], topf[r, 0:1], None, op0=ALU.is_equal))
            ch(dve.tensor_scalar(oh[r, 1, :], iota8[r, :], topf[r, 1:2], None, op0=ALU.is_equal))
            dve.tensor_tensor(oh[r, 2, :], oh[r, 0, :], oh[r, 1, :], ALU.add).then_inc(s_both, 1)
            dve.wait_ge(s_ed, t + 1)
            ch(dve.tensor_scalar(gt[r, 2:3], gt[r, 1:2], 1.0, None, op0=ALU.add))
            ch(dve.reciprocal(gt[r, 3:4], gt[r, 2:3]))
            ch(dve.tensor_tensor(row[r, D + 2:D + 3], gt[r, 1:2], gt[r, 3:4], ALU.mult))
            ch.did(dve.tensor_tensor(row[r, D + 3:D + 4], gt[r, 3:4], row[r, D + 2:D + 3], ALU.subtract))
            ch.did(dve.tensor_copy(row[r, D + 1:D + 2], topf[r, 0:1]))
            ch(dve.tensor_copy(row[r, D:D + 1], tok[r, :]))
            ch.did(dve.tensor_scalar(tok[:, :], tok[:, :], float(P), None, op0=ALU.add))
            dve.wait_ge(s_rank, t + 1)
            ch(dve.tensor_tensor(rk[r, :], banks[7][r, 264:264 + NEXP], base[r, :], ALU.add))
            ch.did(dve.tensor_tensor(base[:, :], base[:, :], banks[7][:, 272:272 + NEXP], ALU.add))
            ch(dve.tensor_tensor(prod[r, :, :], oh[r, 0:2, :], rk[r, :].unsqueeze(1).to_broadcast([rows, 2, NEXP]), ALU.mult))
            ch(dve.reduce_sum(slotf[r, :], prod[r, :, :], axis=X))
            dve.tensor_copy(slot[r, :], slotf[r, :]).then_inc(s_slot, 1)
            assert ch.n == NODE_STEPS, ch.n

        with dve.Fori(0, CTX_IT + 1) as i:
            edges(i, 0)
            edges(i, 1)
        dve.wait_ge(s_cc, NT + 2)
        one(dve.reciprocal(ksum[:, :], psC[:, D:D + KC]))
        one(dve.tensor_scalar(ksum[:, :], ksum[:, :], float(DH) ** -0.5, None, op0=ALU.mult))
        for c in range(KC):
            for b in range(P // DH):
                b_ = slice(b * DH, (b + 1) * DH)
                last = dve.tensor_copy(bd[b_, c, b * DH:(b + 1) * DH], psC[b_, c * P + b * DH:c * P + (b + 1) * DH])
        last.then_inc(s_bd, 1)
        dve.wait_ge(s_mp, 1)
        for c in range(KC):
            last = dve.tensor_scalar(M[:, c, :], banks[6][:, c * D:(c + 1) * D], ksum[:, c:c + 1], None, op0=ALU.mult)
        last.then_inc(s_M, 1)
        assert M_CHAIN == one.start + one.n - CH0, one.n - CH0
        with dve.Fori(CTX_IT + 1, EIT) as i:
            edges(i, 0)
            node(i - (CTX_IT + 1), lambda: edges(i, 1))
        with dve.Fori(EIT - CTX_IT - 1, FULL) as t:
            node(t)
        node(FULL)

    @block.tensor
    def _(pe):
        def mm(o, lhsT, rhs, start, stop, **kw):
            return pe.matmul(o, lhsT, rhs, start=start, stop=stop, **kw)

        pe.sem_inc(s_kT, 2)
        pe.sem_inc(s_cT, 2)
        pe.sem_inc(s_ckv, 2)
        pe.sem_inc(s_cc, 2)
        pe.sem_inc(s_nT, 1)
        pe.sem_inc(s_stored, 2)
        pe.sem_inc(s_xsTp, 2)
        pe.sem_inc(s_x2free, 1)
        pe.sem_inc(s_slot, 1)
        pe.wait_ge(s_gp, 12)
        pe.wait_ge(s_const, 10)
        pe.wait_ge(s_dabs, 1)
        mm(banks[6][:, 0:EB], first4[:, :], dabs[:, :, 0], True, True).then_inc(s_gb, 1)
        pe.wait_ge(s_bad, 1)
        LB = ET - (EB - 1) * P
        for b in range(EB):
            n = P if b < EB - 1 else LB
            if b:
                pe.wait_ge(s_blkc, b)
            for bank, a in ((4, s_blk[0:n, b, :]), (5, e_blk[0:n, b, :]), (6, dabs[0:n, b, :]), (7, w_blk[0:n, b, :])):
                last = pe.transpose(banks[bank][:, 0:n], a, ident[0:n, 0:n])
            last.then_inc(s_blkT, 1)
        pe.wait_ge(s_blkc, EB)
        mm(banks[6][:, 0:P], badc[:, 0:1].to_broadcast([P, P]), ident[:, :], True, True).then_inc(s_badb, 1)
        pe.wait_ge(s_w, 16 * 9)
        for m in range(2):
            for c in range(KC):
                for o in range(KC):
                    last = pe.transpose(banks[4 + m][:, c * D + o * P:c * D + (o + 1) * P], wraw[:, m, o, c * P:(c + 1) * P], ident[:, :])
            last.then_inc(s_wt, 1)

        def group(g, h, tiles):
            pe.wait_ge(s_xs, g + 1)
            pe.wait_ge(s_xsT, g + 2)
            for c in range(KC):
                for k in range(tiles):
                    last = pe.transpose(banks[c][:, k * P:(k + 1) * P], xs[:, h, k, c * P:(c + 1) * P], ident[:, :])
            last.then_inc(s_xsTp, 1)
            pe.wait_ge(s_xsT, g + 3)
            pe.wait_ge(s_km, g + 1)
            for o in range(KC):
                for c in range(KC):
                    last = mm(banks[2 + o][:, 0:tiles * P], wqkv[:, c, D + o * P:D + (o + 1) * P],
                              xsT[:, h, c, 0:tiles * P], c == 0, c == KC - 1)
            last.then_inc(s_kT, 1)

        pe.sem_inc(s_xsT, 2)
        pe.sem_inc(s_km, 1)
        with pe.Fori(0, 6) as g:
            for h in range(2):
                group(2 * g + h, h, 4)
        group(12, 0, 1)
        pe.wait_ge(s_nk, 1)
        for c in range(KC):
            last = mm(banks[6][0:1, c * P:(c + 1) * P], kmax[:, c:c + 1], ident[:, :], True, True)
        last.then_inc(s_nkc, 1)
        pe.wait_ge(s_flag, 1)
        bad = pe.value_load(flag[0:1, 0:1], min_val=0, max_val=1)
        with pe.If(bad):
            with pe.Fori(0, ET) as t:
                pe.wait_ge(s_gg, 16 * t + 16)
                pe.sem_inc(s_holdp, 1)
                with pe.Fori(0, NT) as n:
                    pe.wait_ge(s_gd, t * NT + n + 1)
                    for c in range(KC):
                        last = mm(banks[7][:, c * P:(c + 1) * P], got[0][:, 0, c * P:(c + 1) * P], ghot[:, :], True, True)
                    last.then_inc(s_gm, 1)

        pe.sem_inc(s_added, 2)
        pe.sem_inc(s_cx, 2)
        pe.sem_inc(s_cek, 2)

        def edges(i, h):
            pe.wait_ge(s_added, 2 * i + h + 1)
            pe.wait_ge(s_idx, 2 * i + h + 1)
            for g in range(HALF // GROUP):
                for k in range(g * GROUP, (g + 1) * GROUP):
                    pe.wait_ge(s_got[h][k], 16 * i + 16)
                    for c in range(KC):
                        last = mm(psE[h][:, (g * KC + c) * W:(g * KC + c + 1) * W], got[h][:, k, c * P:(c + 1) * P],
                                  hot[h][:, k, :], g == 0 and k == 0 and c == 0, k == HALF - 1 and c == KC - 1,
                                  skip_group_check=True)
            last.then_inc(s_mult, 1)

        def ctx_T(t, c):
            h, rows = c % 2, rows_of(t)
            pe.wait_ge(s_cl[h], load_count(t, c))
            pe.wait_ge(s_cx, t + 1)
            for k in range(KC):
                last = pe.transpose(psTc[h][:, k * P:k * P + rows], xin[0:rows, h, k * P:(k + 1) * P], ident[0:rows, 0:rows])
            last.then_inc(s_cT, 1)

        def ctx_kv(t, c):
            h, rows = c % 2, rows_of(t)
            pe.wait_ge(s_cx, t + 3)
            pe.wait_ge(s_cek, t + 1)
            for k in range(KC):
                mm(psKV[h][0:rows, :], xT[:, h, k, 0:rows], wqkv[:, k, D:3 * D], k == 0, False)
            mm(psKV[h][0:rows, :], ones[0:1, 0:rows], negk[0:1, :], False, True).then_inc(s_ckv, 1)

        def ctx_sum(t, c):
            h, rows = c % 2, rows_of(t)
            last_tile = isinstance(t, int) and t == FULL
            pe.wait_ge(s_cek, t + 3)
            for k in range(KC):
                mm(psC[:, k * P:(k + 1) * P], v[0:rows, h, k * P:(k + 1) * P], ek[0:rows, h, k * P:(k + 1) * P], False, False, skip_group_check=True)
                last = mm(psC[:, D + k:D + k + 1], ek[0:rows, h, k * P:(k + 1) * P], ones[0:rows, 0:1], False, last_tile, skip_group_check=True)
            last.then_inc(s_cc, 1)

        it = [None]

        def load_count(t, c):
            return 16 * (CTX // 2) * it[0] + 16 * (c // 2) + 16

        pe.wait_ge(s_wtc, 3)
        mm(psC[:, 0:D + KC], zeros[:, 0:P], zeros[:, 0:D + KC], True, False, skip_group_check=True)
        with pe.Fori(0, CTX_IT) as i:
            it[0] = i
            edges(i, 0)
            for c in range(CTX):
                t = i * CTX + c
                ctx_T(t, c)
                if c:
                    ctx_kv(t - 1, c - 1)
                if c == CTX // 2:
                    edges(i, 1)
                if c > 1:
                    ctx_sum(t - 2, c - 2)
            t = i * CTX + CTX
            ctx_kv(t - 1, CTX - 1)
            ctx_sum(t - 2, CTX - 2)
            ctx_sum(t - 1, CTX - 1)
        it[0] = CTX_IT
        edges(CTX_IT, 0)
        ctx_T(FULL, 0)
        ctx_kv(FULL, 0)
        ctx_sum(FULL, 0)
        edges(CTX_IT, 1)
        pe.wait_ge(s_bd, 1)
        for c in range(KC):
            last = mm(banks[6][:, c * D:(c + 1) * D], bd[:, c, :], wout[:, c, :], True, True)
        last.then_inc(s_mp, 1)
        pe.wait_ge(s_M, 1)

        def node_in(t):
            rows = rows_of(t)
            pe.wait_ge(s_nl, 16 * t + 16)
            pe.wait_ge(s_slot, t + 1)
            for c in range(KC):
                last = pe.transpose(psT[:, c * P:c * P + rows], xn_in[0:rows, c * P:(c + 1) * P], ident[0:rows, 0:rows])
            last.then_inc(s_nT, 1)
            pe.wait_ge(s_nTc, t + 1)
            for c in range(KC):
                last = mm(banks[3][0:rows, 0:D], nT[:, c, 0:rows], wqkv[:, c, 0:D], c == 0, c == KC - 1)
            last.then_inc(s_q, 1)
            mm(banks[4][0:rows, 0:D], nT[:, 0, 0:rows], w1T[:, 0, :], True, False)
            mm(banks[4][0:rows, 0:D], nT[:, 1, 0:rows], w1T[:, 1, :], False, False)
            mm(banks[4][0:rows, 0:D], ones[0:1, 0:rows], bsum[0:1, :], False, False)
            pe.wait_ge(s_sT, t + 1)
            mm(banks[4][0:rows, 0:D], sT[:, 0, 0:rows], w2T[:, 0, :], False, False)
            mm(banks[4][0:rows, 0:D], sT[:, 1, 0:rows], w2T[:, 1, :], False, True).then_inc(s_g, 1)
            pe.wait_ge(s_qn, t + 1)
            for c in range(KC):
                last = pe.transpose(psT[:, 256 + c * P:256 + c * P + rows], qn[0:rows, c * P:(c + 1) * P], ident[0:rows, 0:rows])
            last.then_inc(s_qT, 1)

        def node_out(t):
            rows = rows_of(t)
            pe.wait_ge(s_qTc, t + 1)
            for c in range(KC):
                last = mm(banks[6][0:rows, 0:D], qT[:, c, 0:rows], M[:, c, :], c == 0, c == KC - 1)
            last.then_inc(s_mix, 1)
            pe.wait_ge(s_x2n, t + 1)
            for c in range(KC):
                last = pe.transpose(banks[7][:, c * P:c * P + rows], x2n[0:rows, c * P:(c + 1) * P], ident[0:rows, 0:rows])
            last.then_inc(s_x2T, 1)
            pe.wait_ge(s_x2Tc, t + 1)
            lo = banks[7][0:rows, 256:256 + NEXP]
            for c in range(KC):
                mm(lo, x2T[:, c, 0:rows], wr[:, c, :], c == 0, False)
            mm(lo, ones[0:1, 0:rows], br_row[0:1, :], False, True).then_inc(s_lg, 1)
            pe.wait_ge(s_both, t + 1)
            mm(banks[7][0:rows, 264:264 + NEXP], tri[0:rows, 0:rows], oh[0:rows, 2, :], True, True)
            mm(banks[7][:, 272:272 + NEXP], ones[0:rows, :], oh[0:rows, 2, :], True, True).then_inc(s_rank, 1)

        with pe.Fori(CTX_IT + 1, EIT) as i:
            edges(i, 0)
            node_in(i - (CTX_IT + 1))
            edges(i, 1)
            node_out(i - (CTX_IT + 1))
        with pe.Fori(EIT - CTX_IT - 1, FULL) as t:
            node_in(t)
            node_out(t)
        node_in(FULL)
        node_out(FULL)


def experts(nc, part, banks, base, pid, ident, padrow, slots, ln_g, ln_b, ffn_W1, ffn_b1, ffn_W2, ffn_b2, out):
    def sb(name, shape, dt=F32):
        return part.enter_context(nc.sbuf_tensor(name, shape, dt))

    def sem(name):
        return part.enter_context(nc.semaphore(name))

    W1N, W2N = KC * H, HC * D
    w1h, w1l = (sb(n, [P, NEXP * W1N], F16) for n in ("w1h", "w1l"))
    w2h, w2l = (sb(n, [P, NEXP * W2N], F16) for n in ("w2h", "w2l"))
    w1s = sb("w1s", [P, W1N])
    w2s = sb("w2s", [P, W2N])
    gT = sb("gT", [P, KC, NEXP])
    bT = sb("bT", [P, KC, NEXP])
    grow = sb("grow", [NEXP, 2, D])
    b1raw = sb("b1raw", [NEXP, H])
    b1 = sb("b1", [P, NEXP * HC])
    b2 = sb("b2", [P, NEXP * D])
    cnt = sb("cnt", [P, NEXP])
    tiles = sb("tiles", [P, NEXP])
    ends = sb("ends", [P, NEXP])
    ks = sb("ks", [P, NT])
    big = sb("big", [P, NEXP, SLOT_TILES])
    js = sb("js", [P, SLOT_TILES])
    ej = sb("ej", [P, SLOT_TILES])
    sj = sb("sj", [P, SLOT_TILES])
    ro = sb("ro", [P, SLOT_TILES])
    roff = sb("roff", [P, SLOT_TILES], I32)
    eidx = sb("eidx", [P, SLOT_TILES], I32)
    reg0 = sb("reg0", [P, NEXP])
    padf = sb("padf", [P, NEXP])
    padi = sb("padi", [P, NEXP], I32)
    xe = sb("xe", [P, 2, ROW])
    xh, xl = (sb(n, [P, 2, KC, P], F16) for n in ("xh", "xl"))
    h32 = sb("h32", [P, 2, HC, P])
    hh, hl = (sb(n, [P, 2, HC, P], F16) for n in ("hh", "hl"))
    y = sb("y", [P, 2, D])
    yg = sb("yg", [P, 2, D])
    gates = sb("gates", [P, SLOT_TILES])
    tokf = sb("tokf", [P, SLOT_TILES])
    toki = [sb(f"toki{h}", [P, 1], I32) for h in range(2)]
    psT = [banks[0], banks[7]]
    psH = [[banks[1], banks[2]], [banks[3], banks[4]]]
    psY = [banks[5], banks[6]]

    s_c = sem("f_c")
    s_ch = sem("f_ch")
    s_l = [sem(f"f_l{i}") for i in range(2)]
    s_b = sem("f_b")
    s_bT = sem("f_bT")
    s_bTc = sem("f_bTc")
    s_w1s = sem("f_w1s")
    s_hi = sem("f_hi")
    s_hi2 = sem("f_hi2")
    s_lo = sem("f_lo")
    s_pb = sem("f_pb")
    s_pi = sem("f_pi")
    s_pad = sem("f_pad")
    s_tab = sem("f_tab")
    s_padded = sem("f_padded")
    s_xe = [sem(f"f_xe{h}") for h in range(2)]
    s_hold = sem("f_hold")
    s_T = sem("f_T")
    s_xh = sem("f_xh")
    s_xl = sem("f_xl")
    s_H = sem("f_H")
    s_gelu = sem("f_gelu")
    s_hh = sem("f_hh")
    s_hl = sem("f_hl")
    s_Y = sem("f_Y")
    s_y1 = sem("f_y1")
    s_gt = sem("f_gt")
    s_y = sem("f_y")
    s_add = sem("f_add")
    s_g = sem("f_g")
    JT = SLOT_TILES // 2

    block = part.enter_context(nc.Block())

    @block.sync
    def _(sp):
        sp.dma_start(grow[:, 0, :], ln_g).then_inc(s_b, 16)
        sp.dma_start(grow[:, 1, :], ln_b).then_inc(s_b, 16)
        sp.dma_start(b1raw[:, :], ffn_b1).then_inc(s_b, 16)
        sp.dma_start(b2[:, :], ffn_b2.rearrange("e d -> (e d)").partition_broadcast(P)).then_inc(s_b, 16)
        w1v = ffn_W1.rearrange("e (c p) h -> e p c h", p=P)
        w2v = ffn_W2.rearrange("e (c p) d -> e p c d", p=P)
        for e in range(NEXP):
            if e:
                sp.wait_ge(s_lo, e)
            sp.dma_start(w1s[:, :].rearrange("p (c h) -> p c h", c=KC), w1v[e]).then_inc(s_l[0], 16)
            sp.dma_start(w2s[:, :].rearrange("p (c d) -> p c d", c=HC), w2v[e]).then_inc(s_l[1], 16)
        sp.wait_ge(s_tab, 1)
        sp.wait_ge(s_padded, 16 * NEXP)
        with sp.Fori(0, JT) as i:
            for h in range(2):
                j = 2 * i + h
                r = sp.value_load(roff[0:1, bass.ds(j, 1)], min_val=0, max_val=NEXP * CAP)
                sp.wait_ge(s_xl, j + 1)
                sp.dma_start(xe[:, h, :], slots[bass.ds(r, P), :]).then_inc(s_xe[h], 16)

    @block.gpsimd
    def _(pool):
        pool.iota(ks[:, :], pattern=[[P, NT]], base=0, channel_multiplier=0,
                  allow_small_or_imprecise_dtypes=True).then_inc(s_c, 1)
        pool.iota(js[:, :], pattern=[[1, SLOT_TILES]], base=0, channel_multiplier=0,
                  allow_small_or_imprecise_dtypes=True).then_inc(s_c, 1)
        pool.iota(reg0[:, :], pattern=[[CAP, NEXP]], base=0, channel_multiplier=0,
                  allow_small_or_imprecise_dtypes=True).then_inc(s_c, 1)
        pool.wait_ge(s_pad, 1)
        for e in range(NEXP):
            pool.indirect_dma_start(out=slots[:, :], out_offset=bass.IndirectOffsetOnAxis(ap=padi[:, e:e + 1], axis=0),
                                    in_=padrow[:, :], in_offset=None).then_inc(s_padded, 16)
        with pool.Fori(0, JT) as i:
            for h in range(2):
                j = 2 * i + h
                pool.wait_ge(s_y, j + 3)
                if h:
                    pool.wait_ge(s_add, 32 * i + 16)
                    pool.sem_inc(s_hold, 1)
                else:
                    pool.wait_ge(s_g, i + 1)
                    pool.sem_inc(s_hold, 1)
                pool.indirect_dma_start(out=out[:, :], out_offset=bass.IndirectOffsetOnAxis(ap=toki[h][:, 0:1], axis=0),
                                        in_=yg[:, h, :], in_offset=None, compute_op=ALU.add).then_inc(s_add, 16)
            pool.wait_ge(s_add, 32 * i + 32)
            pool.sem_inc(s_g, 1)

    @block.scalar
    def _(act):
        for e in range(NEXP):
            act.wait_ge(s_w1s, e + 1)
            act.activation(w1h[:, e * W1N:(e + 1) * W1N], w1s[:, :], ACT.Copy).then_inc(s_hi, 1)
            act.wait_ge(s_l[1], 16 * e + 16)
            act.activation(w2h[:, e * W2N:(e + 1) * W2N], w2s[:, :], ACT.Copy, scale=WSCALE).then_inc(s_hi2, 1)

        def gelu(j, h, m, e8):
            act.wait_ge(s_H, 2 * j + 5 + m)
            act.sem_inc(s_hold, 1)
            for c in range(4):
                last = act.activation(h32[:, h, 4 * m + c, :], psH[h][m][:, c * P:(c + 1) * P], ACT.Gelu,
                                      bias=b1[:, bass.ds(e8 + (4 * m + c), 1)], scale=1.0 / WSCALE)
            last.then_inc(s_gelu, 1)

        def tile(j, h):
            act.wait_ge(s_hl, j + 1)
            act.sem_inc(s_hold, 1)
            e8 = act.value_load(eidx[0:1, bass.ds(j, 1)], min_val=0, max_val=NEXP - 1) * HC
            gelu(j, h, 0, e8)
            gelu(j, h, 1, e8)

        act.wait_ge(s_tab, 1)
        with act.Fori(0, JT) as i:
            tile(2 * i, 0)
            tile(2 * i + 1, 1)

    @block.vector
    def _(dve):
        ch = Chain(dve, s_ch)
        dve.wait_ge(s_c, 3)
        ch(dve.tensor_tensor(cnt[:, :], base[:, :], reg0[:, :], ALU.subtract))
        ch(dve.tensor_scalar(padf[:, :], base[:, :], pid[:, 0:1], None, op0=ALU.add))
        dve.tensor_copy(padi[:, :], padf[:, :]).then_inc(s_pad, 1)
        ch(dve.tensor_tensor(big[:, :, 0:NT], cnt[:, :].unsqueeze(2).to_broadcast([P, NEXP, NT]),
                             ks[:, :].unsqueeze(1).to_broadcast([P, NEXP, NT]), ALU.is_gt))
        ch(dve.reduce_sum(tiles[:, :], big[:, :, 0:NT], axis=X))
        ch(dve.tensor_copy(ends[:, 0:1], tiles[:, 0:1]))
        for e in range(1, NEXP):
            ch(dve.tensor_tensor(ends[:, e:e + 1], ends[:, e - 1:e], tiles[:, e:e + 1], ALU.add))
        ch(dve.tensor_tensor(big[:, :, :], js[:, :].unsqueeze(1).to_broadcast([P, NEXP, SLOT_TILES]),
                             ends[:, :].unsqueeze(2).to_broadcast([P, NEXP, SLOT_TILES]), ALU.is_ge))
        ch(dve.reduce_sum(ej[:, :], big[:, :, :].rearrange("p e j -> p j e"), axis=X))
        ch(dve.tensor_tensor(big[:, :, :], big[:, :, :], tiles[:, :].unsqueeze(2).to_broadcast([P, NEXP, SLOT_TILES]), ALU.mult))
        ch(dve.reduce_sum(sj[:, :], big[:, :, :].rearrange("p e j -> p j e"), axis=X))
        ch(dve.tensor_tensor(sj[:, :], js[:, :], sj[:, :], ALU.subtract))
        ch(dve.tensor_scalar(sj[:, :], sj[:, :], float(P), None, op0=ALU.mult))
        ch(dve.scalar_tensor_tensor(out=ro[:, :], in0=ej[:, :], scalar=float(CAP), in1=sj[:, :], op0=ALU.mult, op1=ALU.add))
        ch(dve.tensor_scalar(ro[:, :], ro[:, :], float(NEXP * CAP), None, op0=ALU.min))
        ch(dve.tensor_copy(roff[:, :], ro[:, :]))
        ch(dve.tensor_scalar(sj[:, :], ej[:, :], float(NEXP - 1), None, op0=ALU.min))
        ch(dve.tensor_copy(eidx[:, :], sj[:, :]))
        dve.wait_ge(s_bT, 1)
        ch(dve.tensor_copy(gT[:, :, :].rearrange("p c e -> p (c e)"), banks[0][:, 0:16]))
        ch(dve.tensor_copy(bT[:, :, :].rearrange("p c e -> p (c e)"), banks[0][:, 16:32]))
        ch(dve.tensor_copy(b1[:, :].rearrange("p (e c) -> p e c", c=HC),
                           banks[0][:, 32:96].rearrange("p (c e) -> p e c", c=HC)))
        dve.sem_inc(s_bTc, 1)
        for e in range(NEXP):
            dve.wait_ge(s_pb, e + 1)
            ch(dve.tensor_tensor(b1[:, e * HC:(e + 1) * HC], b1[:, e * HC:(e + 1) * HC], banks[1][:, (e % 2) * HC:(e % 2) * HC + HC], ALU.add))
            for c in range(KC):
                last = dve.tensor_scalar(w1s[:, c * H:(c + 1) * H], w1s[:, c * H:(c + 1) * H], gT[:, c, e:e + 1], WSCALE,
                                         op0=ALU.mult, op1=ALU.mult)
            last.then_inc(s_w1s, 1)
            dve.wait_ge(s_hi, e + 1)
            dve.tensor_tensor(w1l[:, e * W1N:(e + 1) * W1N], w1s[:, :], w1h[:, e * W1N:(e + 1) * W1N], ALU.subtract)
            dve.wait_ge(s_hi2, e + 1)
            dve.scalar_tensor_tensor(out=w2l[:, e * W2N:(e + 1) * W2N], in0=w2s[:, :], scalar=WSCALE,
                                     in1=w2h[:, e * W2N:(e + 1) * W2N], op0=ALU.mult, op1=ALU.subtract).then_inc(s_lo, 1)
        dve.wait_ge(s_lo, NEXP)
        dve.sem_inc(s_tab, 1)
        dve.sem_inc(s_hl, 2)
        dve.sem_inc(s_y, 2)
        dve.sem_inc(s_H, 4)
        dve.sem_inc(s_hh, 2)

        def split_x(j, h):
            dve.wait_ge(s_xe[h], 16 * (j // 2 if isinstance(j, int) else pair(j, h)) + 16)
            dve.tensor_scalar(gates[:, bass.ds(j, 1)], xe[:, h, D + 1:D + 2], ej[:, bass.ds(j, 1)], None, op0=ALU.is_equal).then_inc(s_gt, 1)
            dve.tensor_scalar(tokf[:, bass.ds(j, 1)], xe[:, h, D:D + 1], 0.0, None, op0=ALU.add)
            dve.wait_ge(s_gt, j + 1)
            dve.scalar_tensor_tensor(out=gates[:, bass.ds(j, 1)], in0=gates[:, bass.ds(j, 1)], scalar=xe[:, h, D + 3:D + 4],
                                     in1=xe[:, h, D + 2:D + 3], op0=ALU.mult, op1=ALU.add)
            dve.wait_ge(s_T, j + 3)
            dve.wait_ge(s_H, 2 * j + 2)
            dve.tensor_copy(xh[:, h, :, :].rearrange("p c n -> p (c n)"), psT[h][:, 0:256]).then_inc(s_xh, 1)
            dve.wait_ge(s_xh, j + 1)
            dve.tensor_tensor(xl[:, h, :, :].rearrange("p c n -> p (c n)"), psT[h][:, 0:256],
                              xh[:, h, :, :].rearrange("p c n -> p (c n)"), ALU.subtract).then_inc(s_xl, 1)

        at = [None, None]

        def pair(j, h):
            return at[h]

        def split_h(j, h):
            dve.wait_ge(s_Y, j + 1)
            for m in range(2):
                dve.wait_ge(s_gelu, 2 * j + m + 5)
                dve.tensor_copy(hh[:, h, 4 * m:4 * m + 4, :], h32[:, h, 4 * m:4 * m + 4, :]).then_inc(s_hh, 1)
                dve.wait_ge(s_hh, 2 * j + m + 3)
                last = dve.tensor_tensor(hl[:, h, 4 * m:4 * m + 4, :], h32[:, h, 4 * m:4 * m + 4, :], hh[:, h, 4 * m:4 * m + 4, :], ALU.subtract)
            last.then_inc(s_hl, 1)

        def gated(j, h, i):
            e = dve.value_load(eidx[0:1, bass.ds(j, 1)], min_val=0, max_val=NEXP - 1)
            dve.wait_ge(s_Y, j + 3)
            dve.scalar_tensor_tensor(out=y[:, h, :], in0=psY[h][:, 0:D], scalar=1.0 / WSCALE,
                                     in1=b2[:, bass.ds(e * D, D)], op0=ALU.mult, op1=ALU.add).then_inc(s_y1, 1)
            dve.wait_ge(s_y1, j + 1)
            dve.wait_ge(s_g, i + 1)
            dve.tensor_scalar(toki[h][:, :], tokf[:, bass.ds(j, 1)], 0.0, None, op0=ALU.add)
            dve.tensor_scalar(yg[:, h, :], y[:, h, :], gates[:, bass.ds(j, 1)], None, op0=ALU.mult).then_inc(s_y, 1)

        split_x(0, 0)
        split_x(1, 1)
        split_h(0, 0)
        with dve.Fori(0, JT - 1) as i:
            at[0] = i + 1
            split_x(2 * i + 2, 0)
            split_h(2 * i + 1, 1)
            gated(2 * i, 0, i)
            at[1] = i + 1
            split_x(2 * i + 3, 1)
            split_h(2 * i + 2, 0)
            gated(2 * i + 1, 1, i)
        split_h(SLOT_TILES - 1, 1)
        gated(SLOT_TILES - 2, 0, JT - 1)
        gated(SLOT_TILES - 1, 1, JT - 1)

    @block.tensor
    def _(pe):
        pe.sem_inc(s_T, 2)
        pe.sem_inc(s_Y, 2)
        pe.sem_inc(s_g, 1)
        pe.wait_ge(s_b, 64)
        for c in range(KC):
            for k in range(2):
                pe.transpose(banks[0][:, (2 * k + c) * NEXP:(2 * k + c + 1) * NEXP], grow[:, k, c * P:(c + 1) * P], ident[0:NEXP, 0:NEXP])
        for c in range(HC):
            last = pe.transpose(banks[0][:, 32 + c * NEXP:32 + (c + 1) * NEXP], b1raw[:, c * P:(c + 1) * P], ident[0:NEXP, 0:NEXP])
        last.then_inc(s_bT, 1)
        pe.wait_ge(s_bTc, 1)
        for e in range(NEXP):
            pe.wait_ge(s_l[0], 16 * e + 16)
            for c in range(HC):
                for k in range(KC):
                    last = pe.matmul(banks[1][:, (e % 2) * HC + c:(e % 2) * HC + c + 1], w1s[:, k * H + c * P:k * H + (c + 1) * P],
                                     bT[:, k, e:e + 1], start=k == 0, stop=k == KC - 1)
            last.then_inc(s_pb, 1)
        pe.wait_ge(s_tab, 1)

        def transposes(j, h, i):
            pe.wait_ge(s_xe[h], 16 * i + 16)
            pe.wait_ge(s_xl, j + 1)
            for c in range(KC):
                last = pe.transpose(psT[h][:, c * P:(c + 1) * P], xe[:, h, c * P:(c + 1) * P], ident[:, :])
            last.then_inc(s_T, 1)

        def up(j, h, between=None):
            e = pe.value_load(eidx[0:1, bass.ds(j, 1)], min_val=0, max_val=NEXP - 1) * W1N
            pe.wait_ge(s_gelu, 2 * j + 2)
            pe.wait_ge(s_xl, j + 3)
            for m in range(2):
                for c in range(4):
                    first = True
                    for k in range(KC):
                        at = bass.ds(e + (k * H + (4 * m + c) * P), P)
                        for w, xp in ((w1h, xh), (w1h, xl), (w1l, xh)):
                            last = pe.matmul(psH[h][m][:, c * P:(c + 1) * P], w[:, at], xp[:, h, k, :], start=first,
                                             stop=k == KC - 1 and w is w1l)
                            first = False
                last.then_inc(s_H, 1)
                if between and m == 0:
                    between()

        def down(j, h):
            e = pe.value_load(eidx[0:1, bass.ds(j, 1)], min_val=0, max_val=NEXP - 1) * W2N
            pe.wait_ge(s_hl, j + 3)
            pe.wait_ge(s_y, j + 1)
            for c in range(HC):
                at = bass.ds(e + c * D, D)
                for hp, w in ((hh, w2h), (hh, w2l), (hl, w2h)):
                    last = pe.matmul(psY[h][:, 0:D], hp[:, h, c, :], w[:, at], start=c == 0 and hp is hh and w is w2h,
                                     stop=c == HC - 1 and hp is hl)
            last.then_inc(s_Y, 1)

        pe.sem_inc(s_xl, 2)
        pe.sem_inc(s_gelu, 4)
        transposes(0, 0, 0)
        up(0, 0, lambda: transposes(1, 1, 0))
        with pe.Fori(0, JT - 1) as i:
            up(2 * i + 1, 1, lambda: transposes(2 * i + 2, 0, i + 1))
            down(2 * i, 0)
            up(2 * i + 2, 0, lambda: transposes(2 * i + 3, 1, i + 1))
            down(2 * i + 1, 1)
        up(SLOT_TILES - 1, 1)
        down(SLOT_TILES - 2, 0)
        down(SLOT_TILES - 1, 1)


_INS = ['x', 'src', 'dst', 'edge_weight', 'L0_gnn_W1', 'L0_gnn_b1', 'L0_gnn_W2', 'L0_gnn_b2', 'L0_mix_Wqkv',
        'L0_mix_Wout', 'L0_mix_gamma', 'L0_ffn_Wr', 'L0_ffn_br', 'L0_ffn_ln_g', 'L0_ffn_ln_b', 'L0_ffn_W1',
        'L0_ffn_b1', 'L0_ffn_W2', 'L0_ffn_b2']
_PAD = {'src': 0, 'dst': N - 1, 'edge_weight': 0}


def kernel(**inputs):
    import numpy as _np
    import concourse.bacc as _bacc
    from concourse import mybir as _mybir
    from concourse.bass_utils import run_bass_kernel_spmd as _run

    nc = _bacc.Bacc("TRN2", target_bir_lowering=False, num_devices=1)
    arrays, args = {}, []
    for name in _INS:
        a = _np.ascontiguousarray(inputs[name])
        if name in _PAD:
            a = _np.pad(a, (0, ET * P - E), constant_values=_PAD[name])
        arrays[f"in_{name}_dram"] = a
        args.append(nc.dram_tensor(f"in_{name}_dram", a.shape, _mybir.dt.from_np(a.dtype), kind="ExternalInput").ap())
    args.append(nc.dram_tensor("out_0_dram", (N + P, D), _mybir.dt.float32, kind="ExternalOutput").ap())
    program(nc, *args)
    r = _run(nc, [arrays], core_ids=[0])
    return r.results[0]["out_0_dram"][:N]
```

```python
import concourse.bass as bass
from concourse import mybir
from contextlib import ExitStack

F32 = mybir.dt.float32
F16 = mybir.dt.float16
I32 = mybir.dt.int32
U32 = mybir.dt.uint32
ALU = mybir.AluOpType
ACT = mybir.ActivationFunctionType
X = mybir.AxisListType.X

P = 128
N = 6250
D = 256
KC = D // P
NT = -(-N // P)
FULL = N // P
LAG = 8
LAST = N - FULL * P
E = 106250
HALF = 8
PER_IT = 2 * HALF
EIT = -(-E // (P * PER_IT))
ET = EIT * PER_IT
EB = -(-ET // P)
GROUP = 4
W = 64
ACCN = NT * P + W
HEADS = 8
DH = D // HEADS
CTX = 4
CTX_IT = FULL // CTX
NEXP = 8
H = 1024
HC = H // P
CAP = NT * P + P
ROW = D + 4
SLOT_TILES = 2 * (-(-(2 * N // P + NEXP) // 2))
WSCALE = 64.0


def program(nc, x, src, dst, edge_weight, gnn_W1, gnn_b1, gnn_W2, gnn_b2, Wqkv, Wout, gamma,
            Wr, br, ln_g, ln_b, ffn_W1, ffn_b1, ffn_W2, ffn_b2, out):
    xn_table = nc.dram_tensor("xn_table", (N, D), F32, kind="Internal").ap()
    slots = nc.dram_tensor("slots", (NEXP * CAP + P, ROW), F32, kind="Internal").ap()
    with ExitStack() as ctx:
        base = ctx.enter_context(nc.sbuf_tensor("base", [P, NEXP], F32))
        pid = ctx.enter_context(nc.sbuf_tensor("pid", [P, 1], F32))
        ident = ctx.enter_context(nc.sbuf_tensor("ident", [P, P], F32))
        padrow = ctx.enter_context(nc.sbuf_tensor("padrow", [P, ROW], F32))
        banks = [ctx.enter_context(nc.psum_tensor(f"bank{i}", [P, 512], F32)) for i in range(8)]
        with ExitStack() as part:
            nodes_and_edges(nc, part, banks, base, pid, ident, padrow, xn_table, slots, x, src, dst, edge_weight,
                            gnn_W1, gnn_b1, gnn_W2, gnn_b2, Wqkv, Wout, gamma, Wr, br, out)
        with ExitStack() as part:
            experts(nc, part, banks, base, pid, ident, padrow, slots, ln_g, ln_b, ffn_W1, ffn_b1, ffn_W2, ffn_b2, out)


class Chain:

    def __init__(self, eng, sem, start=0):
        self.eng, self.sem, self.start, self.n = eng, sem, start, 0

    def did(self, ins):
        ins.then_inc(self.sem, 1)
        self.n += 1

    def settle(self):
        self.eng.wait_ge(self.sem, self.start + self.n)

    def __call__(self, ins):
        self.did(ins)
        self.settle()


def nodes_and_edges(nc, part, banks, base, pid, ident, padrow, xn_table, slots, x, src, dst, edge_weight,
                    gnn_W1, gnn_b1, gnn_W2, gnn_b2, Wqkv, Wout, gamma, Wr, br, out):
    def sb(name, shape, dt=F32):
        return part.enter_context(nc.sbuf_tensor(name, shape, dt))

    def sem(name):
        return part.enter_context(nc.semaphore(name))

    acc_flat = sb("acc", [P, KC * ACCN])
    acc = acc_flat[:, :].rearrange("p (c n) -> p c n", c=KC)
    xall = acc_flat[:, 0:NT * D].rearrange("p (t d) -> p t d", d=D)
    st6 = sb("st6", [P, NT, 6])
    mean = sb("mean", [P, NT])
    rstd = sb("rstd", [P, NT])
    tmp49 = sb("tmp49", [P, NT])
    xs = sb("xs", [P, 2, 4, D])
    xsT = sb("xsT", [P, 2, KC, 4 * P])
    kmaxg = sb("kmaxg", [P, KC, 13])
    kmaxb = sb("kmaxb", [P, D])
    kmax = sb("kmax", [P, KC])
    e_raw = sb("e_raw", [P, EB, P], I32)
    s_raw = sb("s_raw", [P, EB, P], I32)
    e_blk = sb("e_blk", [P, EB, P])
    s_blk = sb("s_blk", [P, EB, P])
    w_blk = sb("w_blk", [P, EB, P])
    floor_ = sb("floor_", [P, EB])
    dabs = sb("dabs", [P, EB, P])
    gbase = sb("gbase", [P, EB])
    ends = sb("edge_ends", [P, 3, EB])
    badc = sb("badc", [P, 1])
    good = sb("good", [P, 1])
    flag = sb("flag", [P, 1], I32)
    dst0 = sb("dst0", [1, ET // GROUP], I32)
    dwT = sb("dwT", [P, 2, ET + PER_IT])
    dstT, wT = dwT[:, 0, :], dwT[:, 1, :]
    dw = [sb(f"dw{h}", [P, 2, HALF]) for h in range(2)]
    first4 = sb("first4", [P, P])
    dabT = sb("dabT", [P, ET + PER_IT])
    srcT = sb("srcT", [P, ET + PER_IT])
    wallT = sb("wallT", [P, ET + PER_IT])
    idx = [sb(f"idx{h}", [P, HALF], I32) for h in range(2)]
    got = [sb(f"got{h}", [P, HALF, D]) for h in range(2)]
    hot = [sb(f"hot{h}", [P, HALF, W]) for h in range(2)]
    gidx = sb("gidx", [P, 1], I32)
    gdw = sb("gdw", [P, 2])
    ghot = sb("ghot", [P, P])
    iota = sb("iota", [P, P])
    iota8 = sb("iota8", [P, NEXP])
    node0 = sb("node0", [P, 1])
    tri = sb("tri", [P, P])
    ones = sb("ones", [P, P])
    zeros = sb("zeros", [P, D + KC])
    wqkv = sb("wqkv", [P, KC, 3 * D])
    wraw = sb("wraw", [P, 2, KC, D])
    w1T = sb("w1T", [P, KC, D])
    w2T = sb("w2T", [P, KC, D])
    wout = sb("wout", [P, KC, D])
    M = sb("M", [P, KC, D])
    bd = sb("bd", [P, KC, P])
    ksum = sb("ksum", [P, KC])
    wr = sb("wr", [P, KC, NEXP])
    brow = sb("brow", [1, 2, D])
    bsum = sb("bsum", [1, D])
    br_row = sb("br_row", [1, NEXP])
    gam = sb("gam", [P, D])
    xin = sb("xin", [P, CTX, D])
    xT = sb("xT", [P, 2, KC, P])
    ek = sb("ek", [P, 2, D])
    v = sb("v", [P, 2, D])
    xn_in = sb("xn_in", [P, D])
    x_in = sb("x_in", [P, D])
    nT = sb("nT", [P, KC, P])
    sT = sb("sT", [P, KC, P])
    qs = sb("qs", [P, D])
    eq = sb("eq", [P, D])
    qn = sb("qn", [P, D])
    qT = sb("qT", [P, KC, P])
    hd = sb("hd", [P, 3, HEADS])
    gr = sb("gr", [P, D])
    gl = sb("gl", [P, D])
    sq = sb("sq", [P, D])
    bn = sb("bn", [P, 3, 6])
    mv = sb("mv", [P, 3, 2])
    eps = sb("eps", [P, 1])
    ss = sb("ss", [P, 1])
    sd = sb("sd", [P, 4])
    rs = sb("rs", [P, 4])
    t1 = sb("t1", [P, D])
    t2 = sb("t2", [P, D])
    x2 = sb("x2", [P, D])
    x2n = sb("x2n", [P, D])
    x2T = sb("x2T", [P, KC, P])
    row = sb("row", [P, ROW])
    lg = sb("lg", [P, NEXP])
    top = sb("top", [P, NEXP])
    topi = sb("topi", [P, NEXP], U32)
    topf = sb("topf", [P, 2])
    oh = sb("oh", [P, 3, NEXP])
    gt = sb("gt", [P, 5])
    rk = sb("rk", [P, NEXP])
    prod = sb("prod", [P, 2, NEXP])
    slotf = sb("slotf", [P, 2])
    slot = sb("slot", [P, 2], I32)
    tokens = sb("tokens", [P, NT])

    psE = [banks[0], banks[1]]
    psT = banks[2]
    psTc = [banks[2], banks[7]]
    psKV = [banks[3], banks[4]]
    psC = banks[5]

    s_x = [sem(f"s_xload{g}") for g in range(7)]
    s_w = sem("s_w")
    s_e = sem("s_e")
    s_gp = sem("s_gp")
    s_const = sem("s_const")
    s_dve = sem("s_dve")
    s_var = sem("s_var")
    s_st = sem("s_st")
    s_std = sem("s_std")
    s_xs = sem("s_xs")
    s_tab = [sem(f"s_tab{h}") for h in range(2)]
    s_stored = sem("s_stored")
    s_xsTp = sem("s_xsTp")
    s_xsT = sem("s_xsT")
    s_kT = sem("s_kT")
    s_km = sem("s_km")
    s_wt = sem("s_wt")
    s_wtc = sem("s_wtc")
    s_nk = sem("s_nk")
    s_nkc = sem("s_nkc")
    s_blkT = sem("s_blkT")
    s_blkc = sem("s_blkc")
    s_raw0 = sem("s_raw0")
    s_dabs = sem("s_dabs")
    s_gb = sem("s_gb")
    s_bad = sem("s_bad")
    s_badb = sem("s_badb")
    s_flag = sem("s_flag")
    s_table = sem("s_table")
    s_idx = sem("s_idx")
    s_dw = sem("s_dw")
    s_hot = sem("s_hot")
    s_got = [[sem(f"s_got{h}_{k}") for k in range(HALF)] for h in range(2)]
    s_mult = sem("s_mult")
    s_acc = sem("s_acc")
    s_hold = sem("s_hold")
    s_holdv, s_holdp = sem("s_holdv"), sem("s_holdp")
    s_gi, s_gg, s_gm, s_gd, s_gc = (sem(f"s_general{i}") for i in range(5))
    s_cl = [sem(f"s_cl{b}") for b in range(CTX)]
    s_cT = sem("s_cT")
    s_cx = sem("s_cx")
    s_ckv = sem("s_ckv")
    s_ckd = sem("s_ckd")
    s_cek = sem("s_cek")
    s_cc = sem("s_cc")
    s_bd = sem("s_bd")
    s_mp = sem("s_mp")
    s_M = sem("s_M")
    s_nl, s_nlx = sem("s_nl"), sem("s_nlx")
    s_nT = sem("s_nT")
    s_nTc = sem("s_nTc")
    s_sT = sem("s_sT")
    s_q = sem("s_q")
    s_g = sem("s_g")
    s_qs = sem("s_qs")
    s_eq = sem("s_eq")
    s_qn = sem("s_qn")
    s_qT = sem("s_qT")
    s_qTc = sem("s_qTc")
    s_mix = sem("s_mix")
    s_gl = sem("s_gl")
    s_v = sem("s_v")
    s_sd = sem("s_sd")
    s_x2 = sem("s_x2ready")
    s_x2free = sem("s_x2free")
    s_out = sem("s_out")
    s_x2n = sem("s_x2n")
    s_x2T = sem("s_x2T")
    s_x2Tc = sem("s_x2Tc")
    s_lg = sem("s_lg")
    s_d = sem("s_d")
    s_ed = sem("s_ed")
    s_both = sem("s_both")
    s_rank = sem("s_rank")
    s_slot = sem("s_slot")
    s_sc = [sem(f"s_sc{k}") for k in range(2)]
    s_gr = sem("s_gr")
    s_lk = sem("s_lk")
    s_front, s_back, s_router = sem("s_front"), sem("s_back"), sem("s_router")

    NW = 14
    NCONST = 8

    def rows_of(t):
        return LAST if isinstance(t, int) and t == FULL else P

    block = part.enter_context(nc.Block())

    @block.sync
    def _(sp):
        sp.wait_ge(s_raw0, 1)
        sp.dma_start(e_raw[:, 0:EB - 1, :], dst[0:(EB - 1) * P * P].rearrange("(b p e) -> p b e", p=P, e=P)).then_inc(s_e, 16)
        LB = ET - (EB - 1) * P
        sp.dma_start(e_raw[0:LB, EB - 1, :], dst[(EB - 1) * P * P:ET * P].rearrange("(p e) -> p e", e=P)).then_inc(s_e, 16)
        for g in range(6):
            sp.dma_start(xall[:, 8 * g:8 * g + 8, :],
                         x[8 * g * P:8 * (g + 1) * P, :].rearrange("(t p) d -> p t d", p=P)).then_inc(s_x[g], 16)
        sp.wait_ge(s_const, 3)
        sp.dma_start(xall[0:LAST, FULL, :], x[FULL * P:N, :]).then_inc(s_x[6], 16)
        with sp.Fori(0, 6) as g:
            for h in range(2):
                sp.wait_ge(s_xs, 2 * g + h + 1)
                sp.dma_start(xn_table[bass.ds((2 * g + h) * 4 * P, 4 * P), :].rearrange("(t p) d -> p t d", p=P),
                             xs[:, h, :, :]).then_inc(s_tab[h], 16)
                sp.wait_ge(s_tab[h], 16 * g + 16)
                sp.sem_inc(s_stored, 1)
        sp.wait_ge(s_xs, 13)
        sp.dma_start(xn_table[FULL * P:N, :], xs[0:LAST, 0, 0, :]).then_inc(s_tab[0], 16)
        sp.wait_ge(s_tab[0], 16 * 7)
        sp.dma_start(out[N:N + P, :], zeros[:, 0:D]).then_inc(s_out, 16)
        sp.sem_inc(s_table, 1)

        def context_load(t, b):
            rows = rows_of(t)
            sp.wait_ge(s_cT, t + 1)
            sp.dma_start(xin[0:rows, b, :], xn_table[bass.ds(t * P, rows), :]).then_inc(s_cl[b], 16)

        def xn_load(t):
            rows = rows_of(t)
            sp.wait_ge(s_nT, t + 1)
            sp.dma_start(xn_in[0:rows, :], xn_table[bass.ds(t * P, rows), :]).then_inc(s_nl, 16)

        def x_load(t):
            rows = rows_of(t)
            sp.wait_ge(s_x2free, t + 1)
            sp.dma_start(x_in[0:rows, :], x[bass.ds(t * P, rows), :]).then_inc(s_nlx, 16)

        def node_store(t):
            rows = rows_of(t)
            sp.wait_ge(s_x2, t + 1)
            sp.dma_start(out[bass.ds(t * P, rows), :], x2[0:rows, :]).then_inc(s_out, 16)

        with sp.Fori(0, CTX_IT) as i:
            for b in range(CTX):
                context_load(i * CTX + b, b)
        context_load(FULL, 0)
        xn_load(0)
        x_load(0)
        with sp.Fori(0, FULL - 1) as t:
            xn_load(t + 1)
            x_load(t + 1)
            node_store(t)
        xn_load(FULL)
        x_load(FULL)
        node_store(FULL - 1)
        node_store(FULL)
        sp.wait_ge(s_out, 16 * NT + 16)

    @block.gpsimd
    def _(pool):
        def diagonal(buf, op, fill, pattern, mult, base_=0):
            return pool.affine_select(out=buf, in_=buf, compare_op=op, fill=fill, base=base_, pattern=pattern,
                                      channel_multiplier=mult)

        pool.memset(ident[:, :], 0.0).then_inc(s_gp, 1)
        pool.memset(tri[:, :], 1.0).then_inc(s_gp, 1)
        pool.iota(iota[:, :], pattern=[[1, P]], base=0, channel_multiplier=0,
                  allow_small_or_imprecise_dtypes=True).then_inc(s_gp, 1)
        pool.iota(pid[:, :], pattern=[[0, 1]], base=0, channel_multiplier=1,
                  allow_small_or_imprecise_dtypes=True).then_inc(s_gp, 1)
        pool.iota(iota8[:, :], pattern=[[1, NEXP]], base=0, channel_multiplier=0,
                  allow_small_or_imprecise_dtypes=True).then_inc(s_gp, 1)
        pool.iota(base[:, :], pattern=[[CAP, NEXP]], base=0, channel_multiplier=0,
                  allow_small_or_imprecise_dtypes=True).then_inc(s_gp, 1)
        pool.iota(floor_[:, :], pattern=[[P, EB]], base=0, channel_multiplier=1,
                  allow_small_or_imprecise_dtypes=True).then_inc(s_gp, 1)
        pool.iota(padrow[:, D:D + 1], pattern=[[0, 1]], base=N, channel_multiplier=1,
                  allow_small_or_imprecise_dtypes=True).then_inc(s_gp, 1)
        pool.memset(first4[:, :], 1.0).then_inc(s_gp, 1)
        pool.iota(tokens[:, :], pattern=[[P, NT]], base=0, channel_multiplier=1,
                  allow_small_or_imprecise_dtypes=True).then_inc(s_gp, 1)
        pool.wait_ge(s_gp, 10)
        diagonal(ident[:, :], ALU.not_equal, 1.0, [[-1, P]], 1).then_inc(s_gp, 1)
        diagonal(tri[:, :], ALU.is_gt, 0.0, [[1, P]], -1).then_inc(s_gp, 1)
        view = first4[:, :].rearrange("p (g r) -> p g r", r=GROUP)
        diagonal(view, ALU.is_equal, 0.0, [[-GROUP, P // GROUP], [0, GROUP]], 1).then_inc(s_gp, 1)
        pool.wait_ge(s_const, 10)
        for k in range(2):
            r = slice(k * P // 2, (k + 1) * P // 2)
            pool.dma_start(slots[NEXP * CAP + k * P // 2:NEXP * CAP + (k + 1) * P // 2, :], padrow[r, :]).then_inc(s_sc[k], 16)

        pool.wait_ge(s_flag, 1)
        pool.wait_ge(s_table, 1)
        bad = pool.value_load(flag[0:1, 0:1], min_val=0, max_val=1)
        with pool.If(bad):
            with pool.Fori(0, ET) as t:
                pool.wait_ge(s_gi, t + 1)
                pool.sem_inc(s_hold, 1)
                pool.indirect_dma_start(out=got[0][:, 0, :], out_offset=None, in_=xn_table[:, :],
                                        in_offset=bass.IndirectOffsetOnAxis(ap=gidx[:, 0:1], axis=0)).then_inc(s_gg, 16)

        def gathers(i, h):
            pool.wait_ge(s_idx, 2 * i + h + 1)
            pool.sem_inc(s_hold, 1)
            for k in range(HALF):
                pool.indirect_dma_start(out=got[h][:, k, :], out_offset=None, in_=xn_table[:, :],
                                        in_offset=bass.IndirectOffsetOnAxis(ap=idx[h][:, k:k + 1], axis=0)
                                        ).then_inc(s_got[h][k], 16)

        def scatters(t):
            rows = rows_of(t)
            pool.wait_ge(s_slot, t + 2)
            pool.sem_inc(s_hold, 1)
            for k in range(2):
                pool.indirect_dma_start(out=slots[:, :], out_offset=bass.IndirectOffsetOnAxis(ap=slot[0:rows, k:k + 1], axis=0),
                                        in_=row[0:rows, :], in_offset=None).then_inc(s_sc[k], 16)

        with pool.Fori(0, CTX_IT + 3) as i:
            gathers(i, 0)
            gathers(i, 1)
        with pool.Fori(CTX_IT + 3, EIT) as i:
            gathers(i, 0)
            scatters(i - (CTX_IT + 3))
            gathers(i, 1)
        with pool.Fori(EIT - CTX_IT - 3, FULL) as t:
            scatters(t)
        scatters(FULL)
        for k in range(2):
            pool.wait_ge(s_sc[k], 16 * NT + 16)

    @block.scalar
    def _(act):
        act.wait_ge(s_raw0, 2)
        act.dma_start(s_raw[:, 0:EB - 1, :], src[0:(EB - 1) * P * P].rearrange("(b p e) -> p b e", p=P, e=P)).then_inc(s_e, 16)
        LB = ET - (EB - 1) * P
        act.dma_start(s_raw[0:LB, EB - 1, :], src[(EB - 1) * P * P:ET * P].rearrange("(p e) -> p e", e=P)).then_inc(s_e, 16)
        act.dma_start(w_blk[:, 0:EB - 1, :], edge_weight[0:(EB - 1) * P * P].rearrange("(b p e) -> p b e", p=P, e=P)).then_inc(s_e, 16)
        act.dma_start(w_blk[0:LB, EB - 1, :], edge_weight[(EB - 1) * P * P:ET * P].rearrange("(p e) -> p e", e=P)).then_inc(s_e, 16)
        act.dma_start(dst0[0:1, :], dst[0:ET * P].rearrange("(t e) -> e t", e=GROUP * P)[0:1, :],
                      allow_slow_non_contiguous=True).then_inc(s_e, 16)

        def two(ap):
            return ap.rearrange("(c p) n -> p c n", p=P)

        act.dma_start(wqkv[:, :, :], two(Wqkv)).then_inc(s_w, 16)
        act.dma_start(wraw[:, 0, :, :], two(gnn_W1)).then_inc(s_w, 16)
        act.dma_start(wraw[:, 1, :, :], two(gnn_W2)).then_inc(s_w, 16)
        act.dma_start(wout[:, :, :], two(Wout)).then_inc(s_w, 16)
        act.dma_start(wr[:, :, :], two(Wr)).then_inc(s_w, 16)
        act.dma_start(brow[0:1, 0, :], gnn_b1.rearrange("(a n) -> a n", a=1)).then_inc(s_w, 16)
        act.dma_start(brow[0:1, 1, :], gnn_b2.rearrange("(a n) -> a n", a=1)).then_inc(s_w, 16)
        act.dma_start(br_row[0:1, :], br.rearrange("(a n) -> a n", a=1)).then_inc(s_w, 16)
        act.dma_start(gam[:, :], gamma.partition_broadcast(P)).then_inc(s_w, 16)
        act.wait_ge(s_var, 1)
        act.activation(rstd[:, :], tmp49[:, :], ACT.Sqrt).then_inc(s_std, 1)

        def group_copy(g, h):
            act.wait_ge(s_xsTp, g + 3)
            act.wait_ge(s_kT, g + 1)
            for c in range(KC):
                last = act.activation(xsT[:, h, c, :], banks[c][:, :], ACT.Copy)
            last.then_inc(s_xsT, 1)

        with act.Fori(0, 6) as g:
            for h in range(2):
                group_copy(2 * g + h, h)
        act.wait_ge(s_xsTp, 15)
        act.wait_ge(s_kT, 13)
        for c in range(KC):
            last = act.activation(xsT[:, 0, c, 0:P], banks[c][:, 0:P], ACT.Copy)
        last.then_inc(s_xsT, 1)

        for m, wt in enumerate((w1T, w2T)):
            act.wait_ge(s_wt, m + 1)
            act.activation(wt[:, :, :].rearrange("p c n -> p (c n)"), banks[4 + m][:, :], ACT.Copy).then_inc(s_wtc, 1)

        def context_copy(t, h):
            rows = rows_of(t)
            act.wait_ge(s_cT, t + CTX + 1)
            act.wait_ge(s_ckv, t + 1)
            act.activation(xT[:, h, :, 0:rows], psTc[h][:, 0:256].rearrange("p (c n) -> p c n", c=KC)[:, :, 0:rows],
                           ACT.Copy).then_inc(s_cx, 1)

        def context_exp(t, h):
            rows = rows_of(t)
            act.wait_ge(s_ckd, t + 3)
            act.activation(ek[0:rows, h, :], ek[0:rows, h, :], ACT.Exp).then_inc(s_cek, 1)

        context_copy(0, 0)
        context_copy(1, 1)
        context_exp(0, 0)
        with act.Fori(0, CTX_IT - 1) as i:
            for c in range(CTX):
                context_copy(i * CTX + c + 2, c % 2)
                context_exp(i * CTX + c + 1, (c + 1) % 2)
        for t in range(FULL - CTX, FULL):
            if t + 2 <= FULL:
                context_copy(t + 2, t % 2)
            context_exp(t + 1, (t + 1) % 2)

        def node(n, m):
            rows = rows_of(n)
            r = slice(0, rows)
            act.wait_ge(s_nT, n + 2)
            act.activation(nT[:, :, 0:rows], psT[:, 0:256].rearrange("p (c n) -> p c n", c=KC)[:, :, 0:rows],
                           ACT.Copy).then_inc(s_nTc, 1)
            if m is not None:
                gate_exp(m)
            act.wait_ge(s_qs, n + 1)
            act.activation(eq[r, :], qs[r, :], ACT.Exp).then_inc(s_eq, 1)
            act.wait_ge(s_g, n + 1)
            act.activation(gr[r, :], banks[4][r, 0:D], ACT.Copy).then_inc(s_gr, 1)
            act.wait_ge(s_qT, n + 1)
            act.activation(qT[:, :, 0:rows], psT[:, 256:512].rearrange("p (c n) -> p c n", c=KC)[:, :, 0:rows],
                           ACT.Copy).then_inc(s_qTc, 1)
            act.wait_ge(s_lk, n + 1)
            act.activation(sq[r, :], gl[r, :], ACT.Square, accum_out=ss[r, 0:1]).then_inc(s_gl, 1)
            act.wait_ge(s_gl, n + 1)
            act.activation(sd[r, 0:1], ss[r, 0:1], ACT.Sqrt).then_inc(s_sd, 1)
            for k in range(3):
                act.wait_ge(s_v, 3 * n + k + 1)
                act.activation(sd[r, k + 1:k + 2], mv[r, k, 1:2], ACT.Sqrt, bias=eps[r, 0:1]).then_inc(s_sd, 1)
                if k == 1:
                    act.wait_ge(s_x2T, n + 1)
                    act.activation(x2T[:, :, 0:rows], banks[7][:, 0:256].rearrange("p (c n) -> p c n", c=KC)[:, :, 0:rows],
                                   ACT.Copy).then_inc(s_x2Tc, 1)

        def gate_exp(m):
            rows = rows_of(m)
            act.wait_ge(s_d, m + 1)
            act.activation(gt[0:rows, 1:2], gt[0:rows, 0:1], ACT.Exp).then_inc(s_ed, 1)

        node(0, None)
        with act.Fori(1, FULL) as t:
            node(t, t - 1)
        node(FULL, FULL - 1)
        gate_exp(FULL)

    @block.vector
    def _(dve):
        one = Chain(dve, s_dve)
        dve.memset(e_raw[:, EB - 1, :], 0).then_inc(s_raw0, 1)
        dve.memset(s_raw[:, EB - 1, :], 0).then_inc(s_raw0, 1)
        dve.memset(xall[:, FULL, :], 0.0).then_inc(s_const, 1)
        dve.memset(ones[:, :], 1.0).then_inc(s_const, 1)
        dve.memset(zeros[:, :], 0.0).then_inc(s_const, 1)
        dve.memset(eps[:, :], 1e-5).then_inc(s_const, 1)
        dve.memset(padrow[:, 0:D], 0.0).then_inc(s_const, 1)
        dve.memset(padrow[:, D + 1:ROW], 0.0).then_inc(s_const, 1)
        dve.memset(bd[:, :, :], 0.0).then_inc(s_const, 1)
        for buf in (srcT, dstT, wT):
            dve.memset(buf[:, ET:ET + PER_IT], 0.0).then_inc(s_const, 1)
        LB = ET - (EB - 1) * P
        dve.wait_ge(s_e, 16 * 7)
        dve.wait_ge(s_gp, 13)
        dve.tensor_copy(dabs[:, :, :], e_raw[:, :, :]).then_inc(s_dabs, 1)
        one.did(dve.tensor_copy(s_blk[:, :, :], s_raw[:, :, :]))
        one.did(dve.tensor_scalar(floor_[:, :], floor_[:, :], float(P // PER_IT), -float(P * LAG), op0=ALU.mult, op1=ALU.add))
        dve.wait_ge(s_gb, 1)
        one(dve.tensor_copy(gbase[:, :], banks[6][:, 0:EB]))
        one(dve.tensor_tensor(e_blk[:, :, :], dabs[:, :, :], gbase[:, :].unsqueeze(2).to_broadcast([P, EB, P]), ALU.subtract))
        one.did(dve.reduce_max(ends[:, 0, :], e_blk[:, :, :], axis=X))
        one(dve.tensor_reduce(ends[:, 1, :], e_blk[:, :, :], axis=X, op=ALU.min))
        one.did(dve.tensor_tensor(ends[:, 2, :], ends[:, 1, :], gbase[:, :], ALU.add))
        one.did(dve.tensor_scalar(ends[:, 0, :], ends[:, 0, :], float(W), None, op0=ALU.is_ge))
        one(dve.tensor_scalar(ends[:, 1, :], ends[:, 1, :], 0.0, None, op0=ALU.is_lt))
        one(dve.tensor_tensor(ends[:, 2, :], ends[:, 2, :], floor_[:, :], ALU.is_lt))
        one(dve.memset(ends[LB:P, :, EB - 1:EB], 0.0))
        dve.reduce_max(badc[:, :], ends[:, :, :].rearrange("p k b -> p (k b)"), axis=X).then_inc(s_bad, 1)
        for b in range(EB):
            n = P if b < EB - 1 else LB
            dve.wait_ge(s_blkT, b + 1)
            dve.tensor_copy(srcT[:, b * P:b * P + n], banks[4][:, 0:n])
            dve.tensor_copy(dstT[:, b * P:b * P + n], banks[5][:, 0:n])
            dve.tensor_copy(dabT[:, b * P:b * P + n], banks[6][:, 0:n])
            dve.tensor_copy(wallT[:, b * P:b * P + n], banks[7][:, 0:n]).then_inc(s_blkc, 1)
        dve.wait_ge(s_badb, 1)
        one(dve.reduce_max(good[:, :], banks[6][:, 0:P], axis=X))
        one(dve.tensor_copy(flag[:, :], good[:, :]))
        one(dve.tensor_scalar(good[:, :], good[:, :], -1.0, 1.0, op0=ALU.mult, op1=ALU.add))
        one(dve.tensor_scalar(wT[:, 0:ET], wallT[:, 0:ET], good[:, 0:1], None, op0=ALU.mult))
        for g in range(6):
            dve.wait_ge(s_x[g], 16)
            with dve.Fori(8 * g, 8 * g + 8) as t:
                dve.bn_stats(st6[:, bass.ds(t, 1), :], xall[:, bass.ds(t, 1), :]).then_inc(s_st, 1)
        dve.wait_ge(s_x[6], 16)
        dve.bn_stats(st6[:, FULL, :], xall[:, FULL, :]).then_inc(s_st, 1)
        dve.wait_ge(s_st, NT)
        one(dve.tensor_tensor(mean[:, :], st6[:, :, 1], st6[:, :, 4], ALU.add))
        one(dve.tensor_scalar(mean[:, :], mean[:, :], 0.5, None, op0=ALU.mult))
        one(dve.tensor_tensor(tmp49[:, :], st6[:, :, 1], st6[:, :, 4], ALU.subtract))
        one(dve.tensor_tensor(tmp49[:, :], tmp49[:, :], tmp49[:, :], ALU.mult))
        one(dve.tensor_scalar(tmp49[:, :], tmp49[:, :], 0.25, 1e-5, op0=ALU.mult, op1=ALU.add))
        one(dve.tensor_tensor(rstd[:, :], st6[:, :, 2], st6[:, :, 5], ALU.add))
        dve.scalar_tensor_tensor(out=tmp49[:, :], in0=rstd[:, :], scalar=1.0 / D, in1=tmp49[:, :],
                                 op0=ALU.mult, op1=ALU.add).then_inc(s_var, 1)
        dve.wait_ge(s_std, 1)
        one(dve.reciprocal(rstd[:, :], rstd[:, :]))

        def normalise(t, h, k):
            return dve.tensor_scalar(xs[:, h, k, :], xall[:, bass.ds(t, 1), :].rearrange("p a d -> p (a d)"),
                                     mean[:, bass.ds(t, 1)], rstd[:, bass.ds(t, 1)], op0=ALU.subtract, op1=ALU.mult)

        def key_max(g, cols):
            dve.wait_ge(s_kT, g + 3)
            for c in range(KC):
                last = dve.reduce_max(kmaxg[:, c, bass.ds(g, 1)], banks[2 + c][:, 0:cols], axis=X)
            last.then_inc(s_km, 1)

        def normalise_group(g, h):
            dve.wait_ge(s_stored, g + 1)
            dve.wait_ge(s_xsTp, g + 1)
            for k in range(4):
                last = normalise(4 * g + k, h, k)
            last.then_inc(s_xs, 1)

        normalise_group(0, 0)
        with dve.Fori(0, 5) as g:
            normalise_group(2 * g + 1, 1)
            key_max(2 * g, 4 * P)
            normalise_group(2 * g + 2, 0)
            key_max(2 * g + 1, 4 * P)
        normalise_group(11, 1)
        key_max(10, 4 * P)
        dve.wait_ge(s_stored, 13)
        dve.wait_ge(s_xsTp, 13)
        normalise(FULL, 0, 0).then_inc(s_xs, 1)
        key_max(11, 4 * P)
        key_max(12, LAST)
        dve.wait_ge(s_km, 14)
        dve.memset(acc_flat[:, :], 0.0).then_inc(s_dve, 1)
        one.n += 1
        one(dve.reduce_max(kmax[:, :], kmaxg[:, :, :], axis=X))
        dve.sem_inc(s_nk, 1)
        dve.wait_ge(s_nkc, 1)
        one(dve.tensor_copy(kmaxb[:, :], banks[6][:, 0:D]))
        dve.wait_ge(s_w, 16 * 9)
        dve.tensor_tensor(bsum[0:1, :], brow[0:1, 0, :], brow[0:1, 1, :], ALU.add).then_inc(s_wtc, 1)
        dve.sem_inc(s_flag, 1)

        bad = dve.value_load(flag[0:1, 0:1], min_val=0, max_val=1)
        with dve.If(bad):
            with dve.Fori(0, ET) as t:
                dve.tensor_scalar(gidx[:, :], srcT[:, bass.ds(t, 1)], 0.0, None, op0=ALU.add).then_inc(s_gi, 1)
                dve.tensor_scalar(gdw[:, 0:1], dabT[:, bass.ds(t, 1)], 0.0, None, op0=ALU.add)
                dve.tensor_scalar(gdw[:, 1:2], wallT[:, bass.ds(t, 1)], 0.0, None, op0=ALU.add)
                dve.memset(node0[:, :], 0.0).then_inc(s_gc, 1)
                dve.wait_ge(s_gc, t * (3 * NT + 1) + 1)
                dve.sem_inc(s_holdv, 1)
                with dve.Fori(0, NT) as n:
                    done = t * (3 * NT + 1) + 1 + n * 3
                    dve.tensor_scalar(ghot[:, :], iota[:, :], node0[:, 0:1], gdw[:, 0:1], op0=ALU.add, op1=ALU.is_equal).then_inc(s_gc, 1)
                    dve.wait_ge(s_gc, done + 1)
                    dve.tensor_scalar(ghot[:, :], ghot[:, :], gdw[:, 1:2], None, op0=ALU.mult).then_inc(s_gc, 1)
                    dve.wait_ge(s_gc, done + 2)
                    dve.sem_inc(s_gd, 1)
                    dve.tensor_scalar(node0[:, :], node0[:, :], float(P), None, op0=ALU.add)
                    dve.wait_ge(s_gm, t * NT + n + 1)
                    dve.tensor_tensor(acc[:, :, bass.ds(n * P, P)], acc[:, :, bass.ds(n * P, P)],
                                      banks[7][:, 0:256].rearrange("p (c n) -> p c n", c=KC), ALU.add).then_inc(s_gc, 1)
                    dve.wait_ge(s_gc, done + 3)

        GPH = HALF // GROUP
        d0 = [dve.alloc_register(f"first_dst{g}") for g in range(2 * GPH)]

        def stage(i, h):
            t = i * PER_IT + h * HALF
            dve.tensor_scalar(idx[h][:, :], srcT[:, bass.ds(t, HALF)], 0.0, None, op0=ALU.add).then_inc(s_idx, 1)
            dve.tensor_scalar(dw[h][:, :, :], dwT[:, :, bass.ds(t, HALF)], 0.0, None, op0=ALU.add).then_inc(s_dw, 1)

        def hots(i, h, ks=range(HALF)):
            for k in ks:
                if k == 0:
                    dve.wait_ge(s_dw, 2 * i + h + 1)
                ins = dve.tensor_scalar(hot[h][:, k, :], iota[:, 0:W], dw[h][:, 0, k:k + 1], dw[h][:, 1, k:k + 1],
                                        op0=ALU.is_equal, op1=ALU.mult)
                if k == HALF - 1:
                    ins.then_inc(s_hot, 1)

        def adds(i, h):
            dve.wait_ge(s_mult, 2 * i + h + 1)
            stage(i + 1, h)
            if h == 0:
                dve.load(d0, dst0[0:1, bass.ds(i * 2 * GPH, 2 * GPH)])
            for g in range(GPH):
                dve.wait_ge(s_acc, 2 * GPH + (2 * i + h) * GPH + g)
                first = dve.snap(d0[h * GPH + g], min_val=0, max_val=N - 1)
                view = acc[:, :, bass.ds(first, W)]
                dve.tensor_tensor(view, view, psE[h][:, g * KC * W:(g + 1) * KC * W].rearrange("p (c w) -> p c w", c=KC),
                                  ALU.add).then_inc(s_acc, 1)

        for h in range(2):
            stage(0, h)
        hots(0, 0)

        def keys_values(t, h):
            r = slice(0, rows_of(t))
            dve.wait_ge(s_ckv, t + 3)
            dve.wait_ge(s_cc, t + 1)
            dve.tensor_tensor(ek[r, h, :], psKV[h][r, 0:D], kmaxb[r, :], ALU.subtract)
            dve.tensor_scalar(v[r, h, :], psKV[h][r, D:2 * D], 0.0, None, op0=ALU.add).then_inc(s_ckd, 1)

        def context_iteration(i):
            hots(i, 1)
            for c in range(CTX):
                if c % 2:
                    adds(i, c // 2)
                if c == 1:
                    hots(i + 1, 0)
                keys_values(i * CTX + c + 1, (c + 1) % 2)

        keys_values(0, 0)
        with dve.Fori(0, CTX_IT - 1) as i:
            context_iteration(i)
        context_iteration(CTX_IT - 1)

        FRONT, BACK, ROUTER = 3, 8, 19

        def fill(i, h, ks):
            if i is not None:
                hots(i, h, ks)

        def node_front(n, i):
            rows = rows_of(n)
            r = slice(0, rows)
            ch = Chain(dve, s_front, n * FRONT)
            dve.wait_ge(s_nTc, n + 1)
            dve.wait_ge(s_acc, 2 * GPH + 2 * GPH * (EIT if i is None else i))
            dve.scalar_tensor_tensor(out=sT[:, :, 0:rows], in0=nT[:, :, 0:rows], scalar=1.0,
                                     in1=acc[:, :, bass.ds(n * P, rows)], op0=ALU.add, op1=ALU.mult).then_inc(s_sT, 1)
            dve.wait_ge(s_q, n + 1)
            q8 = banks[3][r, 0:D].rearrange("p (h e) -> p h e", h=HEADS)
            qs8, eq8, qn8 = (b[r, :].rearrange("p (h e) -> p h e", h=HEADS) for b in (qs, eq, qn))
            ch.did(dve.reduce_max(hd[r, 0, :], q8, axis=X))
            fill(i, 1, (4,))
            ch.settle()
            dve.tensor_tensor(qs8, q8, hd[r, 0, :].unsqueeze(2).to_broadcast([rows, HEADS, DH]), ALU.subtract).then_inc(s_qs, 1)
            fill(i, 1, (5, 6, 7))
            dve.wait_ge(s_eq, n + 1)
            ch(dve.reduce_sum(hd[r, 1, :], eq8, axis=X))
            ch(dve.reciprocal(hd[r, 2, :], hd[r, 1, :]))
            dve.tensor_tensor(qn8, eq8, hd[r, 2, :].unsqueeze(2).to_broadcast([rows, HEADS, DH]), ALU.mult).then_inc(s_qn, 1)
            dve.wait_ge(s_gr, n + 2)
            dve.scalar_tensor_tensor(out=gl[r, :], in0=gr[r, :], scalar=0.2, in1=gr[r, :], op0=ALU.mult, op1=ALU.max).then_inc(s_lk, 1)
            assert ch.n == FRONT, ch.n

        def node_back(n, i):
            r = slice(0, rows_of(n))
            ch = Chain(dve, s_back, n * BACK)
            dve.wait_ge(s_mix, n + 1)
            ch(dve.bn_stats(bn[r, 0, :], banks[6][r, 0:D]))
            dve.sem_inc(s_holdv, 1)
            dve.bn_aggr(mv[r, 0, :], bn[r, 0, :]).then_inc(s_v, 1)
            dve.wait_ge(s_sd, 4 * n + 1)
            ch(dve.tensor_scalar(sd[r, 0:1], sd[r, 0:1], 1e-12, None, op0=ALU.max))
            ch.did(dve.reciprocal(rs[r, 0:1], sd[r, 0:1]))
            dve.wait_ge(s_v, 3 * n + 1)
            ch.did(dve.scalar_tensor_tensor(out=t2[r, :], in0=banks[6][r, 0:D], scalar=mv[r, 0, 0:1], in1=gam[r, :],
                                            op0=ALU.subtract, op1=ALU.mult))
            ch.settle()
            dve.wait_ge(s_nlx, 16 * n + 16)
            dve.scalar_tensor_tensor(out=t1[r, :], in0=gl[r, :], scalar=rs[r, 0:1], in1=x_in[r, :],
                                     op0=ALU.mult, op1=ALU.add).then_inc(s_x2free, 1)
            dve.wait_ge(s_sd, 4 * n + 2)
            ch.did(dve.reciprocal(rs[r, 1:2], sd[r, 1:2]))
            fill(i, 0, (0,))
            ch.settle()
            dve.wait_ge(s_x2free, n + 2)
            dve.wait_ge(s_out, 16 * n + 16)
            dve.scalar_tensor_tensor(out=x2[r, :], in0=t2[r, :], scalar=rs[r, 1:2], in1=t1[r, :],
                                     op0=ALU.mult, op1=ALU.add).then_inc(s_x2, 1)
            fill(i, 0, (1,))
            dve.wait_ge(s_x2, n + 1)
            ch.did(dve.bn_stats(bn[r, 1, :], x2[r, :]))
            fill(i, 0, (2,))
            ch.settle()
            dve.sem_inc(s_holdv, 1)
            dve.bn_aggr(mv[r, 1, :], bn[r, 1, :]).then_inc(s_v, 1)
            fill(i, 0, (3, 4))
            dve.wait_ge(s_sd, 4 * n + 3)
            ch.did(dve.reciprocal(rs[r, 2:3], sd[r, 2:3]))
            fill(i, 0, (5,))
            ch.settle()
            dve.tensor_scalar(x2n[r, :], x2[r, :], mv[r, 1, 0:1], rs[r, 2:3], op0=ALU.subtract, op1=ALU.mult).then_inc(s_x2n, 1)
            fill(i, 0, (6,))
            dve.wait_ge(s_x2n, n + 1)
            ch.did(dve.bn_stats(bn[r, 2, :], x2n[r, :]))
            fill(i, 0, (7,))
            ch.settle()
            dve.sem_inc(s_holdv, 1)
            dve.bn_aggr(mv[r, 2, :], bn[r, 2, :]).then_inc(s_v, 1)
            assert ch.n == BACK, ch.n

        def router_top(m, i):
            r = slice(0, rows_of(m))
            ch = Chain(dve, s_router, m * ROUTER)
            dve.wait_ge(s_lg, m + 1)
            ch.did(dve.tensor_copy(lg[r, :], banks[7][r, 256:256 + NEXP]))
            dve.wait_ge(s_sd, 4 * m + 4)
            ch.did(dve.reciprocal(rs[r, 3:4], sd[r, 3:4]))
            ch.settle()
            dve.sem_inc(s_holdv, 1)
            ch.did(dve.max(top[r, :], lg[r, :]))
            fill(i, 1, (0,))
            ch.settle()
            dve.tensor_tensor(gt[r, 0:1], top[r, 1:2], top[r, 0:1], ALU.subtract).then_inc(s_d, 1)
            ch.did(dve.max_index(topi[r, :], top[r, :], lg[r, :]))
            fill(i, 1, (1,))
            ch.settle()
            ch.did(dve.tensor_copy(topf[r, :], topi[r, 0:2]))
            for k in range(2):
                dve.wait_ge(s_sc[k], 16 * m + 16)
            ch.did(dve.tensor_scalar(row[r, 0:D], x2n[r, :], mv[r, 2, 0:1], rs[r, 3:4], op0=ALU.subtract, op1=ALU.mult))
            ch.settle()
            ch.did(dve.tensor_scalar(oh[r, 0, :], iota8[r, :], topf[r, 0:1], None, op0=ALU.is_equal))
            ch.did(dve.tensor_scalar(oh[r, 1, :], iota8[r, :], topf[r, 1:2], None, op0=ALU.is_equal))
            fill(i, 1, (2,))
            ch.settle()
            dve.tensor_tensor(oh[r, 2, :], oh[r, 0, :], oh[r, 1, :], ALU.add).then_inc(s_both, 1)
            fill(i, 1, (3,))
            return ch

        def router_slots(m, ch):
            rows = rows_of(m)
            r = slice(0, rows)
            dve.wait_ge(s_ed, m + 1)
            ch.did(dve.tensor_scalar(gt[r, 2:3], gt[r, 1:2], 1.0, None, op0=ALU.add))
            dve.wait_ge(s_rank, m + 1)
            ch.did(dve.tensor_tensor(rk[r, :], banks[7][r, 264:264 + NEXP], base[r, :], ALU.add))
            ch.settle()
            ch.did(dve.reciprocal(gt[r, 3:4], gt[r, 2:3]))
            ch.did(dve.tensor_tensor(base[:, :], base[:, :], banks[7][:, 272:272 + NEXP], ALU.add))
            ch.did(dve.tensor_tensor(prod[r, :, :], oh[r, 0:2, :], rk[r, :].unsqueeze(1).to_broadcast([rows, 2, NEXP]), ALU.mult))
            ch.settle()
            ch.did(dve.tensor_tensor(row[r, D + 2:D + 3], gt[r, 1:2], gt[r, 3:4], ALU.mult))
            ch.did(dve.reduce_sum(slotf[r, :], prod[r, :, :], axis=X))
            ch.did(dve.tensor_copy(row[r, D + 1:D + 2], topf[r, 0:1]))
            ch.settle()
            ch.did(dve.tensor_tensor(row[r, D + 3:D + 4], gt[r, 3:4], row[r, D + 2:D + 3], ALU.subtract))
            ch.did(dve.tensor_scalar(row[r, D:D + 1], tokens[r, bass.ds(m, 1)], 0.0, None, op0=ALU.add))
            dve.tensor_copy(slot[r, :], slotf[r, :]).then_inc(s_router, 1)
            ch.n += 1
            ch.settle()
            dve.sem_inc(s_slot, 1)
            assert ch.n == ROUTER, ch.n

        def node(i, n, m):
            if m is not None:
                ch = router_top(m, i)
            else:
                fill(i, 1, range(4))
            node_front(n, i)
            if m is not None:
                router_slots(m, ch)
            if i is not None:
                adds(i, 0)
            node_back(n, None if i is None else i + 1)
            if i is not None:
                adds(i, 1)

        hots(CTX_IT, 1)
        adds(CTX_IT, 0)
        hots(CTX_IT + 1, 0)
        dve.wait_ge(s_cc, NT + 2)
        one(dve.reciprocal(ksum[:, :], psC[:, D:D + KC]))
        one(dve.tensor_scalar(ksum[:, :], ksum[:, :], float(DH) ** -0.5, None, op0=ALU.mult))
        for c in range(KC):
            for b in range(P // DH):
                b_ = slice(b * DH, (b + 1) * DH)
                last = dve.tensor_copy(bd[b_, c, b * DH:(b + 1) * DH], psC[b_, c * P + b * DH:c * P + (b + 1) * DH])
        last.then_inc(s_bd, 1)
        dve.wait_ge(s_mp, 1)
        for c in range(KC):
            last = dve.tensor_scalar(M[:, c, :], banks[6][:, c * D:(c + 1) * D], ksum[:, c:c + 1], None, op0=ALU.mult)
        last.then_inc(s_M, 1)
        adds(CTX_IT, 1)
        node(CTX_IT + 1, 0, None)
        with dve.Fori(CTX_IT + 2, EIT) as i:
            node(i, i - (CTX_IT + 1), i - (CTX_IT + 2))
        with dve.Fori(EIT - CTX_IT - 1, FULL) as t:
            node(None, t, t - 1)
        node(None, FULL, FULL - 1)
        router_slots(FULL, router_top(FULL, None))

    @block.tensor
    def _(pe):
        def mm(o, lhsT, rhs, start, stop, **kw):
            return pe.matmul(o, lhsT, rhs, start=start, stop=stop, **kw)

        pe.sem_inc(s_kT, 2)
        pe.sem_inc(s_cT, CTX)
        pe.sem_inc(s_ckv, 2)
        pe.sem_inc(s_cc, 2)
        pe.sem_inc(s_nT, 1)
        pe.sem_inc(s_stored, 2)
        pe.sem_inc(s_xsTp, 2)
        pe.sem_inc(s_x2free, 1)
        pe.sem_inc(s_slot, 1)
        pe.sem_inc(s_gr, 1)
        pe.wait_ge(s_gp, 13)
        pe.wait_ge(s_const, 10)
        pe.wait_ge(s_dabs, 1)
        mm(banks[6][:, 0:EB], first4[:, :], dabs[:, :, 0], True, True).then_inc(s_gb, 1)
        pe.wait_ge(s_bad, 1)
        LB = ET - (EB - 1) * P
        for b in range(EB):
            n = P if b < EB - 1 else LB
            if b:
                pe.wait_ge(s_blkc, b)
            for bank, a in ((4, s_blk[0:n, b, :]), (5, e_blk[0:n, b, :]), (6, dabs[0:n, b, :]), (7, w_blk[0:n, b, :])):
                last = pe.transpose(banks[bank][:, 0:n], a, ident[0:n, 0:n])
            last.then_inc(s_blkT, 1)
        pe.wait_ge(s_blkc, EB)
        mm(banks[6][:, 0:P], badc[:, 0:1].to_broadcast([P, P]), ident[:, :], True, True).then_inc(s_badb, 1)
        pe.wait_ge(s_w, 16 * 9)
        for m in range(2):
            for c in range(KC):
                for o in range(KC):
                    last = pe.transpose(banks[4 + m][:, c * D + o * P:c * D + (o + 1) * P], wraw[:, m, o, c * P:(c + 1) * P], ident[:, :])
            last.then_inc(s_wt, 1)

        def group(g, h, tiles):
            pe.wait_ge(s_xs, g + 1)
            pe.wait_ge(s_xsT, g + 2)
            for c in range(KC):
                for k in range(tiles):
                    last = pe.transpose(banks[c][:, k * P:(k + 1) * P], xs[:, h, k, c * P:(c + 1) * P], ident[:, :])
            last.then_inc(s_xsTp, 1)
            pe.wait_ge(s_xsT, g + 3)
            pe.wait_ge(s_km, g + 1)
            for o in range(KC):
                for c in range(KC):
                    last = mm(banks[2 + o][:, 0:tiles * P], wqkv[:, c, D + o * P:D + (o + 1) * P],
                              xsT[:, h, c, 0:tiles * P], c == 0, c == KC - 1)
            last.then_inc(s_kT, 1)

        pe.sem_inc(s_xsT, 2)
        pe.sem_inc(s_km, 1)
        with pe.Fori(0, 6) as g:
            for h in range(2):
                group(2 * g + h, h, 4)
        group(12, 0, 1)
        pe.wait_ge(s_nk, 1)
        for c in range(KC):
            last = mm(banks[6][:, c * P:(c + 1) * P], kmax[:, c:c + 1].to_broadcast([P, P]), ident[:, :], True, True)
        last.then_inc(s_nkc, 1)
        pe.wait_ge(s_flag, 1)
        bad = pe.value_load(flag[0:1, 0:1], min_val=0, max_val=1)
        with pe.If(bad):
            with pe.Fori(0, ET) as t:
                pe.wait_ge(s_gg, 16 * t + 16)
                pe.sem_inc(s_holdp, 1)
                with pe.Fori(0, NT) as n:
                    pe.wait_ge(s_gd, t * NT + n + 1)
                    for c in range(KC):
                        last = mm(banks[7][:, c * P:(c + 1) * P], got[0][:, 0, c * P:(c + 1) * P], ghot[:, :], True, True)
                    last.then_inc(s_gm, 1)

        pe.sem_inc(s_acc, 2 * (HALF // GROUP))
        pe.sem_inc(s_cx, 2)
        pe.sem_inc(s_ckd, 2)

        def edges(i, q):
            h, g = divmod(q, HALF // GROUP)
            if g == 0:
                pe.wait_ge(s_acc, (2 * i + h + 1) * (HALF // GROUP))
                pe.wait_ge(s_hot, 2 * i + h + 1)
            for k in range(g * GROUP, (g + 1) * GROUP):
                pe.wait_ge(s_got[h][k], 16 * i + 16)
                for c in range(KC):
                    last = mm(psE[h][:, (g * KC + c) * W:(g * KC + c + 1) * W], got[h][:, k, c * P:(c + 1) * P],
                              hot[h][:, k, :], g == 0 and k == 0 and c == 0, k == HALF - 1 and c == KC - 1,
                              skip_group_check=True)
            if k == HALF - 1:
                last.then_inc(s_mult, 1)

        def ctx_T(t, b, loads):
            h, rows = b % 2, rows_of(t)
            pe.wait_ge(s_cl[b], 16 * loads)
            pe.wait_ge(s_cx, t + 1)
            for k in range(KC):
                last = pe.transpose(psTc[h][:, k * P:k * P + rows], xin[0:rows, b, k * P:(k + 1) * P], ident[0:rows, 0:rows])
            last.then_inc(s_cT, 1)

        def ctx_kv(t, h):
            rows = rows_of(t)
            pe.wait_ge(s_cx, t + 3)
            pe.wait_ge(s_ckd, t + 1)
            for k in range(KC):
                last = mm(psKV[h][0:rows, :], xT[:, h, k, 0:rows], wqkv[:, k, D:3 * D], k == 0, k == KC - 1)
            last.then_inc(s_ckv, 1)

        def ctx_sum(t, h):
            rows = rows_of(t)
            last_tile = isinstance(t, int) and t == FULL
            pe.wait_ge(s_cek, t + 1)
            for k in range(KC):
                mm(psC[:, k * P:(k + 1) * P], v[0:rows, h, k * P:(k + 1) * P], ek[0:rows, h, k * P:(k + 1) * P], False, False, skip_group_check=True)
                last = mm(psC[:, D + k:D + k + 1], ek[0:rows, h, k * P:(k + 1) * P], ones[0:rows, 0:1], False, last_tile, skip_group_check=True)
            last.then_inc(s_cc, 1)

        def context_iteration(i):
            for c in range(CTX):
                t = i * CTX + c
                edges(i, c)
                if not (isinstance(t, int) and t + 2 > FULL):
                    ctx_T(t + 2, (c + 2) % CTX, i + 1 + (c + 2) // CTX)
                ctx_sum(t, c % 2)
                ctx_kv(t + 1, (c + 1) % 2)

        pe.wait_ge(s_wtc, 3)
        mm(psC[:, 0:D + KC], zeros[:, 0:P], zeros[:, 0:D + KC], True, False, skip_group_check=True)
        ctx_T(0, 0, 1)
        ctx_T(1, 1, 1)
        ctx_kv(0, 0)
        with pe.Fori(0, CTX_IT - 1) as i:
            context_iteration(i)
        context_iteration(CTX_IT - 1)
        edges(CTX_IT, 0)
        ctx_sum(FULL, 0)
        edges(CTX_IT, 1)
        pe.wait_ge(s_bd, 1)
        for c in range(KC):
            last = mm(banks[6][:, c * D:(c + 1) * D], bd[:, c, :], wout[:, c, :], True, True)
        last.then_inc(s_mp, 1)
        edges(CTX_IT, 2)
        edges(CTX_IT, 3)
        pe.wait_ge(s_M, 1)

        def node_in(n):
            rows = rows_of(n)
            pe.wait_ge(s_nl, 16 * n + 16)
            for c in range(KC):
                last = pe.transpose(psT[:, c * P:c * P + rows], xn_in[0:rows, c * P:(c + 1) * P], ident[0:rows, 0:rows])
            last.then_inc(s_nT, 1)
            pe.wait_ge(s_nTc, n + 1)
            for c in range(KC):
                last = mm(banks[3][0:rows, 0:D], nT[:, c, 0:rows], wqkv[:, c, 0:D], c == 0, c == KC - 1)
            last.then_inc(s_q, 1)
            pe.wait_ge(s_gr, n + 1)
            mm(banks[4][0:rows, 0:D], nT[:, 0, 0:rows], w1T[:, 0, :], True, False)
            mm(banks[4][0:rows, 0:D], nT[:, 1, 0:rows], w1T[:, 1, :], False, False)
            mm(banks[4][0:rows, 0:D], ones[0:1, 0:rows], bsum[0:1, :], False, False)

        def node_mid(n):
            rows = rows_of(n)
            pe.wait_ge(s_sT, n + 1)
            mm(banks[4][0:rows, 0:D], sT[:, 0, 0:rows], w2T[:, 0, :], False, False)
            mm(banks[4][0:rows, 0:D], sT[:, 1, 0:rows], w2T[:, 1, :], False, True).then_inc(s_g, 1)
            pe.wait_ge(s_qn, n + 1)
            for c in range(KC):
                last = pe.transpose(psT[:, 256 + c * P:256 + c * P + rows], qn[0:rows, c * P:(c + 1) * P], ident[0:rows, 0:rows])
            last.then_inc(s_qT, 1)

        def node_mix(n):
            rows = rows_of(n)
            pe.wait_ge(s_qTc, n + 1)
            for c in range(KC):
                last = mm(banks[6][0:rows, 0:D], qT[:, c, 0:rows], M[:, c, :], c == 0, c == KC - 1)
            last.then_inc(s_mix, 1)

        def node_logits(n):
            rows = rows_of(n)
            pe.wait_ge(s_x2n, n + 1)
            pe.wait_ge(s_slot, n + 1)
            for c in range(KC):
                last = pe.transpose(banks[7][:, c * P:c * P + rows], x2n[0:rows, c * P:(c + 1) * P], ident[0:rows, 0:rows])
            last.then_inc(s_x2T, 1)
            pe.wait_ge(s_x2Tc, n + 1)
            lo = banks[7][0:rows, 256:256 + NEXP]
            for c in range(KC):
                mm(lo, x2T[:, c, 0:rows], wr[:, c, :], c == 0, False)
            mm(lo, ones[0:1, 0:rows], br_row[0:1, :], False, True).then_inc(s_lg, 1)

        def ranks(m):
            rows = rows_of(m)
            pe.wait_ge(s_both, m + 1)
            mm(banks[7][0:rows, 264:264 + NEXP], tri[0:rows, 0:rows], oh[0:rows, 2, :], True, True)
            mm(banks[7][:, 272:272 + NEXP], ones[0:rows, :], oh[0:rows, 2, :], True, True).then_inc(s_rank, 1)

        def node(i, n, m):
            node_in(n)
            if m is not None:
                ranks(m)
            if i is not None:
                edges(i, 0)
            node_mid(n)
            if i is not None:
                edges(i, 1)
            node_mix(n)
            if i is not None:
                edges(i, 2)
                edges(i, 3)
            node_logits(n)

        node(CTX_IT + 1, 0, None)
        with pe.Fori(CTX_IT + 2, EIT) as i:
            node(i, i - (CTX_IT + 1), i - (CTX_IT + 2))
        with pe.Fori(EIT - CTX_IT - 1, FULL) as t:
            node(None, t, t - 1)
        node(None, FULL, FULL - 1)
        ranks(FULL)


def experts(nc, part, banks, base, pid, ident, padrow, slots, ln_g, ln_b, ffn_W1, ffn_b1, ffn_W2, ffn_b2, out):
    def sb(name, shape, dt=F32):
        return part.enter_context(nc.sbuf_tensor(name, shape, dt))

    def sem(name):
        return part.enter_context(nc.semaphore(name))

    W1N, W2N = KC * H, HC * D
    w1h, w1l = (sb(n, [P, NEXP * W1N], F16) for n in ("w1h", "w1l"))
    w2h, w2l = (sb(n, [P, NEXP * W2N], F16) for n in ("w2h", "w2l"))
    w1s = sb("w1s", [P, W1N])
    w2s = sb("w2s", [P, W2N])
    gT = sb("gT", [P, KC, NEXP])
    bT = sb("bT", [P, KC, NEXP])
    grow = sb("grow", [NEXP, 2, D])
    b1raw = sb("b1raw", [NEXP, H])
    b1 = sb("b1", [P, NEXP * HC])
    b2 = sb("b2", [P, NEXP * D])
    cnt = sb("cnt", [P, NEXP])
    tiles = sb("tiles", [P, NEXP])
    ends = sb("ends", [P, NEXP])
    ks = sb("ks", [P, NT])
    big = sb("big", [P, NEXP, SLOT_TILES])
    js = sb("js", [P, SLOT_TILES])
    ej = sb("ej", [P, SLOT_TILES])
    sj = sb("sj", [P, SLOT_TILES])
    ro = sb("ro", [P, SLOT_TILES])
    roff = sb("roff", [P, SLOT_TILES], I32)
    eidx = sb("eidx", [P, SLOT_TILES], I32)
    reg0 = sb("reg0", [P, NEXP])
    padf = sb("padf", [P, NEXP])
    padi = sb("padi", [P, NEXP], I32)
    xe = sb("xe", [P, 2, ROW])
    xh, xl = (sb(n, [P, 2, KC, P], F16) for n in ("xh", "xl"))
    h32 = sb("h32", [P, 2, HC, P])
    hh, hl = (sb(n, [P, 2, HC, P], F16) for n in ("hh", "hl"))
    y = sb("y", [P, 2, D])
    yg = sb("yg", [P, 2, D])
    gates = sb("gates", [P, SLOT_TILES])
    tokf = sb("tokf", [P, SLOT_TILES])
    toki = [sb(f"toki{h}", [P, 1], I32) for h in range(2)]
    psT = [banks[0], banks[7]]
    psH = [[banks[1], banks[2]], [banks[3], banks[4]]]
    psY = [banks[5], banks[6]]

    s_c = sem("f_c")
    s_ch = sem("f_ch")
    s_l = [sem(f"f_l{i}") for i in range(2)]
    s_b = sem("f_b")
    s_bT = sem("f_bT")
    s_bTc = sem("f_bTc")
    s_w1s = sem("f_w1s")
    s_hi = sem("f_hi")
    s_hi2 = sem("f_hi2")
    s_lo = sem("f_lo")
    s_pb = sem("f_pb")
    s_pi = sem("f_pi")
    s_pad = sem("f_pad")
    s_tab = sem("f_tab")
    s_padded = sem("f_padded")
    s_xe = [sem(f"f_xe{h}") for h in range(2)]
    s_hold = sem("f_hold")
    s_T = sem("f_T")
    s_xh = sem("f_xh")
    s_xl = sem("f_xl")
    s_H = sem("f_H")
    s_gelu = sem("f_gelu")
    s_hh = sem("f_hh")
    s_hl = sem("f_hl")
    s_Y = sem("f_Y")
    s_y1 = sem("f_y1")
    s_gt = sem("f_gt")
    s_y = sem("f_y")
    s_add = sem("f_add")
    s_g = sem("f_g")
    JT = SLOT_TILES // 2

    block = part.enter_context(nc.Block())

    @block.sync
    def _(sp):
        sp.dma_start(grow[:, 0, :], ln_g).then_inc(s_b, 16)
        sp.dma_start(grow[:, 1, :], ln_b).then_inc(s_b, 16)
        sp.dma_start(b1raw[:, :], ffn_b1).then_inc(s_b, 16)
        sp.dma_start(b2[:, :], ffn_b2.rearrange("e d -> (e d)").partition_broadcast(P)).then_inc(s_b, 16)
        w1v = ffn_W1.rearrange("e (c p) h -> e p c h", p=P)
        w2v = ffn_W2.rearrange("e (c p) d -> e p c d", p=P)
        for e in range(NEXP):
            if e:
                sp.wait_ge(s_lo, e)
            sp.dma_start(w1s[:, :].rearrange("p (c h) -> p c h", c=KC), w1v[e]).then_inc(s_l[0], 16)
            sp.dma_start(w2s[:, :].rearrange("p (c d) -> p c d", c=HC), w2v[e]).then_inc(s_l[1], 16)
        sp.wait_ge(s_tab, 1)
        sp.wait_ge(s_padded, 16 * NEXP)
        with sp.Fori(0, JT) as i:
            for h in range(2):
                j = 2 * i + h
                r = sp.value_load(roff[0:1, bass.ds(j, 1)], min_val=0, max_val=NEXP * CAP)
                sp.wait_ge(s_xl, j + 1)
                sp.dma_start(xe[:, h, :], slots[bass.ds(r, P), :]).then_inc(s_xe[h], 16)

    @block.gpsimd
    def _(pool):
        pool.iota(ks[:, :], pattern=[[P, NT]], base=0, channel_multiplier=0,
                  allow_small_or_imprecise_dtypes=True).then_inc(s_c, 1)
        pool.iota(js[:, :], pattern=[[1, SLOT_TILES]], base=0, channel_multiplier=0,
                  allow_small_or_imprecise_dtypes=True).then_inc(s_c, 1)
        pool.iota(reg0[:, :], pattern=[[CAP, NEXP]], base=0, channel_multiplier=0,
                  allow_small_or_imprecise_dtypes=True).then_inc(s_c, 1)
        pool.wait_ge(s_pad, 1)
        for e in range(NEXP):
            pool.indirect_dma_start(out=slots[:, :], out_offset=bass.IndirectOffsetOnAxis(ap=padi[:, e:e + 1], axis=0),
                                    in_=padrow[:, :], in_offset=None).then_inc(s_padded, 16)
        with pool.Fori(0, JT) as i:
            for h in range(2):
                j = 2 * i + h
                pool.wait_ge(s_y, j + 3)
                if h:
                    pool.wait_ge(s_add, 32 * i + 16)
                    pool.sem_inc(s_hold, 1)
                else:
                    pool.wait_ge(s_g, i + 1)
                    pool.sem_inc(s_hold, 1)
                pool.indirect_dma_start(out=out[:, :], out_offset=bass.IndirectOffsetOnAxis(ap=toki[h][:, 0:1], axis=0),
                                        in_=yg[:, h, :], in_offset=None, compute_op=ALU.add).then_inc(s_add, 16)
            pool.wait_ge(s_add, 32 * i + 32)
            pool.sem_inc(s_g, 1)

    @block.scalar
    def _(act):
        for e in range(NEXP):
            act.wait_ge(s_w1s, e + 1)
            act.activation(w1h[:, e * W1N:(e + 1) * W1N], w1s[:, :], ACT.Copy).then_inc(s_hi, 1)
            act.wait_ge(s_l[1], 16 * e + 16)
            act.activation(w2h[:, e * W2N:(e + 1) * W2N], w2s[:, :], ACT.Copy, scale=WSCALE).then_inc(s_hi2, 1)

        def gelu(j, h, m, e8):
            act.wait_ge(s_H, 2 * j + 5 + m)
            act.sem_inc(s_hold, 1)
            for c in range(4):
                last = act.activation(h32[:, h, 4 * m + c, :], psH[h][m][:, c * P:(c + 1) * P], ACT.Gelu,
                                      bias=b1[:, bass.ds(e8 + (4 * m + c), 1)], scale=1.0 / WSCALE)
            last.then_inc(s_gelu, 1)

        def tile(j, h):
            act.wait_ge(s_hl, j + 1)
            act.sem_inc(s_hold, 1)
            e8 = act.value_load(eidx[0:1, bass.ds(j, 1)], min_val=0, max_val=NEXP - 1) * HC
            gelu(j, h, 0, e8)
            gelu(j, h, 1, e8)

        act.wait_ge(s_tab, 1)
        with act.Fori(0, JT) as i:
            tile(2 * i, 0)
            tile(2 * i + 1, 1)

    @block.vector
    def _(dve):
        ch = Chain(dve, s_ch)
        dve.wait_ge(s_c, 3)
        ch(dve.tensor_tensor(cnt[:, :], base[:, :], reg0[:, :], ALU.subtract))
        ch(dve.tensor_scalar(padf[:, :], base[:, :], pid[:, 0:1], None, op0=ALU.add))
        dve.tensor_copy(padi[:, :], padf[:, :]).then_inc(s_pad, 1)
        ch(dve.tensor_tensor(big[:, :, 0:NT], cnt[:, :].unsqueeze(2).to_broadcast([P, NEXP, NT]),
                             ks[:, :].unsqueeze(1).to_broadcast([P, NEXP, NT]), ALU.is_gt))
        ch(dve.reduce_sum(tiles[:, :], big[:, :, 0:NT], axis=X))
        ch(dve.tensor_copy(ends[:, 0:1], tiles[:, 0:1]))
        for e in range(1, NEXP):
            ch(dve.tensor_tensor(ends[:, e:e + 1], ends[:, e - 1:e], tiles[:, e:e + 1], ALU.add))
        ch(dve.tensor_tensor(big[:, :, :], js[:, :].unsqueeze(1).to_broadcast([P, NEXP, SLOT_TILES]),
                             ends[:, :].unsqueeze(2).to_broadcast([P, NEXP, SLOT_TILES]), ALU.is_ge))
        ch(dve.reduce_sum(ej[:, :], big[:, :, :].rearrange("p e j -> p j e"), axis=X))
        ch(dve.tensor_tensor(big[:, :, :], big[:, :, :], tiles[:, :].unsqueeze(2).to_broadcast([P, NEXP, SLOT_TILES]), ALU.mult))
        ch(dve.reduce_sum(sj[:, :], big[:, :, :].rearrange("p e j -> p j e"), axis=X))
        ch(dve.tensor_tensor(sj[:, :], js[:, :], sj[:, :], ALU.subtract))
        ch(dve.tensor_scalar(sj[:, :], sj[:, :], float(P), None, op0=ALU.mult))
        ch(dve.scalar_tensor_tensor(out=ro[:, :], in0=ej[:, :], scalar=float(CAP), in1=sj[:, :], op0=ALU.mult, op1=ALU.add))
        ch(dve.tensor_scalar(ro[:, :], ro[:, :], float(NEXP * CAP), None, op0=ALU.min))
        ch(dve.tensor_copy(roff[:, :], ro[:, :]))
        ch(dve.tensor_scalar(sj[:, :], ej[:, :], float(NEXP - 1), None, op0=ALU.min))
        ch(dve.tensor_copy(eidx[:, :], sj[:, :]))
        dve.wait_ge(s_bT, 1)
        ch(dve.tensor_copy(gT[:, :, :].rearrange("p c e -> p (c e)"), banks[0][:, 0:16]))
        ch(dve.tensor_copy(bT[:, :, :].rearrange("p c e -> p (c e)"), banks[0][:, 16:32]))
        ch(dve.tensor_copy(b1[:, :].rearrange("p (e c) -> p e c", c=HC),
                           banks[0][:, 32:96].rearrange("p (c e) -> p e c", c=HC)))
        dve.sem_inc(s_bTc, 1)
        for e in range(NEXP):
            dve.wait_ge(s_pb, e + 1)
            ch(dve.tensor_tensor(b1[:, e * HC:(e + 1) * HC], b1[:, e * HC:(e + 1) * HC], banks[1][:, (e % 2) * HC:(e % 2) * HC + HC], ALU.add))
            for c in range(KC):
                last = dve.tensor_scalar(w1s[:, c * H:(c + 1) * H], w1s[:, c * H:(c + 1) * H], gT[:, c, e:e + 1], WSCALE,
                                         op0=ALU.mult, op1=ALU.mult)
            last.then_inc(s_w1s, 1)
            dve.wait_ge(s_hi, e + 1)
            dve.tensor_tensor(w1l[:, e * W1N:(e + 1) * W1N], w1s[:, :], w1h[:, e * W1N:(e + 1) * W1N], ALU.subtract)
            dve.wait_ge(s_hi2, e + 1)
            dve.scalar_tensor_tensor(out=w2l[:, e * W2N:(e + 1) * W2N], in0=w2s[:, :], scalar=WSCALE,
                                     in1=w2h[:, e * W2N:(e + 1) * W2N], op0=ALU.mult, op1=ALU.subtract).then_inc(s_lo, 1)
        dve.wait_ge(s_lo, NEXP)
        dve.sem_inc(s_tab, 1)
        dve.sem_inc(s_hl, 2)
        dve.sem_inc(s_y, 2)
        dve.sem_inc(s_H, 4)
        dve.sem_inc(s_hh, 2)

        def split_x(j, h):
            dve.wait_ge(s_xe[h], 16 * (j // 2 if isinstance(j, int) else pair(j, h)) + 16)
            dve.tensor_scalar(gates[:, bass.ds(j, 1)], xe[:, h, D + 1:D + 2], ej[:, bass.ds(j, 1)], None, op0=ALU.is_equal).then_inc(s_gt, 1)
            dve.tensor_scalar(tokf[:, bass.ds(j, 1)], xe[:, h, D:D + 1], 0.0, None, op0=ALU.add)
            dve.wait_ge(s_gt, j + 1)
            dve.scalar_tensor_tensor(out=gates[:, bass.ds(j, 1)], in0=gates[:, bass.ds(j, 1)], scalar=xe[:, h, D + 3:D + 4],
                                     in1=xe[:, h, D + 2:D + 3], op0=ALU.mult, op1=ALU.add)
            dve.wait_ge(s_T, j + 3)
            dve.wait_ge(s_H, 2 * j + 2)
            dve.tensor_copy(xh[:, h, :, :].rearrange("p c n -> p (c n)"), psT[h][:, 0:256]).then_inc(s_xh, 1)
            dve.wait_ge(s_xh, j + 1)
            dve.tensor_tensor(xl[:, h, :, :].rearrange("p c n -> p (c n)"), psT[h][:, 0:256],
                              xh[:, h, :, :].rearrange("p c n -> p (c n)"), ALU.subtract).then_inc(s_xl, 1)

        at = [None, None]

        def pair(j, h):
            return at[h]

        def split_h(j, h):
            dve.wait_ge(s_Y, j + 1)
            for m in range(2):
                dve.wait_ge(s_gelu, 2 * j + m + 5)
                dve.tensor_copy(hh[:, h, 4 * m:4 * m + 4, :], h32[:, h, 4 * m:4 * m + 4, :]).then_inc(s_hh, 1)
                dve.wait_ge(s_hh, 2 * j + m + 3)
                last = dve.tensor_tensor(hl[:, h, 4 * m:4 * m + 4, :], h32[:, h, 4 * m:4 * m + 4, :], hh[:, h, 4 * m:4 * m + 4, :], ALU.subtract)
            last.then_inc(s_hl, 1)

        def gated(j, h, i):
            e = dve.value_load(eidx[0:1, bass.ds(j, 1)], min_val=0, max_val=NEXP - 1)
            dve.wait_ge(s_Y, j + 3)
            dve.scalar_tensor_tensor(out=y[:, h, :], in0=psY[h][:, 0:D], scalar=1.0 / WSCALE,
                                     in1=b2[:, bass.ds(e * D, D)], op0=ALU.mult, op1=ALU.add).then_inc(s_y1, 1)
            dve.wait_ge(s_y1, j + 1)
            dve.wait_ge(s_g, i + 1)
            dve.tensor_scalar(toki[h][:, :], tokf[:, bass.ds(j, 1)], 0.0, None, op0=ALU.add)
            dve.tensor_scalar(yg[:, h, :], y[:, h, :], gates[:, bass.ds(j, 1)], None, op0=ALU.mult).then_inc(s_y, 1)

        split_x(0, 0)
        split_x(1, 1)
        split_h(0, 0)
        with dve.Fori(0, JT - 1) as i:
            at[0] = i + 1
            split_x(2 * i + 2, 0)
            split_h(2 * i + 1, 1)
            gated(2 * i, 0, i)
            at[1] = i + 1
            split_x(2 * i + 3, 1)
            split_h(2 * i + 2, 0)
            gated(2 * i + 1, 1, i)
        split_h(SLOT_TILES - 1, 1)
        gated(SLOT_TILES - 2, 0, JT - 1)
        gated(SLOT_TILES - 1, 1, JT - 1)

    @block.tensor
    def _(pe):
        pe.sem_inc(s_T, 2)
        pe.sem_inc(s_Y, 2)
        pe.sem_inc(s_g, 1)
        pe.wait_ge(s_b, 64)
        for c in range(KC):
            for k in range(2):
                pe.transpose(banks[0][:, (2 * k + c) * NEXP:(2 * k + c + 1) * NEXP], grow[:, k, c * P:(c + 1) * P], ident[0:NEXP, 0:NEXP])
        for c in range(HC):
            last = pe.transpose(banks[0][:, 32 + c * NEXP:32 + (c + 1) * NEXP], b1raw[:, c * P:(c + 1) * P], ident[0:NEXP, 0:NEXP])
        last.then_inc(s_bT, 1)
        pe.wait_ge(s_bTc, 1)
        for e in range(NEXP):
            pe.wait_ge(s_l[0], 16 * e + 16)
            for c in range(HC):
                for k in range(KC):
                    last = pe.matmul(banks[1][:, (e % 2) * HC + c:(e % 2) * HC + c + 1], w1s[:, k * H + c * P:k * H + (c + 1) * P],
                                     bT[:, k, e:e + 1], start=k == 0, stop=k == KC - 1)
            last.then_inc(s_pb, 1)
        pe.wait_ge(s_tab, 1)

        def transposes(j, h, i):
            pe.wait_ge(s_xe[h], 16 * i + 16)
            pe.wait_ge(s_xl, j + 1)
            for c in range(KC):
                last = pe.transpose(psT[h][:, c * P:(c + 1) * P], xe[:, h, c * P:(c + 1) * P], ident[:, :])
            last.then_inc(s_T, 1)

        def up(j, h, between=None):
            e = pe.value_load(eidx[0:1, bass.ds(j, 1)], min_val=0, max_val=NEXP - 1) * W1N
            pe.wait_ge(s_gelu, 2 * j + 2)
            pe.wait_ge(s_xl, j + 3)
            for m in range(2):
                for c in range(4):
                    first = True
                    for k in range(KC):
                        at = bass.ds(e + (k * H + (4 * m + c) * P), P)
                        for w, xp in ((w1h, xh), (w1h, xl), (w1l, xh)):
                            last = pe.matmul(psH[h][m][:, c * P:(c + 1) * P], w[:, at], xp[:, h, k, :], start=first,
                                             stop=k == KC - 1 and w is w1l)
                            first = False
                last.then_inc(s_H, 1)
                if between and m == 0:
                    between()

        def down(j, h):
            e = pe.value_load(eidx[0:1, bass.ds(j, 1)], min_val=0, max_val=NEXP - 1) * W2N
            pe.wait_ge(s_hl, j + 3)
            pe.wait_ge(s_y, j + 1)
            for c in range(HC):
                at = bass.ds(e + c * D, D)
                for hp, w in ((hh, w2h), (hh, w2l), (hl, w2h)):
                    last = pe.matmul(psY[h][:, 0:D], hp[:, h, c, :], w[:, at], start=c == 0 and hp is hh and w is w2h,
                                     stop=c == HC - 1 and hp is hl)
            last.then_inc(s_Y, 1)

        pe.sem_inc(s_xl, 2)
        pe.sem_inc(s_gelu, 4)
        transposes(0, 0, 0)
        up(0, 0, lambda: transposes(1, 1, 0))
        with pe.Fori(0, JT - 1) as i:
            up(2 * i + 1, 1, lambda: transposes(2 * i + 2, 0, i + 1))
            down(2 * i, 0)
            up(2 * i + 2, 0, lambda: transposes(2 * i + 3, 1, i + 1))
            down(2 * i + 1, 1)
        up(SLOT_TILES - 1, 1)
        down(SLOT_TILES - 2, 0)
        down(SLOT_TILES - 1, 1)


_INS = ['x', 'src', 'dst', 'edge_weight', 'L0_gnn_W1', 'L0_gnn_b1', 'L0_gnn_W2', 'L0_gnn_b2', 'L0_mix_Wqkv',
        'L0_mix_Wout', 'L0_mix_gamma', 'L0_ffn_Wr', 'L0_ffn_br', 'L0_ffn_ln_g', 'L0_ffn_ln_b', 'L0_ffn_W1',
        'L0_ffn_b1', 'L0_ffn_W2', 'L0_ffn_b2']
_PAD = {'src': 0, 'dst': N - 1, 'edge_weight': 0}


def kernel(**inputs):
    import numpy as _np
    import concourse.bacc as _bacc
    from concourse import mybir as _mybir
    from concourse.bass_utils import run_bass_kernel_spmd as _run

    nc = _bacc.Bacc("TRN2", target_bir_lowering=False, num_devices=1)
    arrays, args = {}, []
    for name in _INS:
        a = _np.ascontiguousarray(inputs[name])
        if name in _PAD:
            a = _np.pad(a, (0, ET * P - E), constant_values=_PAD[name])
        arrays[f"in_{name}_dram"] = a
        args.append(nc.dram_tensor(f"in_{name}_dram", a.shape, _mybir.dt.from_np(a.dtype), kind="ExternalInput").ap())
    args.append(nc.dram_tensor("out_0_dram", (N + P, D), _mybir.dt.float32, kind="ExternalOutput").ap())
    program(nc, *args)
    r = _run(nc, [arrays], core_ids=[0])
    return r.results[0]["out_0_dram"][:N]
```

```python
import concourse.bass as bass
from concourse import mybir
from contextlib import ExitStack

F32 = mybir.dt.float32
F16 = mybir.dt.float16
BF16 = mybir.dt.bfloat16
I32 = mybir.dt.int32
U32 = mybir.dt.uint32
ALU = mybir.AluOpType
ACT = mybir.ActivationFunctionType
X = mybir.AxisListType.X

P = 128
N = 6250
D = 256
KC = D // P
NT = -(-N // P)
FULL = N // P
LAST = N - FULL * P
E = 106250
HALF = 8
PER_IT = 2 * HALF
EIT = -(-E // (P * PER_IT))
ET = EIT * PER_IT
EB = -(-ET // P)
GROUP = 4
W = 64
ACCN = NT * P + W
HEADS = 8
DH = D // HEADS
CTX = 12
CTX_IT = FULL // CTX
LAG = CTX_IT
XB = 4
NEXP = 8
H = 1024
HC = H // P
GW = NT * P // 14
GN = NT * P // GW
CAP = NT * P + 2 * P
ROW = D + 4
PAIRS = 2 * (-(-(2 * N // (2 * P) + NEXP) // 2))
WSCALE = 64.0


def program(nc, x, src, dst, edge_weight, gnn_W1, gnn_b1, gnn_W2, gnn_b2, Wqkv, Wout, gamma,
            Wr, br, ln_g, ln_b, ffn_W1, ffn_b1, ffn_W2, ffn_b2, out):
    xn_table = nc.dram_tensor("xn_table", (N, D), F32, kind="Internal").ap()
    xn16_table = nc.dram_tensor("xn16_table", (N, 2 * D), F16, kind="Internal").ap()
    slots = nc.dram_tensor("slots", (NEXP * CAP + 2 * P, ROW), F32, kind="Internal").ap()
    with ExitStack() as ctx:
        base = ctx.enter_context(nc.sbuf_tensor("base", [P, NEXP], F32))
        pid = ctx.enter_context(nc.sbuf_tensor("pid", [P, 1], F32))
        ident = ctx.enter_context(nc.sbuf_tensor("ident", [P, P], F32))
        padrow = ctx.enter_context(nc.sbuf_tensor("padrow", [P, 2, ROW], F32))
        banks = [ctx.enter_context(nc.psum_tensor(f"bank{i}", [P, 512], F32)) for i in range(8)]
        stage0 = ctx.enter_context(nc.sbuf_tensor("stage0", [P, 2 * KC * H], F32))
        with ExitStack() as part:
            nodes_and_edges(nc, part, banks, stage0, ffn_W1, ffn_W2, base, pid, ident, padrow, xn_table, xn16_table,
                            slots, x, src, dst, edge_weight, gnn_W1, gnn_b1, gnn_W2, gnn_b2, Wqkv, Wout, gamma, Wr, br, out)
        with ExitStack() as part:
            experts(nc, part, banks, stage0, base, pid, ident, padrow, slots, ln_g, ln_b, ffn_W1, ffn_b1, ffn_W2, ffn_b2, out)


def load_expert(eng, stage, e, ffn_W1, ffn_W2, sems):
    half = KC * H
    eng.dma_start(stage[:, 0:half].rearrange("p (c h) -> p c h", c=KC),
                  ffn_W1.rearrange("e (c p) h -> e p c h", p=P)[e]).then_inc(sems[0], 16)
    eng.dma_start(stage[:, half:2 * half].rearrange("p (c d) -> p c d", c=HC),
                  ffn_W2.rearrange("e (c p) d -> e p c d", p=P)[e]).then_inc(sems[1], 16)


class Chain:

    def __init__(self, eng, sem, start=0):
        self.eng, self.sem, self.start, self.n = eng, sem, start, 0

    def did(self, ins):
        ins.then_inc(self.sem, 1)
        self.n += 1

    def settle(self):
        self.eng.wait_ge(self.sem, self.start + self.n)

    def __call__(self, ins):
        self.did(ins)
        self.settle()


def nodes_and_edges(nc, part, banks, stage0, ffn_W1, ffn_W2, base, pid, ident, padrow, xn_table, xn16_table,
                    slots, x, src, dst, edge_weight, gnn_W1, gnn_b1, gnn_W2, gnn_b2, Wqkv, Wout, gamma, Wr, br, out):
    def sb(name, shape, dt=F32):
        return part.enter_context(nc.sbuf_tensor(name, shape, dt))

    def sem(name):
        return part.enter_context(nc.semaphore(name))

    acc_flat = sb("acc", [P, KC * ACCN])
    acc = acc_flat[:, :].rearrange("p (c n) -> p c n", c=KC)
    xall = acc_flat[:, 0:NT * D].rearrange("p (t d) -> p t d", d=D)
    st6 = sb("st6", [P, NT, 6])
    mean = sb("mean", [P, NT])
    rstd = sb("rstd", [P, NT])
    tmp49 = sb("tmp49", [P, NT])
    xs01 = sb("xs01", [P, 2, 4, D])
    xs = [xs01[:, 0, :, :], xs01[:, 1, :, :],
          stage0[:, 0:4 * D].rearrange("p (t d) -> p t d", d=D)]
    xsT = sb("xsT", [P, 3, KC, 4 * P], F16)
    kmaxg = sb("kmaxg", [P, KC, 13])
    kmaxb = sb("kmaxb", [P, D])
    kmax = sb("kmax", [P, KC])
    e_raw = sb("e_raw", [P, EB, P], I32)
    s_raw = sb("s_raw", [P, EB, P], I32)
    e_blk = sb("e_blk", [P, EB, P])
    s_blk = sb("s_blk", [P, EB, P])
    w_blk = sb("w_blk", [P, EB, P])
    floor_ = sb("floor_", [P, EB])
    dabs = sb("dabs", [P, EB, P])
    gbase = sb("gbase", [P, EB])
    ends = sb("edge_ends", [P, 5, EB])
    badc = sb("badc", [P, 1])
    good = sb("good", [P, 1])
    flag = sb("flag", [P, 1], I32)
    dst0 = sb("dst0", [1, ET // GROUP], I32)
    dstT = sb("dstT", [P, ET + PER_IT], F16)
    wT = sb("wT", [P, 2, ET + PER_IT], F16)
    wgood = sb("wgood", [P, ET])
    first4 = sb("first4", [P, P])
    dabT = sb("dabT", [P, ET + PER_IT])
    srcT = sb("srcT", [P, ET + PER_IT])
    wallT = sb("wallT", [P, ET + PER_IT])
    idx = [sb(f"idx{h}", [P, HALF], I32) for h in range(2)]
    got = [sb(f"got{h}", [P, HALF, 2 * D], F16) for h in range(2)]
    x16 = [got[0][:, 0:4, :], got[1][:, 0:4, :], got[0][:, 4:8, :]]
    mask = [sb(f"mask{h}", [P, HALF, W], F16) for h in range(2)]
    hot = [sb(f"hot{h}", [P, 2, HALF, W], F16) for h in range(2)]
    gidx = sb("gidx", [P, 1], I32)
    gdw = sb("gdw", [P, 2])
    giota, ghot = (xs[h][:, 0:2, :].rearrange("p a d -> p (a d)")[:, 0:GW] for h in range(2))
    iota = sb("iota", [P, P])
    iota16 = sb("iota16", [P, W], F16)
    ident16 = sb("ident16", [P, P], F16)
    wkvh, wkvl = (sb(n, [P, KC, 2 * D], F16) for n in ("wkvh", "wkvl"))
    iota8 = sb("iota8", [P, NEXP])
    node0 = sb("node0", [P, 1])
    tri = sb("tri", [P, P])
    ones = sb("ones", [P, P])
    zeros = sb("zeros", [P, D + KC])
    wqkv = sb("wqkv", [P, KC, 3 * D])
    wraw = sb("wraw", [P, 2, KC, D])
    w1T = sb("w1T", [P, KC, D])
    w2T = sb("w2T", [P, KC, D])
    wout = sb("wout", [P, KC, D])
    M = sb("M", [P, KC, D])
    bd = sb("bd", [P, KC, P])
    bdT = sb("bdT", [P, KC, P])
    ksum = sb("ksum", [P, KC])
    wr = sb("wr", [P, KC, NEXP])
    brow = sb("brow", [P, 2, D])
    bhi, bmid, bias3 = (sb(n, [P, D], BF16) for n in ("bhi", "bmid", "bias3"))
    ones16 = sb("ones16", [P, P], BF16)
    br_row = sb("br_row", [1, NEXP])
    gam = sb("gam", [P, D])
    xin = sb("xin", [P, XB, 2 * D], F16)
    xT = sb("xT", [P, 2, 2, KC, P], F16)
    ek = sb("ek", [P, 2, D])
    v = sb("v", [P, 2, KC, P + 1])
    xn_in = sb("xn_in", [P, D])
    x_in = sb("x_in", [P, D])
    nT = sb("nT", [P, KC, P])
    sT = sb("sT", [P, KC, P])
    qs = sb("qs", [P, D])
    eq = sb("eq", [P, D])
    qn = sb("qn", [P, D])
    qT = sb("qT", [P, KC, P])
    hd = sb("hd", [P, 3, HEADS])
    gr = sb("gr", [P, D])
    gl = sb("gl", [P, D])
    sq = sb("sq", [P, D])
    bn = sb("bn", [P, 3, 6])
    mv = sb("mv", [P, 3, 2])
    eps = sb("eps", [P, 1])
    ss = sb("ss", [P, 1])
    sd = sb("sd", [P, 4])
    rs = sb("rs", [P, 4])
    t1 = sb("t1", [P, D])
    t2 = sb("t2", [P, D])
    x2 = sb("x2", [P, D])
    x2n = sb("x2n", [P, D])
    x2T = sb("x2T", [P, KC, P])
    row = sb("row", [P, ROW])
    lg = sb("lg", [P, NEXP])
    top = sb("top", [P, NEXP])
    topi = sb("topi", [P, NEXP], U32)
    topf = sb("topf", [P, 2])
    oh = sb("oh", [P, 3, NEXP])
    gt = sb("gt", [P, 5])
    rk = sb("rk", [P, NEXP])
    prod = sb("prod", [P, 2, NEXP])
    slotf = sb("slotf", [P, 2])
    slot = sb("slot", [P, 2], I32)
    tokens = sb("tokens", [P, NT])

    psE = [banks[0], banks[1]]
    psT = banks[2]
    psTc = [banks[2], banks[7]]
    psKV = [banks[3], banks[4]]
    psC = banks[5]

    s_x = [sem(f"s_xload{g}") for g in range(7)]
    s_w0 = sem("s_w0")
    s_w = sem("s_w")
    s_e = sem("s_e")
    s_gp = sem("s_gp")
    s_const = sem("s_const")
    s_dve = sem("s_dve")
    s_var = sem("s_var")
    s_st = sem("s_st")
    s_std = sem("s_std")
    s_xs = sem("s_xs")
    s_tab = [sem(f"s_tab{h}") for h in range(3)]
    s_hi = sem("s_hi")
    s_lo = sem("s_lo")
    s_wk = sem("s_wk")
    s_xsTp = sem("s_xsTp")
    s_xsT = sem("s_xsT")
    s_kT = sem("s_kT")
    s_km = sem("s_km")
    s_wt = sem("s_wt")
    s_wtc = sem("s_wtc")
    s_bias = sem("s_bias")
    s_nk = sem("s_nk")
    s_nkc = sem("s_nkc")
    s_blkT = sem("s_blkT")
    s_blkc = sem("s_blkc")
    s_blka = sem("s_blka")
    s_raw0 = sem("s_raw0")
    s_dabs = sem("s_dabs")
    s_gb = sem("s_gb")
    s_bad = sem("s_bad")
    s_badb = sem("s_badb")
    s_flag = sem("s_flag")
    s_table = sem("s_table")
    s_idx = sem("s_idx")
    s_mask = sem("s_mask")
    s_hot = sem("s_hot")
    s_got = [[sem(f"s_got{h}_{k}") for k in range(HALF)] for h in range(2)]
    s_mult = sem("s_mult")
    s_acc = sem("s_acc")
    s_hold = sem("s_hold")
    s_giota, s_gi, s_gg, s_gz, s_gh, s_gw, s_gm, s_ga = (sem(f"s_general{i}") for i in range(8))
    s_gend = sem("s_gend")
    s_cl = [sem(f"s_cl{b}") for b in range(XB)]
    s_cT = sem("s_cT")
    s_cx = sem("s_cx")
    s_ckv = sem("s_ckv")
    s_ckd = sem("s_ckd")
    s_cks = sem("s_cks")
    s_cek = sem("s_cek")
    s_cc = sem("s_cc")
    s_bd = sem("s_bd")
    s_mp = sem("s_mp")
    s_M = sem("s_M")
    s_nl, s_nlx = sem("s_nl"), sem("s_nlx")
    s_nT = sem("s_nT")
    s_nTc = sem("s_nTc")
    s_sT = sem("s_sT")
    s_q = sem("s_q")
    s_g = sem("s_g")
    s_qs = sem("s_qs")
    s_eq = sem("s_eq")
    s_qn = sem("s_qn")
    s_qT = sem("s_qT")
    s_qTc = sem("s_qTc")
    s_mix = sem("s_mix")
    s_gl = sem("s_gl")
    s_v = sem("s_v")
    s_sd = sem("s_sd")
    s_x2 = sem("s_x2ready")
    s_x2free = sem("s_x2free")
    s_out = sem("s_out")
    s_x2n = sem("s_x2n")
    s_x2T = sem("s_x2T")
    s_x2Tc = sem("s_x2Tc")
    s_lg = sem("s_lg")
    s_d = sem("s_d")
    s_ed = sem("s_ed")
    s_both = sem("s_both")
    s_rank = sem("s_rank")
    s_slot = sem("s_slot")
    s_sc = [sem(f"s_sc{k}") for k in range(2)]
    s_gr = sem("s_gr")
    s_lk = sem("s_lk")
    s_front, s_back, s_router = sem("s_front"), sem("s_back"), sem("s_router")

    def rows_of(t):
        return LAST if isinstance(t, int) and t == FULL else P

    block = part.enter_context(nc.Block())

    @block.sync
    def _(sp):
        sp.wait_ge(s_raw0, 1)
        sp.dma_start(e_raw[:, 0:EB - 1, :], dst[0:(EB - 1) * P * P].rearrange("(b p e) -> p b e", p=P, e=P)).then_inc(s_e, 16)
        LB = ET - (EB - 1) * P
        sp.dma_start(e_raw[0:LB, EB - 1, :], dst[(EB - 1) * P * P:ET * P].rearrange("(p e) -> p e", e=P)).then_inc(s_e, 16)
        for g in range(6):
            sp.dma_start(xall[:, 8 * g:8 * g + 8, :],
                         x[8 * g * P:8 * (g + 1) * P, :].rearrange("(t p) d -> p t d", p=P)).then_inc(s_x[g], 16)
        sp.wait_ge(s_const, 3)
        sp.dma_start(xall[0:LAST, FULL, :], x[FULL * P:N, :]).then_inc(s_x[6], 16)
        def store(g, h, tiles=4):
            sp.wait_ge(s_xs, g + 1)
            sp.dma_start(xn_table[bass.ds(g * 4 * P, tiles * P), :].rearrange("(t p) d -> p t d", p=P),
                         xs[h][:, 0:tiles, :]).then_inc(s_tab[h], 16)
            sp.wait_ge(s_lo, g + 1)
            sp.dma_start(xn16_table[bass.ds(g * 4 * P, tiles * P), :].rearrange("(t p) d -> p t d", p=P),
                         x16[h][:, 0:tiles, :]).then_inc(s_tab[h], 16)

        with sp.Fori(0, 4) as g:
            for h in range(3):
                store(3 * g + h, h)
        sp.wait_ge(s_xs, 13)
        sp.dma_start(xn_table[FULL * P:N, :], xs[0][0:LAST, 0, :]).then_inc(s_tab[0], 16)
        sp.wait_ge(s_lo, 13)
        sp.dma_start(xn16_table[FULL * P:N, :], x16[0][0:LAST, 0, :]).then_inc(s_tab[0], 16)
        sp.wait_ge(s_tab[0], 32 * 5)
        sp.wait_ge(s_tab[1], 32 * 4)
        sp.wait_ge(s_tab[2], 32 * 4)
        load_expert(sp, stage0, 0, ffn_W1, ffn_W2, (s_w0, s_w0))
        sp.dma_start(out[N:N + 2 * P, :].rearrange("(a p) d -> p a d", p=P), zeros[:, 0:D].unsqueeze(1).to_broadcast([P, 2, D])).then_inc(s_out, 16)
        sp.sem_inc(s_table, 1)

        def context_load(t, b):
            rows = rows_of(t)
            sp.wait_ge(s_cT, t + 1)
            sp.dma_start(xin[0:rows, b, :], xn16_table[bass.ds(t * P, rows), :]).then_inc(s_cl[b], 16)

        def xn_load(t):
            rows = rows_of(t)
            sp.wait_ge(s_nT, t + 1)
            sp.dma_start(xn_in[0:rows, :], xn_table[bass.ds(t * P, rows), :]).then_inc(s_nl, 16)

        def x_load(t):
            rows = rows_of(t)
            sp.wait_ge(s_x2free, t + 1)
            sp.dma_start(x_in[0:rows, :], x[bass.ds(t * P, rows), :]).then_inc(s_nlx, 16)

        def node_store(t):
            rows = rows_of(t)
            sp.wait_ge(s_x2, t + 1)
            sp.dma_start(out[bass.ds(t * P, rows), :], x2[0:rows, :]).then_inc(s_out, 16)

        with sp.Fori(0, CTX_IT) as i:
            for c in range(CTX):
                context_load(i * CTX + c, c % XB)
        context_load(FULL, 0)
        xn_load(0)
        x_load(0)
        with sp.Fori(0, FULL - 1) as t:
            xn_load(t + 1)
            x_load(t + 1)
            node_store(t)
        xn_load(FULL)
        x_load(FULL)
        node_store(FULL - 1)
        node_store(FULL)
        sp.wait_ge(s_out, 16 * NT + 16)
        sp.wait_ge(s_w0, 32)

    @block.gpsimd
    def _(pool):
        def diagonal(buf, op, fill, pattern, mult, base_=0):
            return pool.affine_select(out=buf, in_=buf, compare_op=op, fill=fill, base=base_, pattern=pattern,
                                      channel_multiplier=mult)

        pool.memset(ident[:, :], 0.0).then_inc(s_gp, 1)
        pool.memset(tri[:, :], 1.0).then_inc(s_gp, 1)
        pool.iota(iota[:, :], pattern=[[1, P]], base=0, channel_multiplier=0,
                  allow_small_or_imprecise_dtypes=True).then_inc(s_gp, 1)
        pool.iota(pid[:, :], pattern=[[0, 1]], base=0, channel_multiplier=1,
                  allow_small_or_imprecise_dtypes=True).then_inc(s_gp, 1)
        pool.iota(iota8[:, :], pattern=[[1, NEXP]], base=0, channel_multiplier=0,
                  allow_small_or_imprecise_dtypes=True).then_inc(s_gp, 1)
        pool.iota(base[:, :], pattern=[[CAP, NEXP]], base=0, channel_multiplier=0,
                  allow_small_or_imprecise_dtypes=True).then_inc(s_gp, 1)
        pool.iota(floor_[:, :], pattern=[[P, EB]], base=0, channel_multiplier=1,
                  allow_small_or_imprecise_dtypes=True).then_inc(s_gp, 1)
        pool.iota(padrow[:, :, D], pattern=[[P, 2]], base=N, channel_multiplier=1,
                  allow_small_or_imprecise_dtypes=True).then_inc(s_gp, 1)
        pool.memset(first4[:, :], 1.0).then_inc(s_gp, 1)
        pool.iota(tokens[:, :], pattern=[[P, NT]], base=0, channel_multiplier=1,
                  allow_small_or_imprecise_dtypes=True).then_inc(s_gp, 1)
        pool.wait_ge(s_gp, 10)
        diagonal(ident[:, :], ALU.not_equal, 1.0, [[-1, P]], 1).then_inc(s_gp, 1)
        diagonal(tri[:, :], ALU.is_gt, 0.0, [[1, P]], -1).then_inc(s_gp, 1)
        view = first4[:, :].rearrange("p (g r) -> p g r", r=GROUP)
        diagonal(view, ALU.is_equal, 0.0, [[-GROUP, P // GROUP], [0, GROUP]], 1).then_inc(s_gp, 1)
        pool.wait_ge(s_const, 13)
        for k in range(2):
            pool.dma_start(slots[NEXP * CAP + k * P:NEXP * CAP + (k + 1) * P, :], padrow[:, k, :]).then_inc(s_sc[k], 16)

        def low(g, h, tiles=4):
            pool.wait_ge(s_hi, g + 1)
            pool.sem_inc(s_hold, 1)
            pool.tensor_tensor(x16[h][:, 0:tiles, D:2 * D], xs[h][:, 0:tiles, :], x16[h][:, 0:tiles, 0:D], ALU.subtract).then_inc(s_lo, 1)

        with pool.Fori(0, 4) as g:
            for h in range(3):
                low(3 * g + h, h)
        low(12, 0, 1)

        pool.wait_ge(s_flag, 1)
        pool.wait_ge(s_table, 1)
        bad = pool.value_load(flag[0:1, 0:1], min_val=0, max_val=1)
        with pool.If(bad):
            pool.iota(giota, pattern=[[1, GW]], base=0, channel_multiplier=0,
                      allow_small_or_imprecise_dtypes=True).then_inc(s_giota, 1)
            with pool.Fori(0, ET) as t:
                pool.wait_ge(s_gi, t + 1)
                pool.sem_inc(s_hold, 1)
                pool.indirect_dma_start(out=t1[:, :], out_offset=None, in_=xn_table[:, :],
                                        in_offset=bass.IndirectOffsetOnAxis(ap=gidx[:, 0:1], axis=0)).then_inc(s_gg, 16)

        def gathers(i, h):
            pool.wait_ge(s_idx, 2 * i + h + 1)
            pool.sem_inc(s_hold, 1)
            for k in range(HALF):
                pool.indirect_dma_start(out=got[h][:, k, :], out_offset=None, in_=xn16_table[:, :],
                                        in_offset=bass.IndirectOffsetOnAxis(ap=idx[h][:, k:k + 1], axis=0)
                                        ).then_inc(s_got[h][k], 16)

        def scatters(t):
            rows = rows_of(t)
            pool.wait_ge(s_slot, t + 2)
            pool.sem_inc(s_hold, 1)
            for k in range(2):
                pool.indirect_dma_start(out=slots[:, :], out_offset=bass.IndirectOffsetOnAxis(ap=slot[0:rows, k:k + 1], axis=0),
                                        in_=row[0:rows, :], in_offset=None).then_inc(s_sc[k], 16)

        with pool.Fori(0, CTX_IT + 3) as i:
            gathers(i, 0)
            gathers(i, 1)
        with pool.Fori(CTX_IT + 3, EIT) as i:
            gathers(i, 0)
            scatters(i - (CTX_IT + 3))
            gathers(i, 1)
        with pool.Fori(EIT - CTX_IT - 3, FULL) as t:
            scatters(t)
        scatters(FULL)
        for k in range(2):
            pool.wait_ge(s_sc[k], 16 * NT + 16)

    @block.scalar
    def _(act):
        act.wait_ge(s_raw0, 2)
        act.dma_start(s_raw[:, 0:EB - 1, :], src[0:(EB - 1) * P * P].rearrange("(b p e) -> p b e", p=P, e=P)).then_inc(s_e, 16)
        LB = ET - (EB - 1) * P
        act.dma_start(s_raw[0:LB, EB - 1, :], src[(EB - 1) * P * P:ET * P].rearrange("(p e) -> p e", e=P)).then_inc(s_e, 16)
        act.wait_ge(s_raw0, 3)
        act.dma_start(w_blk[:, 0:EB - 1, :], edge_weight[0:(EB - 1) * P * P].rearrange("(b p e) -> p b e", p=P, e=P)).then_inc(s_e, 16)
        act.dma_start(w_blk[0:LB, EB - 1, :], edge_weight[(EB - 1) * P * P:ET * P].rearrange("(p e) -> p e", e=P)).then_inc(s_e, 16)
        act.dma_start(dst0[0:1, :], dst[0:ET * P].rearrange("(t e) -> e t", e=GROUP * P)[0:1, :],
                      allow_slow_non_contiguous=True).then_inc(s_e, 16)

        def two(ap):
            return ap.rearrange("(c p) n -> p c n", p=P)

        act.dma_start(wqkv[:, :, :], two(Wqkv)).then_inc(s_w, 16)
        act.dma_start(wraw[:, 0, :, :], two(gnn_W1)).then_inc(s_w, 16)
        act.dma_start(wraw[:, 1, :, :], two(gnn_W2)).then_inc(s_w, 16)
        act.dma_start(wout[:, :, :], two(Wout)).then_inc(s_w, 16)
        act.dma_start(wr[:, :, :], two(Wr)).then_inc(s_w, 16)
        act.dma_start(brow[:, 0, :], gnn_b1.partition_broadcast(P)).then_inc(s_w, 16)
        act.dma_start(brow[:, 1, :], gnn_b2.partition_broadcast(P)).then_inc(s_w, 16)
        act.dma_start(br_row[0:1, :], br.rearrange("(a n) -> a n", a=1)).then_inc(s_w, 16)
        act.dma_start(gam[:, :], gamma.partition_broadcast(P)).then_inc(s_w, 16)
        for b in range(EB):
            n = P if b < EB - 1 else LB
            act.wait_ge(s_blkT, b + 1)
            act.activation(srcT[:, b * P:b * P + n], banks[4][:, 0:n], ACT.Copy)
            act.activation(dstT[:, b * P:b * P + n], banks[5][:, 0:n], ACT.Copy).then_inc(s_blka, 1)
        act.wait_ge(s_var, 1)
        act.activation(rstd[:, :], tmp49[:, :], ACT.Sqrt).then_inc(s_std, 1)

        act.wait_ge(s_w, 16 * 9)
        act.activation(wkvh[:, :, :], wqkv[:, :, D:3 * D], ACT.Copy, scale=WSCALE).then_inc(s_wk, 1)
        for m, (wt, scale) in enumerate(((w1T, 1.0), (w2T, 1.0 / WSCALE))):
            act.wait_ge(s_wt, m + 1)
            act.activation(wt[:, :, :].rearrange("p c n -> p (c n)"), banks[4 + m][:, :], ACT.Copy, scale=scale).then_inc(s_wtc, 1)

        def high(g, h, tiles=4):
            act.wait_ge(s_xs, g + 1)
            act.wait_ge(s_xsTp, g + 1)
            act.activation(x16[h][:, 0:tiles, 0:D], xs[h][:, 0:tiles, :], ACT.Copy).then_inc(s_hi, 1)

        def group_copy(g, h, cols=4 * P):
            act.wait_ge(s_xsTp, g + 4)
            act.wait_ge(s_kT, g + 1)
            for c in range(KC):
                last = act.activation(xsT[:, h, c, 0:cols], banks[c][:, 0:cols], ACT.Copy)
            last.then_inc(s_xsT, 1)

        high(0, 0)
        high(1, 1)
        group_copy(0, 0)
        high(2, 2)
        group_copy(1, 1)
        with act.Fori(1, 4) as g:
            for h in range(3):
                high(3 * g + h, h)
                group_copy(3 * g + h - 1, (h + 2) % 3)
        high(12, 0, 1)
        group_copy(11, 2)
        group_copy(12, 0, P)

        def context_copy(t, h):
            rows = rows_of(t)
            act.wait_ge(s_cT, t + XB + 1)
            act.wait_ge(s_ckv, t + 1)
            act.activation(xT[:, h, :, :, 0:rows].rearrange("p a c n -> p (a c) n"),
                           psTc[h][:, :].rearrange("p (c n) -> p c n", c=2 * KC)[:, :, 0:rows],
                           ACT.Copy).then_inc(s_cx, 1)

        def context_exp(t, h):
            rows = rows_of(t)
            act.wait_ge(s_cks, t + 1)
            act.activation(ek[0:rows, h, :], ek[0:rows, h, :], ACT.Exp).then_inc(s_cek, 1)

        context_copy(0, 0)
        context_copy(1, 1)
        context_exp(0, 0)
        with act.Fori(0, CTX_IT - 1) as i:
            for c in range(CTX):
                context_copy(i * CTX + c + 2, c % 2)
                context_exp(i * CTX + c + 1, (c + 1) % 2)
        for t in range(FULL - CTX, FULL):
            if t + 2 <= FULL:
                context_copy(t + 2, t % 2)
            context_exp(t + 1, (t + 1) % 2)

        def node(n, m):
            rows = rows_of(n)
            r = slice(0, rows)
            act.wait_ge(s_nT, n + 2)
            act.activation(nT[:, :, 0:rows], psT[:, 0:256].rearrange("p (c n) -> p c n", c=KC)[:, :, 0:rows],
                           ACT.Copy).then_inc(s_nTc, 1)
            if m is not None:
                gate_exp(m)
            act.wait_ge(s_qs, n + 1)
            act.activation(eq[r, :], qs[r, :], ACT.Exp).then_inc(s_eq, 1)
            act.wait_ge(s_g, n + 1)
            act.activation(gr[r, :], banks[4][r, 0:D], ACT.Copy).then_inc(s_gr, 1)
            act.wait_ge(s_qT, n + 1)
            act.activation(qT[:, :, 0:rows], psT[:, 256:512].rearrange("p (c n) -> p c n", c=KC)[:, :, 0:rows],
                           ACT.Copy).then_inc(s_qTc, 1)
            act.wait_ge(s_lk, n + 1)
            act.activation(sq[r, :], gl[r, :], ACT.Square, accum_out=ss[r, 0:1]).then_inc(s_gl, 1)
            act.wait_ge(s_gl, n + 1)
            act.activation(sd[r, 0:1], ss[r, 0:1], ACT.Sqrt).then_inc(s_sd, 1)
            for k in range(3):
                act.wait_ge(s_v, 3 * n + k + 1)
                act.activation(sd[r, k + 1:k + 2], mv[r, k, 1:2], ACT.Sqrt, bias=eps[r, 0:1]).then_inc(s_sd, 1)
                if k == 1:
                    act.wait_ge(s_x2T, n + 1)
                    act.activation(x2T[:, :, 0:rows], banks[7][:, 0:256].rearrange("p (c n) -> p c n", c=KC)[:, :, 0:rows],
                                   ACT.Copy).then_inc(s_x2Tc, 1)

        def gate_exp(m):
            rows = rows_of(m)
            act.wait_ge(s_d, m + 1)
            act.activation(gt[0:rows, 1:2], gt[0:rows, 0:1], ACT.Exp).then_inc(s_ed, 1)

        node(0, None)
        with act.Fori(1, FULL) as t:
            node(t, t - 1)
        node(FULL, FULL - 1)
        gate_exp(FULL)

    @block.vector
    def _(dve):
        one = Chain(dve, s_dve)
        dve.memset(e_raw[:, EB - 1, :], 0).then_inc(s_raw0, 1)
        dve.memset(s_raw[:, EB - 1, :], 0).then_inc(s_raw0, 1)
        dve.memset(w_blk[:, EB - 1, :], 0.0).then_inc(s_raw0, 1)
        dve.memset(xall[:, FULL, :], 0.0).then_inc(s_const, 1)
        dve.memset(ones[:, :], 1.0).then_inc(s_const, 1)
        dve.memset(zeros[:, :], 0.0).then_inc(s_const, 1)
        dve.memset(eps[:, :], 1e-5).then_inc(s_const, 1)
        dve.memset(padrow[:, :, 0:D], 0.0).then_inc(s_const, 1)
        dve.memset(padrow[:, :, D + 1:ROW], 0.0).then_inc(s_const, 1)
        dve.memset(bd[:, :, :], 0.0).then_inc(s_const, 1)
        dve.memset(srcT[:, ET:ET + PER_IT], 0.0).then_inc(s_const, 1)
        dve.memset(dstT[:, ET:ET + PER_IT], 0.0).then_inc(s_const, 1)
        dve.memset(wT[:, :, ET:ET + PER_IT], 0.0).then_inc(s_const, 1)
        dve.memset(ones16[:, :], 1.0).then_inc(s_const, 1)
        dve.memset(bias3[:, :], 0.0).then_inc(s_const, 1)
        dve.memset(v[:, :, :, P:P + 1], 1.0).then_inc(s_const, 1)
        LB = ET - (EB - 1) * P
        dve.wait_ge(s_e, 16 * 7)
        dve.wait_ge(s_gp, 13)
        dve.tensor_copy(dabs[:, :, :], e_raw[:, :, :]).then_inc(s_dabs, 1)
        dve.tensor_copy(ident16[:, :], ident[:, :]).then_inc(s_wk, 1)
        one.did(dve.tensor_copy(iota16[:, :], iota[:, 0:W]))
        one.did(dve.tensor_copy(s_blk[:, :, :], s_raw[:, :, :]))
        one.did(dve.tensor_scalar(floor_[:, :], floor_[:, :], float(P // PER_IT), -float(P * LAG), op0=ALU.mult, op1=ALU.add))
        dve.wait_ge(s_gb, 1)
        one(dve.tensor_copy(gbase[:, :], banks[6][:, 0:EB]))
        one(dve.tensor_tensor(e_blk[:, :, :], dabs[:, :, :], gbase[:, :].unsqueeze(2).to_broadcast([P, EB, P]), ALU.subtract))
        one.did(dve.reduce_max(ends[:, 0, :], e_blk[:, :, :], axis=X))
        one(dve.tensor_reduce(ends[:, 1, :], e_blk[:, :, :], axis=X, op=ALU.min))
        one.did(dve.tensor_tensor(ends[:, 2, :], ends[:, 1, :], gbase[:, :], ALU.add))
        one.did(dve.tensor_scalar(ends[:, 0, :], ends[:, 0, :], float(W), None, op0=ALU.is_ge))
        one(dve.tensor_scalar(ends[:, 1, :], ends[:, 1, :], 0.0, None, op0=ALU.is_lt))
        one(dve.tensor_tensor(ends[:, 2, :], ends[:, 2, :], floor_[:, :], ALU.is_lt))
        one.did(dve.reduce_max(ends[:, 3, :], w_blk[:, :, :], axis=X))
        one(dve.tensor_reduce(ends[:, 4, :], w_blk[:, :, :], axis=X, op=ALU.min))
        one.did(dve.tensor_scalar(ends[:, 3, :], ends[:, 3, :], 512.0, None, op0=ALU.is_ge))
        one(dve.tensor_scalar(ends[:, 4, :], ends[:, 4, :], -512.0, None, op0=ALU.is_le))
        one(dve.memset(ends[LB:P, :, EB - 1:EB], 0.0))
        dve.reduce_max(badc[:, :], ends[:, :, :].rearrange("p k b -> p (k b)"), axis=X).then_inc(s_bad, 1)
        def x_stats(g):
            dve.wait_ge(s_x[g], 16)
            for t in range(8 * g, min(8 * g + 8, NT)):
                dve.bn_stats(st6[:, t, :], xall[:, t, :]).then_inc(s_st, 1)

        for b in range(max(EB, len(s_x))):
            if b < EB:
                n = P if b < EB - 1 else LB
                dve.wait_ge(s_blkT, b + 1)
                dve.tensor_copy(dabT[:, b * P:b * P + n], banks[6][:, 0:n])
                dve.tensor_scalar(wallT[:, b * P:b * P + n], banks[7][:, 0:n], WSCALE, None, op0=ALU.mult).then_inc(s_blkc, 1)
            if b < len(s_x):
                x_stats(b)
        dve.wait_ge(s_badb, 1)
        one(dve.reduce_max(good[:, :], banks[6][:, 0:P], axis=X))
        one(dve.tensor_copy(flag[:, :], good[:, :]))
        one(dve.tensor_scalar(good[:, :], good[:, :], -1.0, 1.0, op0=ALU.mult, op1=ALU.add))
        one(dve.tensor_scalar(wgood[:, :], wallT[:, 0:ET], 32768.0, -32768.0, op0=ALU.min, op1=ALU.max))
        one(dve.tensor_scalar(wgood[:, :], wgood[:, :], good[:, 0:1], None, op0=ALU.mult))
        one(dve.tensor_copy(wT[:, 0, 0:ET], wgood[:, :]))
        one(dve.tensor_tensor(wT[:, 1, 0:ET], wgood[:, :], wT[:, 0, 0:ET], ALU.subtract))
        dve.wait_ge(s_st, NT)
        one(dve.tensor_tensor(mean[:, :], st6[:, :, 1], st6[:, :, 4], ALU.add))
        one(dve.tensor_scalar(mean[:, :], mean[:, :], 0.5, None, op0=ALU.mult))
        one(dve.tensor_tensor(tmp49[:, :], st6[:, :, 1], st6[:, :, 4], ALU.subtract))
        one(dve.tensor_tensor(tmp49[:, :], tmp49[:, :], tmp49[:, :], ALU.mult))
        one(dve.tensor_scalar(tmp49[:, :], tmp49[:, :], 0.25, 1e-5, op0=ALU.mult, op1=ALU.add))
        one(dve.tensor_tensor(rstd[:, :], st6[:, :, 2], st6[:, :, 5], ALU.add))
        dve.scalar_tensor_tensor(out=tmp49[:, :], in0=rstd[:, :], scalar=1.0 / D, in1=tmp49[:, :],
                                 op0=ALU.mult, op1=ALU.add).then_inc(s_var, 1)
        dve.wait_ge(s_std, 1)
        one(dve.reciprocal(rstd[:, :], rstd[:, :]))

        def normalise(t, h, k):
            return dve.tensor_scalar(xs[h][:, k, :], xall[:, bass.ds(t, 1), :].rearrange("p a d -> p (a d)"),
                                     mean[:, bass.ds(t, 1)], rstd[:, bass.ds(t, 1)], op0=ALU.subtract, op1=ALU.mult)

        def key_max(g, h, cols):
            dve.wait_ge(s_kT, g + 4)
            for c in range(KC):
                last = dve.reduce_max(kmaxg[:, c, bass.ds(g, 1)], banks[2 + 2 * h + c][:, 0:cols], axis=X)
            last.then_inc(s_km, 1)

        def normalise_group(g, h, k=None):
            if k is not None:
                dve.wait_ge(s_tab[h], 32 * k)
            for j in range(4):
                last = normalise(4 * g + j, h, j)
            last.then_inc(s_xs, 1)

        normalise_group(0, 0)
        normalise_group(1, 1)
        normalise_group(2, 2)
        dve.wait_ge(s_w, 16 * 9)
        one(dve.tensor_tensor(gr[:, :], brow[:, 0, :], brow[:, 1, :], ALU.add))
        one(dve.tensor_copy(bhi[:, :], gr[:, :]))
        one(dve.tensor_tensor(gr[:, :], gr[:, :], bhi[:, :], ALU.subtract))
        one(dve.tensor_copy(bmid[:, :], gr[:, :]))
        one(dve.tensor_tensor(gr[:, :], gr[:, :], bmid[:, :], ALU.subtract))
        dve.tensor_copy(bias3[0:1, :], bhi[0:1, :])
        dve.tensor_copy(bias3[32:33, :], bmid[32:33, :])
        dve.tensor_copy(bias3[64:65, :], gr[64:65, :]).then_inc(s_bias, 1)
        dve.wait_ge(s_wk, 2)
        one(dve.scalar_tensor_tensor(out=wkvl[:, :, :], in0=wqkv[:, :, D:3 * D], scalar=WSCALE, in1=wkvh[:, :, :],
                                     op0=ALU.mult, op1=ALU.subtract))
        with dve.Fori(1, 4) as g:
            for h in range(3):
                normalise_group(3 * g + h, h, g)
                key_max(3 * g + h - 3, h, 4 * P)
        dve.wait_ge(s_tab[0], 32 * 4)
        normalise(FULL, 0, 0).then_inc(s_xs, 1)
        for h in range(3):
            key_max(9 + h, h, 4 * P)
        key_max(12, 0, LAST)
        dve.wait_ge(s_km, 16)
        dve.memset(acc_flat[:, :], 0.0).then_inc(s_dve, 1)
        one.n += 1
        one(dve.reduce_max(kmax[:, :], kmaxg[:, :, :], axis=X))
        dve.sem_inc(s_nk, 1)
        dve.wait_ge(s_nkc, 1)
        one(dve.tensor_scalar(kmaxb[:, :], banks[6][:, 0:D], 1.0 / WSCALE, None, op0=ALU.mult))
        dve.sem_inc(s_flag, 1)

        bad = dve.value_load(flag[0:1, 0:1], min_val=0, max_val=1)
        with dve.If(bad):
            dve.wait_ge(s_giota, 1)
            with dve.Fori(0, ET) as t:
                dve.tensor_scalar(gidx[:, :], srcT[:, bass.ds(t, 1)], 0.0, None, op0=ALU.add).then_inc(s_gi, 1)
                dve.tensor_scalar(gdw[:, 0:1], dabT[:, bass.ds(t, 1)], 0.0, None, op0=ALU.add)
                dve.tensor_scalar(gdw[:, 1:2], wallT[:, bass.ds(t, 1)], 0.0, None, op0=ALU.add)
                dve.memset(node0[:, :], 0.0).then_inc(s_gz, 1)
                dve.wait_ge(s_gz, t + 1)
                dve.sem_inc(s_hold, 1)
                with dve.Fori(0, GN) as n:
                    done = t * GN + n
                    dve.tensor_scalar(ghot, giota, node0[:, 0:1], gdw[:, 0:1], op0=ALU.add, op1=ALU.is_equal).then_inc(s_gh, 1)
                    dve.wait_ge(s_gh, done + 1)
                    dve.tensor_scalar(ghot, ghot, gdw[:, 1:2], None, op0=ALU.mult).then_inc(s_gw, 1)
                    dve.tensor_scalar(node0[:, :], node0[:, :], float(GW), None, op0=ALU.add)
                    dve.wait_ge(s_gm, done + 1)
                    for c in range(KC):
                        window = acc[:, c, bass.ds(n * GW, GW)]
                        dve.tensor_tensor(window, window, banks[6 + c][:, 0:GW], ALU.add).then_inc(s_ga, 1)
                    dve.wait_ge(s_ga, KC * (done + 1))

        dve.sem_inc(s_gend, 1)

        GPH = HALF // GROUP
        d0 = [dve.alloc_register(f"first_dst{g}") for g in range(2 * GPH)]

        def stage(i, h):
            dve.tensor_scalar(idx[h][:, :], srcT[:, bass.ds(i * PER_IT + h * HALF, HALF)], 0.0, None, op0=ALU.add).then_inc(s_idx, 1)

        def hots(i, h, steps=range(3)):
            t = bass.ds(i * PER_IT + h * HALF, HALF)
            shape = [P, HALF, W]
            for k in steps:
                if k == 0:
                    dve.wait_ge(s_hot, 2 * i + h + 1)
                    dve.tensor_tensor(mask[h][:, :, :], iota16[:, :].unsqueeze(1).to_broadcast(shape),
                                      dstT[:, t].unsqueeze(2).to_broadcast(shape), ALU.is_equal).then_inc(s_mask, 1)
                else:
                    if k == 1:
                        dve.wait_ge(s_mask, 2 * i + h + 1)
                    ins = dve.tensor_tensor(hot[h][:, k - 1, :, :], mask[h][:, :, :],
                                            wT[:, k - 1, t].unsqueeze(2).to_broadcast(shape), ALU.mult)
            if k == 2:
                ins.then_inc(s_hot, 1)

        def adds(i, h):
            dve.wait_ge(s_mult, 2 * i + h + 1)
            stage(i + 1, h)
            if h == 0:
                dve.load(d0, dst0[0:1, bass.ds(i * 2 * GPH, 2 * GPH)])
            for g in range(GPH):
                dve.wait_ge(s_acc, 2 * GPH + (2 * i + h) * GPH + g)
                first = dve.snap(d0[h * GPH + g], min_val=0, max_val=N - 1)
                view = acc[:, :, bass.ds(first, W)]
                dve.tensor_tensor(view, view, psE[h][:, g * KC * W:(g + 1) * KC * W].rearrange("p (c w) -> p c w", c=KC),
                                  ALU.add).then_inc(s_acc, 1)

        dve.wait_ge(s_blka, EB)
        for h in range(2):
            stage(0, h)
        hots(0, 0)

        def keys_values(t, h):
            r = slice(0, rows_of(t))
            dve.wait_ge(s_ckv, t + 3)
            dve.wait_ge(s_cc, t + 1)
            dve.scalar_tensor_tensor(out=ek[r, h, :], in0=psKV[h][r, 0:D], scalar=1.0 / WSCALE, in1=kmaxb[r, :],
                                     op0=ALU.mult, op1=ALU.subtract).then_inc(s_cks, 1)
            dve.tensor_scalar(v[r, h, :, 0:P], psKV[h][r, D:2 * D].rearrange("p (c e) -> p c e", c=KC), 1.0 / WSCALE, None,
                              op0=ALU.mult).then_inc(s_ckd, 1)

        def context_iteration(i):
            hots(i, 1)
            for c in range(CTX):
                if c % (CTX // 2) == CTX // 2 - 1:
                    adds(i, c // (CTX // 2))
                if c == CTX // 2 - 1:
                    hots(i + 1, 0)
                keys_values(i * CTX + c + 1, (c + 1) % 2)

        keys_values(0, 0)
        with dve.Fori(0, CTX_IT - 1) as i:
            context_iteration(i)
        context_iteration(CTX_IT - 1)

        FRONT, BACK, ROUTER = 3, 8, 19

        def fill(i, h, ks):
            if i is not None:
                hots(i, h, ks)

        def node_front(n, i):
            rows = rows_of(n)
            r = slice(0, rows)
            ch = Chain(dve, s_front, n * FRONT)
            dve.wait_ge(s_nTc, n + 1)
            dve.wait_ge(s_acc, 2 * GPH + 2 * GPH * (EIT if i is None else i))
            dve.scalar_tensor_tensor(out=sT[:, :, 0:rows], in0=nT[:, :, 0:rows], scalar=1.0,
                                     in1=acc[:, :, bass.ds(n * P, rows)], op0=ALU.add, op1=ALU.mult).then_inc(s_sT, 1)
            dve.wait_ge(s_q, n + 1)
            q8 = banks[3][r, 0:D].rearrange("p (h e) -> p h e", h=HEADS)
            qs8, eq8, qn8 = (b[r, :].rearrange("p (h e) -> p h e", h=HEADS) for b in (qs, eq, qn))
            ch.did(dve.reduce_max(hd[r, 0, :], q8, axis=X))
            ch.settle()
            dve.tensor_tensor(qs8, q8, hd[r, 0, :].unsqueeze(2).to_broadcast([rows, HEADS, DH]), ALU.subtract).then_inc(s_qs, 1)
            fill(i, 1, (2,))
            dve.wait_ge(s_eq, n + 1)
            ch(dve.reduce_sum(hd[r, 1, :], eq8, axis=X))
            ch(dve.reciprocal(hd[r, 2, :], hd[r, 1, :]))
            dve.tensor_tensor(qn8, eq8, hd[r, 2, :].unsqueeze(2).to_broadcast([rows, HEADS, DH]), ALU.mult).then_inc(s_qn, 1)
            dve.wait_ge(s_gr, n + 2)
            dve.scalar_tensor_tensor(out=gl[r, :], in0=gr[r, :], scalar=0.2, in1=gr[r, :], op0=ALU.mult, op1=ALU.max).then_inc(s_lk, 1)
            assert ch.n == FRONT, ch.n

        def node_back(n, i):
            r = slice(0, rows_of(n))
            ch = Chain(dve, s_back, n * BACK)
            fill(i, 0, (0,))
            dve.wait_ge(s_mix, n + 1)
            ch(dve.bn_stats(bn[r, 0, :], banks[6][r, 0:D]))
            dve.sem_inc(s_hold, 1)
            dve.bn_aggr(mv[r, 0, :], bn[r, 0, :]).then_inc(s_v, 1)
            fill(i, 0, (1,))
            dve.wait_ge(s_sd, 4 * n + 1)
            ch(dve.tensor_scalar(sd[r, 0:1], sd[r, 0:1], 1e-12, None, op0=ALU.max))
            ch.did(dve.reciprocal(rs[r, 0:1], sd[r, 0:1]))
            dve.wait_ge(s_v, 3 * n + 1)
            ch.did(dve.scalar_tensor_tensor(out=t2[r, :], in0=banks[6][r, 0:D], scalar=mv[r, 0, 0:1], in1=gam[r, :],
                                            op0=ALU.subtract, op1=ALU.mult))
            ch.settle()
            dve.wait_ge(s_nlx, 16 * n + 16)
            dve.scalar_tensor_tensor(out=t1[r, :], in0=gl[r, :], scalar=rs[r, 0:1], in1=x_in[r, :],
                                     op0=ALU.mult, op1=ALU.add).then_inc(s_x2free, 1)
            dve.wait_ge(s_sd, 4 * n + 2)
            ch.did(dve.reciprocal(rs[r, 1:2], sd[r, 1:2]))
            fill(i, 0, (2,))
            ch.settle()
            dve.wait_ge(s_x2free, n + 2)
            dve.wait_ge(s_out, 16 * n + 16)
            dve.scalar_tensor_tensor(out=x2[r, :], in0=t2[r, :], scalar=rs[r, 1:2], in1=t1[r, :],
                                     op0=ALU.mult, op1=ALU.add).then_inc(s_x2, 1)
            dve.wait_ge(s_x2, n + 1)
            ch.did(dve.bn_stats(bn[r, 1, :], x2[r, :]))
            ch.settle()
            dve.sem_inc(s_hold, 1)
            dve.bn_aggr(mv[r, 1, :], bn[r, 1, :]).then_inc(s_v, 1)
            dve.wait_ge(s_sd, 4 * n + 3)
            ch.did(dve.reciprocal(rs[r, 2:3], sd[r, 2:3]))
            ch.settle()
            dve.tensor_scalar(x2n[r, :], x2[r, :], mv[r, 1, 0:1], rs[r, 2:3], op0=ALU.subtract, op1=ALU.mult).then_inc(s_x2n, 1)
            dve.wait_ge(s_x2n, n + 1)
            ch.did(dve.bn_stats(bn[r, 2, :], x2n[r, :]))
            ch.settle()
            dve.sem_inc(s_hold, 1)
            dve.bn_aggr(mv[r, 2, :], bn[r, 2, :]).then_inc(s_v, 1)
            assert ch.n == BACK, ch.n

        def router_top(m, i):
            r = slice(0, rows_of(m))
            ch = Chain(dve, s_router, m * ROUTER)
            dve.wait_ge(s_lg, m + 1)
            ch.did(dve.tensor_copy(lg[r, :], banks[7][r, 256:256 + NEXP]))
            dve.wait_ge(s_sd, 4 * m + 4)
            ch.did(dve.reciprocal(rs[r, 3:4], sd[r, 3:4]))
            ch.settle()
            dve.sem_inc(s_hold, 1)
            ch.did(dve.max(top[r, :], lg[r, :]))
            fill(i, 1, (0,))
            ch.settle()
            dve.tensor_tensor(gt[r, 0:1], top[r, 1:2], top[r, 0:1], ALU.subtract).then_inc(s_d, 1)
            ch.did(dve.max_index(topi[r, :], top[r, :], lg[r, :]))
            ch.settle()
            ch(dve.tensor_copy(topf[r, :], topi[r, 0:2]))
            ch.did(dve.tensor_scalar(oh[r, 0, :], iota8[r, :], topf[r, 0:1], None, op0=ALU.is_equal))
            ch.did(dve.tensor_scalar(oh[r, 1, :], iota8[r, :], topf[r, 1:2], None, op0=ALU.is_equal))
            fill(i, 1, (1,))
            ch.settle()
            dve.tensor_tensor(oh[r, 2, :], oh[r, 0, :], oh[r, 1, :], ALU.add).then_inc(s_both, 1)
            return ch

        def router_slots(m, ch):
            rows = rows_of(m)
            r = slice(0, rows)
            for k in range(2):
                dve.wait_ge(s_sc[k], 16 * m + 16)
            ch.did(dve.tensor_scalar(row[r, 0:D], x2n[r, :], mv[r, 2, 0:1], rs[r, 3:4], op0=ALU.subtract, op1=ALU.mult))
            dve.wait_ge(s_ed, m + 1)
            ch.did(dve.tensor_scalar(gt[r, 2:3], gt[r, 1:2], 1.0, None, op0=ALU.add))
            dve.wait_ge(s_rank, m + 1)
            ch.did(dve.tensor_tensor(rk[r, :], banks[7][r, 264:264 + NEXP], base[r, :], ALU.add))
            ch.settle()
            ch.did(dve.reciprocal(gt[r, 3:4], gt[r, 2:3]))
            ch.did(dve.tensor_tensor(base[:, :], base[:, :], banks[7][:, 272:272 + NEXP], ALU.add))
            ch.did(dve.tensor_tensor(prod[r, :, :], oh[r, 0:2, :], rk[r, :].unsqueeze(1).to_broadcast([rows, 2, NEXP]), ALU.mult))
            ch.settle()
            ch.did(dve.tensor_tensor(row[r, D + 2:D + 3], gt[r, 1:2], gt[r, 3:4], ALU.mult))
            ch.did(dve.reduce_sum(slotf[r, :], prod[r, :, :], axis=X))
            ch.did(dve.tensor_copy(row[r, D + 1:D + 2], topf[r, 0:1]))
            ch.settle()
            ch.did(dve.tensor_tensor(row[r, D + 3:D + 4], gt[r, 3:4], row[r, D + 2:D + 3], ALU.subtract))
            ch.did(dve.tensor_scalar(row[r, D:D + 1], tokens[r, bass.ds(m, 1)], 0.0, None, op0=ALU.add))
            dve.tensor_copy(slot[r, :], slotf[r, :]).then_inc(s_router, 1)
            ch.n += 1
            ch.settle()
            dve.sem_inc(s_slot, 1)
            assert ch.n == ROUTER, ch.n

        def node(i, n, m):
            if i is not None:
                adds(i, 0)
            if m is not None:
                ch = router_top(m, i)
            else:
                fill(i, 1, (0, 1))
            node_front(n, i)
            if m is not None:
                router_slots(m, ch)
            if i is not None:
                adds(i, 1)
            node_back(n, None if i is None else i + 1)

        hots(CTX_IT, 1)
        adds(CTX_IT, 0)
        hots(CTX_IT + 1, 0)
        dve.wait_ge(s_cc, NT + 2)
        context = psC[:, 0:KC * (P + 1)].rearrange("p (c e) -> p c e", c=KC)
        one(dve.reciprocal(ksum[:, :], context[:, :, P]))
        one(dve.tensor_scalar(ksum[:, :], ksum[:, :], float(DH) ** -0.5, None, op0=ALU.mult))
        for c in range(KC):
            for b in range(P // DH):
                b_ = slice(b * DH, (b + 1) * DH)
                last = dve.tensor_copy(bd[b_, c, b_], context[b_, c, b_])
        last.then_inc(s_bd, 1)
        dve.wait_ge(s_bd, 2)
        dve.tensor_copy(bdT[:, :, :].rearrange("p c n -> p (c n)"), banks[7][:, 0:KC * P]).then_inc(s_bd, 1)
        dve.wait_ge(s_mp, 1)
        for c in range(KC):
            last = dve.tensor_scalar(M[:, c, :], banks[6][:, c * D:(c + 1) * D], ksum[:, c:c + 1], None, op0=ALU.mult)
        last.then_inc(s_M, 1)
        adds(CTX_IT, 1)
        node(CTX_IT + 1, 0, None)
        with dve.Fori(CTX_IT + 2, EIT) as i:
            node(i, i - (CTX_IT + 1), i - (CTX_IT + 2))
        with dve.Fori(EIT - CTX_IT - 1, FULL) as t:
            node(None, t, t - 1)
        node(None, FULL, FULL - 1)
        router_slots(FULL, router_top(FULL, None))

    @block.tensor
    def _(pe):
        def mm(o, lhsT, rhs, start, stop, **kw):
            return pe.matmul(o, lhsT, rhs, start=start, stop=stop, **kw)

        pe.sem_inc(s_kT, 3)
        pe.sem_inc(s_cT, XB)
        pe.sem_inc(s_ckv, 2)
        pe.sem_inc(s_cc, 2)
        pe.sem_inc(s_nT, 1)
        pe.sem_inc(s_xsTp, 3)
        pe.sem_inc(s_x2free, 1)
        pe.sem_inc(s_slot, 1)
        pe.sem_inc(s_gr, 1)
        pe.sem_inc(s_hot, 2)
        pe.wait_ge(s_gp, 13)
        pe.wait_ge(s_const, 13)
        pe.wait_ge(s_dabs, 1)
        mm(banks[6][:, 0:EB], first4[:, :], dabs[:, :, 0], True, True).then_inc(s_gb, 1)
        pe.wait_ge(s_bad, 1)
        LB = ET - (EB - 1) * P
        for b in range(EB):
            n = P if b < EB - 1 else LB
            if b:
                pe.wait_ge(s_blkc, b)
                pe.wait_ge(s_blka, b)
            for bank, a in ((4, s_blk[0:n, b, :]), (5, e_blk[0:n, b, :]), (6, dabs[0:n, b, :]), (7, w_blk[0:n, b, :])):
                last = pe.transpose(banks[bank][:, 0:n], a, ident[0:n, 0:n])
            last.then_inc(s_blkT, 1)
        pe.wait_ge(s_blkc, EB)
        pe.wait_ge(s_blka, EB)
        mm(banks[6][:, 0:P], badc[:, 0:1].to_broadcast([P, P]), ident[:, :], True, True).then_inc(s_badb, 1)
        pe.wait_ge(s_w, 16 * 9)
        for m in range(2):
            for c in range(KC):
                for o in range(KC):
                    last = pe.transpose(banks[4 + m][:, c * D + o * P:c * D + (o + 1) * P], wraw[:, m, o, c * P:(c + 1) * P], ident[:, :])
            last.then_inc(s_wt, 1)

        def group(g, h, tiles):
            pe.wait_ge(s_hi, g + 1)
            pe.wait_ge(s_xsT, g + 2)
            for c in range(KC):
                for k in range(tiles):
                    last = mm(banks[c][:, k * P:(k + 1) * P], x16[h][:, k, c * P:(c + 1) * P], ident16[:, :], True, True)
            last.then_inc(s_xsTp, 1)
            pe.wait_ge(s_xsT, g + 3)
            pe.wait_ge(s_km, g + 1)
            for o in range(KC):
                for c in range(KC):
                    last = mm(banks[2 + 2 * h + o][:, 0:tiles * P], wkvh[:, c, o * P:(o + 1) * P],
                              xsT[:, h, c, 0:tiles * P], c == 0, c == KC - 1)
            last.then_inc(s_kT, 1)

        pe.sem_inc(s_xsT, 2)
        pe.sem_inc(s_km, 3)
        pe.wait_ge(s_wk, 2)
        pe.wait_ge(s_wtc, 2)
        with pe.Fori(0, 4) as g:
            for h in range(3):
                group(3 * g + h, h, 4)
        group(12, 0, 1)
        pe.wait_ge(s_nk, 1)
        for c in range(KC):
            last = mm(banks[6][:, c * P:(c + 1) * P], kmax[:, c:c + 1].to_broadcast([P, P]), ident[:, :], True, True)
        last.then_inc(s_nkc, 1)
        pe.wait_ge(s_flag, 1)
        bad = pe.value_load(flag[0:1, 0:1], min_val=0, max_val=1)
        with pe.If(bad):
            with pe.Fori(0, ET) as t:
                pe.wait_ge(s_gg, 16 * t + 16)
                pe.sem_inc(s_hold, 1)
                with pe.Fori(0, GN) as n:
                    pe.wait_ge(s_gw, t * GN + n + 1)
                    for c in range(KC):
                        last = mm(banks[6 + c][:, 0:GW], t1[:, c * P:(c + 1) * P], ghot, True, True)
                    last.then_inc(s_gm, 1)

        pe.wait_ge(s_gend, 1)
        pe.sem_inc(s_acc, 2 * (HALF // GROUP))
        pe.sem_inc(s_cx, 2)
        pe.sem_inc(s_ckd, 2)

        def edges(i, q):
            h, g = divmod(q, HALF // GROUP)
            if g == 0:
                pe.wait_ge(s_acc, (2 * i + h + 1) * (HALF // GROUP))
                pe.wait_ge(s_hot, 2 * i + h + 3)
            for k in range(g * GROUP, (g + 1) * GROUP):
                pe.wait_ge(s_got[h][k], 16 * i + 16)
                for c in range(KC):
                    window = psE[h][:, (g * KC + c) * W:(g * KC + c + 1) * W]
                    hi = got[h][:, k, c * P:(c + 1) * P]
                    lo = got[h][:, k, D + c * P:D + (c + 1) * P]
                    mm(window, hi, hot[h][:, 0, k, :], g == 0 and k == 0 and c == 0, False, skip_group_check=True)
                    mm(window, hi, hot[h][:, 1, k, :], False, False, skip_group_check=True)
                    last = mm(window, lo, hot[h][:, 0, k, :], False, k == HALF - 1 and c == KC - 1, skip_group_check=True)
            if k == HALF - 1:
                last.then_inc(s_mult, 1)

        def ctx_T(t, b, loads):
            h, rows = b % 2, rows_of(t)
            pe.wait_ge(s_cl[b], 16 * loads)
            pe.wait_ge(s_cx, t + 1)
            for k in range(2 * KC):
                last = mm(psTc[h][:, k * P:k * P + rows], xin[0:rows, b, k * P:(k + 1) * P], ident16[0:rows, 0:rows], True, True)
            last.then_inc(s_cT, 1)

        def ctx_kv(t, h):
            rows = rows_of(t)
            pe.wait_ge(s_cx, t + 3)
            pe.wait_ge(s_ckd, t + 1)
            for k in range(KC):
                for part_, w in ((0, wkvh), (0, wkvl), (1, wkvh)):
                    last = mm(psKV[h][0:rows, :], xT[:, h, part_, k, 0:rows], w[:, k, :], k == 0 and part_ == 0 and w is wkvh,
                              k == KC - 1 and part_ == 1)
            last.then_inc(s_ckv, 1)

        def ctx_sum(t, h):
            rows = rows_of(t)
            last_tile = isinstance(t, int) and t == FULL
            pe.wait_ge(s_ckd, t + 3)
            pe.wait_ge(s_cek, t + 1)
            for k in range(KC):
                last = mm(psC[:, k * (P + 1):(k + 1) * (P + 1)], ek[0:rows, h, k * P:(k + 1) * P], v[0:rows, h, k, :], False,
                          last_tile and k == KC - 1, skip_group_check=True)
            last.then_inc(s_cc, 1)

        def context_iteration(i):
            for c in range(CTX):
                t = i * CTX + c
                if c % (CTX // 4) == 0:
                    edges(i, c // (CTX // 4))
                if not (isinstance(t, int) and t + 2 > FULL):
                    ctx_T(t + 2, (c + 2) % XB, i * (CTX // XB) + (c + 2) // XB + 1)
                ctx_kv(t + 1, (c + 1) % 2)
                ctx_sum(t, c % 2)

        pe.wait_ge(s_bias, 1)
        mm(psC[:, 0:KC * (P + 1)], zeros[:, 0:P], zeros[:, 0:KC * (P + 1)], True, False, skip_group_check=True)
        ctx_T(0, 0, 1)
        ctx_T(1, 1, 1)
        ctx_kv(0, 0)
        with pe.Fori(0, CTX_IT - 1) as i:
            context_iteration(i)
        context_iteration(CTX_IT - 1)
        edges(CTX_IT, 0)
        ctx_sum(FULL, 0)
        edges(CTX_IT, 1)
        pe.wait_ge(s_bd, 1)
        for c in range(KC):
            last = pe.transpose(banks[7][:, c * P:(c + 1) * P], bd[:, c, :], ident[:, :])
        last.then_inc(s_bd, 1)
        pe.wait_ge(s_bd, 3)
        for c in range(KC):
            last = mm(banks[6][:, c * D:(c + 1) * D], bdT[:, c, :], wout[:, c, :], True, True)
        last.then_inc(s_mp, 1)
        edges(CTX_IT, 2)
        edges(CTX_IT, 3)
        pe.wait_ge(s_M, 1)

        def node_in(n):
            rows = rows_of(n)
            pe.wait_ge(s_nl, 16 * n + 16)
            for c in range(KC):
                last = pe.transpose(psT[:, c * P:c * P + rows], xn_in[0:rows, c * P:(c + 1) * P], ident[0:rows, 0:rows])
            last.then_inc(s_nT, 1)
            pe.wait_ge(s_nTc, n + 1)
            for c in range(KC):
                last = mm(banks[3][0:rows, 0:D], nT[:, c, 0:rows], wqkv[:, c, 0:D], c == 0, c == KC - 1)
            last.then_inc(s_q, 1)
            pe.wait_ge(s_gr, n + 1)
            mm(banks[4][0:rows, 0:D], nT[:, 0, 0:rows], w1T[:, 0, :], True, False)
            mm(banks[4][0:rows, 0:D], nT[:, 1, 0:rows], w1T[:, 1, :], False, False)
            mm(banks[4][0:rows, 0:D], ones16[:, 0:rows], bias3[:, :], False, False)

        def node_side(n):
            rows = rows_of(n)
            pe.wait_ge(s_sT, n + 1)
            mm(banks[4][0:rows, 0:D], sT[:, 0, 0:rows], w2T[:, 0, :], False, False)
            mm(banks[4][0:rows, 0:D], sT[:, 1, 0:rows], w2T[:, 1, :], False, True).then_inc(s_g, 1)

        def q_transposed(n):
            rows = rows_of(n)
            pe.wait_ge(s_qn, n + 1)
            for c in range(KC):
                last = pe.transpose(psT[:, 256 + c * P:256 + c * P + rows], qn[0:rows, c * P:(c + 1) * P], ident[0:rows, 0:rows])
            last.then_inc(s_qT, 1)

        def node_mix(n):
            rows = rows_of(n)
            pe.wait_ge(s_qTc, n + 1)
            for c in range(KC):
                last = mm(banks[6][0:rows, 0:D], qT[:, c, 0:rows], M[:, c, :], c == 0, c == KC - 1)
            last.then_inc(s_mix, 1)

        def x2_transposed(n):
            rows = rows_of(n)
            pe.wait_ge(s_x2n, n + 1)
            pe.wait_ge(s_slot, n + 1)
            for c in range(KC):
                last = pe.transpose(banks[7][:, c * P:c * P + rows], x2n[0:rows, c * P:(c + 1) * P], ident[0:rows, 0:rows])
            last.then_inc(s_x2T, 1)

        def logits(n):
            rows = rows_of(n)
            pe.wait_ge(s_x2Tc, n + 1)
            lo = banks[7][0:rows, 256:256 + NEXP]
            for c in range(KC):
                mm(lo, x2T[:, c, 0:rows], wr[:, c, :], c == 0, False)
            mm(lo, ones[0:1, 0:rows], br_row[0:1, :], False, True).then_inc(s_lg, 1)

        def ranks(m):
            rows = rows_of(m)
            pe.wait_ge(s_both, m + 1)
            mm(banks[7][0:rows, 264:264 + NEXP], tri[0:rows, 0:rows], oh[0:rows, 2, :], True, True)
            mm(banks[7][:, 272:272 + NEXP], ones[0:rows, :], oh[0:rows, 2, :], True, True).then_inc(s_rank, 1)

        def node(i, n, m):
            if i is not None:
                edges(i, 0)
                edges(i, 1)
            if m is not None:
                x2_transposed(m)
                logits(m)
            node_in(n)
            if m is not None:
                ranks(m)
            node_side(n)
            if i is not None:
                edges(i, 2)
                edges(i, 3)
            q_transposed(n)
            node_mix(n)

        node(CTX_IT + 1, 0, None)
        with pe.Fori(CTX_IT + 2, EIT) as i:
            node(i, i - (CTX_IT + 1), i - (CTX_IT + 2))
        with pe.Fori(EIT - CTX_IT - 1, FULL) as t:
            node(None, t, t - 1)
        node(None, FULL, FULL - 1)
        x2_transposed(FULL)
        logits(FULL)
        ranks(FULL)


def experts(nc, part, banks, stage0, base, pid, ident, padrow, slots, ln_g, ln_b, ffn_W1, ffn_b1, ffn_W2, ffn_b2, out):
    def sb(name, shape, dt=F32):
        return part.enter_context(nc.sbuf_tensor(name, shape, dt))

    def sem(name):
        return part.enter_context(nc.semaphore(name))

    W1N, W2N = KC * H, HC * D
    NP = -(-N // (2 * P))
    w1h, w1l = (sb(n, [P, NEXP * W1N], F16) for n in ("w1h", "w1l"))
    w2h, w2l = (sb(n, [P, NEXP * W2N], F16) for n in ("w2h", "w2l"))
    h32 = sb("h32", [P, 2, HC, 2 * P])
    hhl = sb("hhl", [P, 2, 2, HC, 2 * P], F16)
    hh, hl = hhl[:, 0, :, :, :], hhl[:, 1, :, :, :]
    stages = [stage0[:, :], h32[:, :, :, :].rearrange("p h c n -> p (h c n)"),
              hhl[:, :, :, :, :].rearrange("p a h c n -> p (a h c n)").bitcast(F32)]
    w1s = [st[:, 0:W1N] for st in stages]
    w2s = [st[:, W1N:W1N + W2N] for st in stages]
    g64 = sb("g64", [P, KC, NEXP])
    gT = sb("gT", [P, KC, NEXP])
    bT = sb("bT", [P, KC, NEXP])
    own = sb("own", [P, NEXP, NEXP])
    bTe = sb("bTe", [P, KC, NEXP, NEXP])
    b1 = sb("b1", [P, NEXP * HC])
    b2 = sb("b2", [P, NEXP * D])
    cnt = sb("cnt", [P, NEXP])
    tiles = sb("tiles", [P, NEXP])
    ends = sb("ends", [P, NEXP])
    ks = sb("ks", [P, NP])
    big = sb("big", [P, NEXP, PAIRS])
    js = sb("js", [P, PAIRS])
    ej = sb("ej", [P, PAIRS])
    sj = sb("sj", [P, PAIRS])
    ro = sb("ro", [P, PAIRS])
    roff = sb("roff", [P, PAIRS], I32)
    eidx = sb("eidx", [P, PAIRS], I32)
    woff = sb("woff", [P, PAIRS], I32)
    reg0 = sb("reg0", [P, NEXP])
    padf = sb("padf", [P, 2, NEXP])
    padi = sb("padi", [P, 2, NEXP], I32)
    xe = sb("xe", [P, 2, 2, ROW])
    xh, xl = (sb(n, [P, 2, KC, 2 * P], F16) for n in ("xh", "xl"))
    y = sb("y", [P, 2, D])
    yg = sb("yg", [P, 2, 2, D])
    grow = y[0:NEXP, :, :]
    b1raw = yg[0:NEXP, :, :, :].rearrange("e a b d -> e (a b d)")
    gates = sb("gates", [P, PAIRS, 2])
    tokf = sb("tokf", [P, PAIRS, 2])
    toki = [sb(f"toki{h}", [P, 2], I32) for h in range(2)]
    psT = [banks[0], banks[7]]
    psH = banks[1:5]
    psY = [banks[5], banks[6]]

    s_c = sem("f_c")
    s_ch = sem("f_ch")
    s_l = [[sem(f"f_l{i}_{b}") for b in range(3)] for i in range(2)]
    s_b = sem("f_b")
    s_bT = sem("f_bT")
    s_bTc = sem("f_bTc")
    s_hi = sem("f_hi")
    s_hi2 = sem("f_hi2")
    s_lo = sem("f_lo")
    s_pb = sem("f_pb")
    s_pad = sem("f_pad")
    s_tab = sem("f_tab")
    s_padded = sem("f_padded")
    s_xe = [sem(f"f_xe{h}") for h in range(2)]
    s_hold = sem("f_hold")
    s_T = sem("f_T")
    s_xh = sem("f_xh")
    s_xl = sem("f_xl")
    s_H = sem("f_H")
    s_gelu = sem("f_gelu")
    s_hh = sem("f_hh")
    s_hl = sem("f_hl")
    s_Y = sem("f_Y")
    s_y1 = sem("f_y1")
    s_gt = sem("f_gt")
    s_y = sem("f_y")
    s_add = sem("f_add")
    s_g = sem("f_g")
    s_g64 = sem("f_g64")
    JT = PAIRS // 2

    def landed(eng, i, e):
        if e:
            eng.wait_ge(s_l[i][e % 3], 16 * (e // 3 + (e % 3 > 0)))

    block = part.enter_context(nc.Block())

    @block.sync
    def _(sp):
        sp.dma_start(grow[:, 0, :], ln_g).then_inc(s_b, 16)
        sp.dma_start(grow[:, 1, :], ln_b).then_inc(s_b, 16)
        sp.dma_start(b1raw[:, :], ffn_b1).then_inc(s_b, 16)
        for e in range(1, NEXP):
            if e >= 3:
                sp.wait_ge(s_lo, e - 2)
            load_expert(sp, stages[e % 3], e, ffn_W1, ffn_W2, (s_l[0][e % 3], s_l[1][e % 3]))
            if e == 2:
                sp.dma_start(b2[:, :], ffn_b2.rearrange("e d -> (e d)").partition_broadcast(P)).then_inc(s_tab, 16)
        sp.wait_ge(s_tab, 17)
        sp.wait_ge(s_padded, 32 * NEXP)
        with sp.Fori(0, JT) as i:
            for h in range(2):
                j = 2 * i + h
                r = sp.value_load(roff[0:1, bass.ds(j, 1)], min_val=0, max_val=NEXP * CAP)
                sp.wait_ge(s_xl, j + 1)
                sp.dma_start(xe[:, h, :, :], slots[bass.ds(r, 2 * P), :].rearrange("(a p) d -> p a d", p=P)).then_inc(s_xe[h], 16)

    @block.gpsimd
    def _(pool):
        pool.iota(ks[:, :], pattern=[[2 * P, NP]], base=0, channel_multiplier=0,
                  allow_small_or_imprecise_dtypes=True).then_inc(s_c, 1)
        pool.iota(js[:, :], pattern=[[1, PAIRS]], base=0, channel_multiplier=0,
                  allow_small_or_imprecise_dtypes=True).then_inc(s_c, 1)
        pool.iota(reg0[:, :], pattern=[[CAP, NEXP]], base=0, channel_multiplier=0,
                  allow_small_or_imprecise_dtypes=True).then_inc(s_c, 1)
        pool.wait_ge(s_pad, 1)
        for e in range(NEXP):
            for a in range(2):
                pool.indirect_dma_start(out=slots[:, :], out_offset=bass.IndirectOffsetOnAxis(ap=padi[:, a, e:e + 1], axis=0),
                                        in_=padrow[:, a, :], in_offset=None).then_inc(s_padded, 16)
        with pool.Fori(0, JT) as i:
            for h in range(2):
                j = 2 * i + h
                pool.wait_ge(s_y, j + 3)
                pool.sem_inc(s_hold, 1)
                for a in range(2):
                    pool.indirect_dma_start(out=out[:, :], out_offset=bass.IndirectOffsetOnAxis(ap=toki[h][:, a:a + 1], axis=0),
                                            in_=yg[:, h, a, :], in_offset=None, compute_op=ALU.add).then_inc(s_add, 16)
                pool.wait_ge(s_add, 32 * j + 32)
                pool.sem_inc(s_g, 1)

    @block.scalar
    def _(act):
        def high1(e):
            landed(act, 0, e)
            if e == 0:
                act.wait_ge(s_g64, 1)
            for c in range(KC):
                last = act.activation(w1h[:, e * W1N + c * H:e * W1N + (c + 1) * H], w1s[e % 3][:, c * H:(c + 1) * H], ACT.Copy,
                                      scale=g64[:, c, e:e + 1])
            last.then_inc(s_hi, 1)

        def high2(e):
            landed(act, 1, e)
            act.activation(w2h[:, e * W2N:(e + 1) * W2N], w2s[e % 3], ACT.Copy, scale=WSCALE).then_inc(s_hi2, 1)

        high2(0)
        high1(0)
        for e in range(1, NEXP):
            high1(e)
            high2(e)

        def tile(j, h):
            act.wait_ge(s_hl, j + 1)
            act.sem_inc(s_hold, 1)
            e8 = act.value_load(eidx[0:1, bass.ds(j, 1)], min_val=0, max_val=NEXP - 1) * HC
            for q in range(4):
                act.wait_ge(s_H, 4 * j + 5 + q)
                act.sem_inc(s_hold, 1)
                for c in range(2):
                    last = act.activation(h32[:, h, 2 * q + c, :], psH[q][:, c * 2 * P:(c + 1) * 2 * P], ACT.Gelu,
                                          bias=b1[:, bass.ds(e8 + (2 * q + c), 1)], scale=1.0 / WSCALE)
                last.then_inc(s_gelu, 1)

        act.wait_ge(s_tab, 17)
        with act.Fori(0, JT) as i:
            tile(2 * i, 0)
            tile(2 * i + 1, 1)

    @block.vector
    def _(dve):
        ch = Chain(dve, s_ch)
        dve.wait_ge(s_c, 3)
        ch(dve.tensor_tensor(cnt[:, :], base[:, :], reg0[:, :], ALU.subtract))
        ch(dve.tensor_scalar(padf[:, 0, :], base[:, :], pid[:, 0:1], None, op0=ALU.add))
        ch(dve.tensor_scalar(padf[:, 1, :], padf[:, 0, :], float(P), None, op0=ALU.add))
        dve.tensor_copy(padi[:, :, :], padf[:, :, :]).then_inc(s_pad, 1)
        ch(dve.tensor_tensor(big[:, :, 0:NP], cnt[:, :].unsqueeze(2).to_broadcast([P, NEXP, NP]),
                             ks[:, :].unsqueeze(1).to_broadcast([P, NEXP, NP]), ALU.is_gt))
        ch(dve.reduce_sum(tiles[:, :], big[:, :, 0:NP], axis=X))
        ch(dve.tensor_copy(ends[:, 0:1], tiles[:, 0:1]))
        for e in range(1, NEXP):
            ch(dve.tensor_tensor(ends[:, e:e + 1], ends[:, e - 1:e], tiles[:, e:e + 1], ALU.add))
        ch(dve.tensor_tensor(big[:, :, :], js[:, :].unsqueeze(1).to_broadcast([P, NEXP, PAIRS]),
                             ends[:, :].unsqueeze(2).to_broadcast([P, NEXP, PAIRS]), ALU.is_ge))
        ch(dve.reduce_sum(ej[:, :], big[:, :, :].rearrange("p e j -> p j e"), axis=X))
        ch(dve.tensor_tensor(big[:, :, :], big[:, :, :], tiles[:, :].unsqueeze(2).to_broadcast([P, NEXP, PAIRS]), ALU.mult))
        ch(dve.reduce_sum(sj[:, :], big[:, :, :].rearrange("p e j -> p j e"), axis=X))
        ch(dve.tensor_tensor(sj[:, :], js[:, :], sj[:, :], ALU.subtract))
        ch(dve.tensor_scalar(sj[:, :], sj[:, :], float(2 * P), None, op0=ALU.mult))
        ch(dve.scalar_tensor_tensor(out=ro[:, :], in0=ej[:, :], scalar=float(CAP), in1=sj[:, :], op0=ALU.mult, op1=ALU.add))
        ch(dve.tensor_scalar(ro[:, :], ro[:, :], float(NEXP * CAP), None, op0=ALU.min))
        ch(dve.tensor_copy(roff[:, :], ro[:, :]))
        ch(dve.tensor_scalar(sj[:, :], ej[:, :], float(NEXP - 1), None, op0=ALU.min))
        ch(dve.tensor_copy(eidx[:, :], sj[:, :]))
        ch(dve.tensor_scalar(sj[:, :], sj[:, :], float(W1N), None, op0=ALU.mult))
        ch(dve.tensor_copy(woff[:, :], sj[:, :]))
        dve.wait_ge(s_bT, 1)
        ch(dve.tensor_copy(gT[:, :, :].rearrange("p c e -> p (c e)"), banks[0][:, 0:16]))
        ch(dve.tensor_copy(bT[:, :, :].rearrange("p c e -> p (c e)"), banks[0][:, 16:32]))
        ch(dve.tensor_tensor(own[:, :, :], reg0[:, :].unsqueeze(2).to_broadcast([P, NEXP, NEXP]),
                             reg0[:, :].unsqueeze(1).to_broadcast([P, NEXP, NEXP]), ALU.is_equal))
        for c in range(KC):
            ch(dve.tensor_tensor(bTe[:, c, :, :], own[:, :, :], bT[:, c, :].unsqueeze(2).to_broadcast([P, NEXP, NEXP]), ALU.mult))
        dve.sem_inc(s_bTc, 1)
        dve.tensor_scalar(g64[:, :, :], gT[:, :, :], WSCALE, None, op0=ALU.mult).then_inc(s_g64, 1)
        dve.wait_ge(s_g64, 1)

        def low1(e):
            dve.wait_ge(s_hi, e + 1)
            for c in range(KC):
                at = slice(e * W1N + c * H, e * W1N + (c + 1) * H)
                last = dve.scalar_tensor_tensor(out=w1l[:, at], in0=w1s[e % 3][:, c * H:(c + 1) * H], scalar=g64[:, c, e:e + 1],
                                                in1=w1h[:, at], op0=ALU.mult, op1=ALU.subtract)
            return last

        def low2(e):
            dve.wait_ge(s_hi2, e + 1)
            return dve.scalar_tensor_tensor(out=w2l[:, e * W2N:(e + 1) * W2N], in0=w2s[e % 3], scalar=WSCALE,
                                            in1=w2h[:, e * W2N:(e + 1) * W2N], op0=ALU.mult, op1=ALU.subtract)

        for e in range(NEXP):
            first, second = (low1, low2) if e else (low2, low1)
            first(e)
            dve.wait_ge(s_pb, e + 1)
            if e == NEXP - 1:
                for q in range(2):
                    part_ = b1raw[:, q * H // 2:(q + 1) * H // 2]
                    last = dve.tensor_tensor(part_, part_, banks[1 + q][0:NEXP, :], ALU.add)
                last.then_inc(s_bTc, 1)
            second(e).then_inc(s_lo, 1)
        dve.wait_ge(s_bT, 2)
        ch(dve.tensor_copy(b1[:, :].rearrange("p (e c) -> p e c", c=HC),
                           banks[0][:, 32:96].rearrange("p (c e) -> p e c", c=HC)))
        dve.wait_ge(s_lo, NEXP)
        dve.sem_inc(s_tab, 1)
        dve.sem_inc(s_hl, 2)
        dve.sem_inc(s_y, 2)
        dve.sem_inc(s_H, 4)

        def split_x(j, h, i):
            dve.wait_ge(s_xe[h], 16 * i + 16)
            g = gates[:, bass.ds(j, 1), :].rearrange("p a b -> p (a b)")
            dve.tensor_scalar(g, xe[:, h, :, D + 1], ej[:, bass.ds(j, 1)], None, op0=ALU.is_equal).then_inc(s_gt, 1)
            dve.tensor_scalar(tokf[:, bass.ds(j, 1), :].rearrange("p a b -> p (a b)"), xe[:, h, :, D], 0.0, None, op0=ALU.add)
            dve.wait_ge(s_gt, 2 * j + 1)
            dve.tensor_tensor(g, g, xe[:, h, :, D + 3], ALU.mult).then_inc(s_gt, 1)
            dve.wait_ge(s_T, j + 3)
            dve.wait_ge(s_H, 4 * j + 1)
            dve.tensor_copy(xh[:, h, :, :].rearrange("p c n -> p (c n)"), psT[h][:, :]).then_inc(s_xh, 1)
            dve.wait_ge(s_gt, 2 * j + 2)
            dve.tensor_tensor(g, g, xe[:, h, :, D + 2], ALU.add)
            dve.wait_ge(s_xh, j + 1)
            dve.tensor_tensor(xl[:, h, :, :].rearrange("p c n -> p (c n)"), psT[h][:, :],
                              xh[:, h, :, :].rearrange("p c n -> p (c n)"), ALU.subtract).then_inc(s_xl, 1)

        def split_h(j, h):
            dve.wait_ge(s_Y, j + 1)
            for q in range(4):
                two_ = slice(2 * q, 2 * q + 2)
                dve.wait_ge(s_gelu, 4 * j + q + 5)
                dve.tensor_copy(hh[:, h, two_, :], h32[:, h, two_, :]).then_inc(s_hh, 1)
                dve.wait_ge(s_hh, 4 * j + q + 1)
                last = dve.tensor_tensor(hl[:, h, two_, :], h32[:, h, two_, :], hh[:, h, two_, :], ALU.subtract)
            last.then_inc(s_hl, 1)

        def gated(j, h):
            e = dve.value_load(eidx[0:1, bass.ds(j, 1)], min_val=0, max_val=NEXP - 1)
            dve.wait_ge(s_y, j + 2)
            dve.wait_ge(s_Y, j + 3)
            dve.scalar_tensor_tensor(out=y[:, :, :], in0=psY[h][:, :].rearrange("p (a d) -> p a d", a=2), scalar=1.0 / WSCALE,
                                     in1=b2[:, bass.ds(e * D, D)].unsqueeze(1).to_broadcast([P, 2, D]),
                                     op0=ALU.mult, op1=ALU.add).then_inc(s_y1, 1)
            dve.wait_ge(s_y1, j + 1)
            dve.wait_ge(s_g, j + 1)
            dve.tensor_scalar(toki[h][:, :], tokf[:, bass.ds(j, 1), :].rearrange("p a b -> p (a b)"), 0.0, None, op0=ALU.add)
            for a in range(2):
                last = dve.tensor_scalar(yg[:, h, a, :], y[:, a, :], gates[:, bass.ds(j, 1), a], None, op0=ALU.mult)
            last.then_inc(s_y, 1)

        split_x(0, 0, 0)
        split_x(1, 1, 0)
        split_h(0, 0)
        with dve.Fori(0, JT - 1) as i:
            split_x(2 * i + 2, 0, i + 1)
            split_h(2 * i + 1, 1)
            gated(2 * i, 0)
            split_x(2 * i + 3, 1, i + 1)
            split_h(2 * i + 2, 0)
            gated(2 * i + 1, 1)
        split_h(PAIRS - 1, 1)
        gated(PAIRS - 2, 0)
        gated(PAIRS - 1, 1)

    @block.tensor
    def _(pe):
        pe.sem_inc(s_T, 2)
        pe.sem_inc(s_Y, 2)
        pe.sem_inc(s_g, 2)
        pe.wait_ge(s_b, 48)
        for c in range(KC):
            for k in range(2):
                last = pe.transpose(banks[0][:, (2 * k + c) * NEXP:(2 * k + c + 1) * NEXP], grow[:, k, c * P:(c + 1) * P], ident[0:NEXP, 0:NEXP])
        last.then_inc(s_bT, 1)
        pe.wait_ge(s_bTc, 1)
        for e in range(NEXP):
            landed(pe, 0, e)
            for q in range(2):
                for k in range(KC):
                    last = pe.matmul(banks[1 + q][0:NEXP, :], bTe[:, k, e, :], w1s[e % 3][:, k * H + q * H // 2:k * H + (q + 1) * H // 2],
                                     start=e == 0 and k == 0, stop=e == NEXP - 1 and k == KC - 1)
            last.then_inc(s_pb, 1)
        pe.wait_ge(s_bTc, 2)
        for c in range(HC):
            last = pe.transpose(banks[0][:, 32 + c * NEXP:32 + (c + 1) * NEXP], b1raw[:, c * P:(c + 1) * P], ident[0:NEXP, 0:NEXP])
        last.then_inc(s_bT, 1)
        pe.wait_ge(s_tab, 17)

        def transposes(j, h, i):
            pe.wait_ge(s_xe[h], 16 * i + 16)
            pe.wait_ge(s_xl, j + 1)
            for c in range(KC):
                for a in range(2):
                    last = pe.transpose(psT[h][:, (2 * c + a) * P:(2 * c + a + 1) * P], xe[:, h, a, c * P:(c + 1) * P], ident[:, :])
            last.then_inc(s_T, 1)

        def up(j, h, e, between=None):
            pe.wait_ge(s_xl, j + 3)
            for q in range(4):
                pe.wait_ge(s_gelu, 4 * j + q + 1)
                for c in range(2):
                    first = True
                    for k in range(KC):
                        at = bass.ds(e + (k * H + (2 * q + c) * P), P)
                        for w, xp in ((w1h, xh), (w1h, xl), (w1l, xh)):
                            last = pe.matmul(psH[q][:, c * 2 * P:(c + 1) * 2 * P], w[:, at], xp[:, h, k, :], start=first,
                                             stop=k == KC - 1 and w is w1l)
                            first = False
                last.then_inc(s_H, 1)
                if between and q == 2:
                    between()

        def down(j, h, e):
            pe.wait_ge(s_hl, j + 3)
            pe.wait_ge(s_y, j + 1)
            for a in range(2):
                for c in range(HC):
                    at = bass.ds(e + c * D, D)
                    for hp, w in ((hh, w2h), (hh, w2l), (hl, w2h)):
                        last = pe.matmul(psY[h][:, a * D:(a + 1) * D], hp[:, h, c, a * P:(a + 1) * P], w[:, at],
                                         start=c == 0 and hp is hh and w is w2h, stop=c == HC - 1 and hp is hl)
            last.then_inc(s_Y, 1)

        pe.sem_inc(s_xl, 2)
        pe.sem_inc(s_gelu, 4)
        starts = [pe.alloc_register(f"weights{k}") for k in range(3)]

        def weights_of(j, count):
            pe.load(starts[0:count], woff[0:1, bass.ds(j, count)])
            return [pe.snap(s, min_val=0, max_val=(NEXP - 1) * W1N) for s in starts[0:count]]

        transposes(0, 0, 0)
        e = weights_of(0, 1)
        up(0, 0, e[0], lambda: transposes(1, 1, 0))
        with pe.Fori(0, JT - 1) as i:
            e = weights_of(2 * i, 3)
            up(2 * i + 1, 1, e[1], lambda: transposes(2 * i + 2, 0, i + 1))
            down(2 * i, 0, e[0])
            up(2 * i + 2, 0, e[2], lambda: transposes(2 * i + 3, 1, i + 1))
            down(2 * i + 1, 1, e[1])
        e = weights_of(PAIRS - 2, 2)
        up(PAIRS - 1, 1, e[1])
        down(PAIRS - 2, 0, e[0])
        down(PAIRS - 1, 1, e[1])


_INS = ['x', 'src', 'dst', 'edge_weight', 'L0_gnn_W1', 'L0_gnn_b1', 'L0_gnn_W2', 'L0_gnn_b2', 'L0_mix_Wqkv',
        'L0_mix_Wout', 'L0_mix_gamma', 'L0_ffn_Wr', 'L0_ffn_br', 'L0_ffn_ln_g', 'L0_ffn_ln_b', 'L0_ffn_W1',
        'L0_ffn_b1', 'L0_ffn_W2', 'L0_ffn_b2']
_PAD = {'src': 0, 'dst': N - 1, 'edge_weight': 0}


def kernel(**inputs):
    import numpy as _np
    import concourse.bacc as _bacc
    from concourse import mybir as _mybir
    from concourse.bass_utils import run_bass_kernel_spmd as _run

    nc = _bacc.Bacc("TRN2", target_bir_lowering=False, num_devices=1)
    arrays, args = {}, []
    for name in _INS:
        a = _np.ascontiguousarray(inputs[name])
        if name in _PAD:
            a = _np.pad(a, (0, ET * P - E), constant_values=_PAD[name])
        arrays[f"in_{name}_dram"] = a
        args.append(nc.dram_tensor(f"in_{name}_dram", a.shape, _mybir.dt.from_np(a.dtype), kind="ExternalInput").ap())
    args.append(nc.dram_tensor("out_0_dram", (N + 2 * P, D), _mybir.dt.float32, kind="ExternalOutput").ap())
    program(nc, *args)
    r = _run(nc, [arrays], core_ids=[0])
    return r.results[0]["out_0_dram"][:N]
```
